# Optimizing a Trainium2 kernel written in Bass

```python
import numpy as np
import jax
import jax.numpy as jnp

def _softmax(x, axis=-1):
    return jax.nn.softmax(x, axis=axis)

def _gelu(x):
    return jax.nn.gelu(x, approximate=True)

def _silu(x):
    return jax.nn.silu(x)

def _sigmoid(x):
    return jax.nn.sigmoid(x)

def _layernorm(x, axis=-1, eps=1e-05):
    m = jnp.mean(x, axis=axis, keepdims=True)
    v = jnp.var(x, axis=axis, keepdims=True)
    return (x - m) / jnp.sqrt(v + eps)

def _scatter_add(tgt, idx, src, axis=0):
    return tgt.at[idx].add(src)

def _segment_sum(src, seg, n):
    return jax.ops.segment_sum(src, seg, n)
kernel_name = 'mk_gnn_resnorm_d4_gnn_r16_a5850b'

def setup_inputs(seed: int=0):
    np.random.seed(seed)
    _w = jnp.asarray

    def _rec_inputs():
        import jax
        import jax.numpy as jnp
        _gk = jax.random.key(seed)
        x = -0.0003713 + 1 * jax.random.normal(jax.random.fold_in(_gk, 1), (3125, 256), jnp.float32)
        src = jax.random.randint(jax.random.fold_in(_gk, 2), (100000,), 0, 3125, jnp.int32)
        dst = jnp.minimum((3125 * jax.random.uniform(jax.random.fold_in(_gk, 3), (100000,)) ** 2.0).astype(jnp.int32), 49999)
        _o = jnp.argsort(dst, stable=True)
        src = src[_o]
        dst = dst[_o]
        edge_type_8 = jax.random.randint(jax.random.fold_in(_gk, 13), (100000,), 0, 8, jnp.int32)
        edge_weight = jax.random.uniform(jax.random.fold_in(_gk, 14), (100000,), jnp.float32, 0.0, 0.999998)
        node_vec = jax.random.uniform(jax.random.fold_in(_gk, 15), (3125,), jnp.float32, 0.0, 0.999833)
        return (x, src, dst, edge_type_8, edge_weight, node_vec)
    x, src, dst, edge_type_8, edge_weight, node_vec = _rec_inputs()

    def _L0_gnn_setup():
        import jax, jax.numpy as jnp
        import numpy as np
        N = 3125

        def _gcn_norm(edge_index, num_nodes):
            src = jnp.concatenate([edge_index[0], jnp.arange(num_nodes, dtype=edge_index.dtype)])
            dst = jnp.concatenate([edge_index[1], jnp.arange(num_nodes, dtype=edge_index.dtype)])
            w = jnp.ones(src.shape[0], dtype=jnp.float32)
            deg = jax.ops.segment_sum(w, dst, num_segments=num_nodes)
            dinv = jnp.where(deg > 0, jax.lax.rsqrt(deg), 0.0)
            norm = dinv[src] * w * dinv[dst]
            return (src, dst, norm)

        def _gcn_conv(h, src, dst, norm, W, b, num_nodes):
            h = h @ W
            msg = norm[:, None] * h[src]
            agg = jax.ops.segment_sum(msg, dst, num_segments=num_nodes)
            return agg + b
        key = jax.random.key(seed)
        ks = jax.random.split(key, 12)
        d = 256
        E = 50000
        inp = {'x': jax.random.normal(ks[0], (N, d), dtype=jnp.float32), 'edge_index': jax.random.randint(ks[1], (2, E), 0, N, dtype=jnp.int32), 'edge_weights': jax.random.uniform(ks[2], (E,), dtype=jnp.float32)}
        dims = [(d, d // 2), (d // 2, d // 4), (d // 4, d // 2), (d // 2, d)]
        for i, (fi, fo) in enumerate(dims):
            s = 1.0 / np.sqrt(fi)
            inp[f'W{i + 1}'] = jax.random.uniform(ks[3 + 2 * i], (fi, fo), dtype=jnp.float32, minval=-s, maxval=s)
            inp[f'b{i + 1}'] = jnp.zeros((fo,), dtype=jnp.float32)
        return inp
    _L0_gnn_all = _L0_gnn_setup()
    _L0_gnn_in = {k: v for k, v in _L0_gnn_all.items() if k in ('W1', 'b1', 'W2', 'b2', 'W3', 'b3', 'W4', 'b4')}
    del _L0_gnn_all

    def _L1_gnn_setup():
        import jax, jax.numpy as jnp
        import numpy as np
        from jax import lax
        N, E, D = (512, 16384, 256)
        NH, FOUT = (4, 64)
        D_STATE, D_CONV, DT_RANK = (16, 4, 16)

        def _layer_norm(x, g, b, eps=1e-05):
            mu = jnp.mean(x, -1, keepdims=True)
            var = jnp.var(x, -1, keepdims=True)
            return (x - mu) * lax.rsqrt(var + eps) * g + b

        def _mamba(xs, in_proj_w, conv_w, conv_b, x_proj_w, dt_proj_w, dt_proj_b, A_log, D_param, out_proj_w):
            n = xs.shape[0]
            xz = xs @ in_proj_w.T
            xc, z = jnp.split(xz, 2, axis=-1)
            K = conv_w.shape[1]
            xp = jnp.pad(xc, ((K - 1, 0), (0, 0)))
            xc = sum((xp[k:k + n] * conv_w[:, k] for k in range(K))) + conv_b
            xc = jax.nn.silu(xc)
            dbc = xc @ x_proj_w.T
            dt = jax.nn.softplus(dbc[:, :DT_RANK] @ dt_proj_w.T + dt_proj_b)
            Bm = dbc[:, DT_RANK:DT_RANK + D_STATE]
            Cm = dbc[:, DT_RANK + D_STATE:]
            A = -jnp.exp(A_log)
            dA = jnp.exp(dt[:, :, None] * A)
            dBx = (dt * xc)[:, :, None] * Bm[:, None, :]

            def step(h, t):
                dA_t, dBx_t, C_t = t
                h = dA_t * h + dBx_t
                return (h, h @ C_t)
            _, y = lax.scan(step, jnp.zeros((xc.shape[1], D_STATE), xs.dtype), (dA, dBx, Cm))
            y = y + xc * D_param
            y = y * jax.nn.silu(z)
            return y @ out_proj_w.T

        def _forward(x, edge_index, deg_noise, gat_w, gat_a_src, gat_a_tgt, gat_b, ln_local_g, ln_local_b, ln_global_g, ln_global_b, ln2_g, ln2_b, in_proj_w, conv_w, conv_b, x_proj_w, dt_proj_w, dt_proj_b, A_log, D_param, out_proj_w, wl, wg, ff1_w, ff1_b, ff2_w, ff2_b):
            n = x.shape[0]
            src, tgt = (edge_index[0], edge_index[1])
            proj = (x @ gat_w.T).reshape(n, NH, FOUT)
            s_src = jnp.sum(proj * gat_a_src, -1)
            s_tgt = jnp.sum(proj * gat_a_tgt, -1)
            e = jax.nn.leaky_relu(s_src[src] + s_tgt[tgt], 0.2)
            exp_e = jnp.exp(e - jnp.max(e))
            denom = jax.ops.segment_sum(exp_e, tgt, num_segments=n)
            attn = exp_e / (denom[tgt] + 1e-16)
            agg = jax.ops.segment_sum(proj[src] * attn[:, :, None], tgt, num_segments=n)
            h_local = jax.nn.elu((agg + x.reshape(n, NH, FOUT)).reshape(n, NH * FOUT) + gat_b)
            h_local = _layer_norm(h_local, ln_local_g, ln_local_b)
            deg = jax.ops.segment_sum(jnp.ones((src.shape[0],), x.dtype), src, num_segments=n)
            perm = jnp.argsort(deg + deg_noise, stable=True)
            inv = jnp.argsort(perm)
            y = _mamba(x[perm], in_proj_w, conv_w, conv_b, x_proj_w, dt_proj_w, dt_proj_b, A_log, D_param, out_proj_w)
            h_attn = _layer_norm(x + y[inv], ln_global_g, ln_global_b)
            gate = jax.nn.sigmoid(h_local @ wl.T + h_attn @ wg.T)
            h = gate * h_local + (1.0 - gate) * h_attn
            ff = jax.nn.relu(h @ ff1_w.T + ff1_b) @ ff2_w.T + ff2_b
            return _layer_norm(h + ff, ln2_g, ln2_b)
        key = jax.random.key(seed)
        ks = jax.random.split(key, 24)
        w = lambda i, shape, s=0.05: jax.random.normal(ks[i], shape, dtype=jnp.float32) * s
        return {'x': jax.random.normal(ks[0], (N, D), dtype=jnp.float32), 'edge_index': jax.random.randint(ks[1], (2, E), 0, N, dtype=jnp.int32), 'edge_prob': jax.random.uniform(ks[2], (E,), dtype=jnp.float32), 'deg_noise': jax.random.uniform(ks[3], (N,), dtype=jnp.float32), 'gat_w': w(4, (NH * FOUT, D)), 'gat_a_src': w(5, (NH, FOUT)), 'gat_a_tgt': w(6, (NH, FOUT)), 'gat_b': jnp.zeros((NH * FOUT,), jnp.float32), 'ln_local_g': jnp.ones((D,), jnp.float32), 'ln_local_b': jnp.zeros((D,), jnp.float32), 'ln_global_g': jnp.ones((D,), jnp.float32), 'ln_global_b': jnp.zeros((D,), jnp.float32), 'ln2_g': jnp.ones((D,), jnp.float32), 'ln2_b': jnp.zeros((D,), jnp.float32), 'in_proj_w': w(7, (2 * D, D)), 'conv_w': w(8, (D, D_CONV), 0.2), 'conv_b': jnp.zeros((D,), jnp.float32), 'x_proj_w': w(9, (DT_RANK + 2 * D_STATE, D)), 'dt_proj_w': w(10, (D, DT_RANK)), 'dt_proj_b': w(11, (D,), 0.1) - 4.0, 'A_log': jnp.log(jnp.tile(jnp.arange(1, D_STATE + 1, dtype=jnp.float32), (D, 1))), 'D_param': jnp.ones((D,), jnp.float32), 'out_proj_w': w(12, (D, D)), 'wl': w(13, (D, D)), 'wg': w(14, (D, D)), 'ff1_w': w(15, (2 * D, D)), 'ff1_b': jnp.zeros((2 * D,), jnp.float32), 'ff2_w': w(16, (D, 2 * D)), 'ff2_b': jnp.zeros((D,), jnp.float32)}
    _L1_gnn_all = _L1_gnn_setup()
    _L1_gnn_in = {k: v for k, v in _L1_gnn_all.items() if k in ('gat_w', 'gat_a_src', 'gat_a_tgt', 'gat_b', 'ln_local_g', 'ln_local_b', 'ln_global_g', 'ln_global_b', 'ln2_g', 'ln2_b', 'in_proj_w', 'conv_w', 'conv_b', 'x_proj_w', 'dt_proj_w', 'dt_proj_b', 'A_log', 'D_param', 'out_proj_w', 'wl', 'wg', 'ff1_w', 'ff1_b', 'ff2_w', 'ff2_b')}
    del _L1_gnn_all

    def _L2_gnn_setup():
        import jax, jax.numpy as jnp
        import numpy as np
        N_NODES = 3125
        N_EDGES = 18750
        N_REL = 8
        D = 256
        N_LAYERS = 3

        def _rgcn_layer(x, W, root, bias, src, dst, seg):
            agg = jax.ops.segment_sum(x[src], seg, num_segments=N_REL * N_NODES)
            agg = agg.reshape(N_REL, N_NODES, -1)
            return jnp.einsum('rnd,rde->ne', agg, W) + x @ root + bias
        key = jax.random.key(seed)
        k1, k2, k3, k4, k5 = jax.random.split(key, 5)
        x = jax.random.normal(k1, (N_NODES, D), dtype=jnp.float32)
        scale = 1.0 / np.sqrt(D)
        weights = jax.random.normal(k2, (N_LAYERS, N_REL, D, D), dtype=jnp.float32) * scale
        roots = jax.random.normal(k3, (N_LAYERS, D, D), dtype=jnp.float32) * scale
        biases = jnp.zeros((N_LAYERS, D), dtype=jnp.float32)
        edge_index = jax.random.randint(k4, (2, N_EDGES), 0, N_NODES, dtype=jnp.int64)
        edge_type = jax.random.randint(k5, (N_EDGES,), 0, N_REL, dtype=jnp.int64)
        return {'x': x, 'weights': weights, 'roots': roots, 'biases': biases, 'edge_index': edge_index, 'edge_type': edge_type}
    _L2_gnn_all = _L2_gnn_setup()
    _L2_gnn_in = {k: v for k, v in _L2_gnn_all.items() if k in ('weights', 'roots', 'biases')}
    del _L2_gnn_all

    def _L3_gnn_setup():
        import jax, jax.numpy as jnp
        import numpy as np
        N_NODES = 6250
        N_EDGES = 100000
        IN_DIM = 256
        HID = 64
        HEADS = 2
        OUT_DIM = 256
        NEG_SLOPE = 0.2
        key = jax.random.key(seed)
        ks = jax.random.split(key, 10)
        feat = jax.random.normal(ks[0], (N_NODES, IN_DIM), dtype=jnp.float32)
        src = jax.random.randint(ks[1], (N_EDGES,), 0, N_NODES)
        dst = jax.random.randint(ks[2], (N_EDGES,), 0, N_NODES)
        W = jax.random.normal(ks[3], (IN_DIM, HEADS * HID), dtype=jnp.float32) * 0.05
        attn_l = jax.random.normal(ks[4], (HEADS, HID), dtype=jnp.float32) * 0.05
        attn_r = jax.random.normal(ks[5], (HEADS, HID), dtype=jnp.float32) * 0.05
        gat_bias = jnp.zeros((HEADS * HID,), dtype=jnp.float32)
        lin_W = jax.random.normal(ks[6], (HEADS * HID, OUT_DIM), dtype=jnp.float32) * 0.05
        lin_b = jnp.zeros((OUT_DIM,), dtype=jnp.float32)
        return {'feat': feat, 'src': src, 'dst': dst, 'W': W, 'attn_l': attn_l, 'attn_r': attn_r, 'gat_bias': gat_bias, 'lin_W': lin_W, 'lin_b': lin_b}
    _L3_gnn_all = _L3_gnn_setup()
    _L3_gnn_in = {k: v for k, v in _L3_gnn_all.items() if k in ('W', 'attn_l', 'attn_r', 'gat_bias', 'lin_W', 'lin_b')}
    del _L3_gnn_all
    return {'x': x, 'src': src, 'dst': dst, 'edge_type_8': edge_type_8, 'edge_weight': edge_weight, 'node_vec': node_vec, 'L0_gnn_W1': _L0_gnn_in['W1'], 'L0_gnn_b1': _L0_gnn_in['b1'], 'L0_gnn_W2': _L0_gnn_in['W2'], 'L0_gnn_b2': _L0_gnn_in['b2'], 'L0_gnn_W3': _L0_gnn_in['W3'], 'L0_gnn_b3': _L0_gnn_in['b3'], 'L0_gnn_W4': _L0_gnn_in['W4'], 'L0_gnn_b4': _L0_gnn_in['b4'], 'L1_gnn_gat_w': _L1_gnn_in['gat_w'], 'L1_gnn_gat_a_src': _L1_gnn_in['gat_a_src'], 'L1_gnn_gat_a_tgt': _L1_gnn_in['gat_a_tgt'], 'L1_gnn_gat_b': _L1_gnn_in['gat_b'], 'L1_gnn_ln_local_g': _L1_gnn_in['ln_local_g'], 'L1_gnn_ln_local_b': _L1_gnn_in['ln_local_b'], 'L1_gnn_ln_global_g': _L1_gnn_in['ln_global_g'], 'L1_gnn_ln_global_b': _L1_gnn_in['ln_global_b'], 'L1_gnn_ln2_g': _L1_gnn_in['ln2_g'], 'L1_gnn_ln2_b': _L1_gnn_in['ln2_b'], 'L1_gnn_in_proj_w': _L1_gnn_in['in_proj_w'], 'L1_gnn_conv_w': _L1_gnn_in['conv_w'], 'L1_gnn_conv_b': _L1_gnn_in['conv_b'], 'L1_gnn_x_proj_w': _L1_gnn_in['x_proj_w'], 'L1_gnn_dt_proj_w': _L1_gnn_in['dt_proj_w'], 'L1_gnn_dt_proj_b': _L1_gnn_in['dt_proj_b'], 'L1_gnn_A_log': _L1_gnn_in['A_log'], 'L1_gnn_D_param': _L1_gnn_in['D_param'], 'L1_gnn_out_proj_w': _L1_gnn_in['out_proj_w'], 'L1_gnn_wl': _L1_gnn_in['wl'], 'L1_gnn_wg': _L1_gnn_in['wg'], 'L1_gnn_ff1_w': _L1_gnn_in['ff1_w'], 'L1_gnn_ff1_b': _L1_gnn_in['ff1_b'], 'L1_gnn_ff2_w': _L1_gnn_in['ff2_w'], 'L1_gnn_ff2_b': _L1_gnn_in['ff2_b'], 'L2_gnn_weights': _L2_gnn_in['weights'], 'L2_gnn_roots': _L2_gnn_in['roots'], 'L2_gnn_biases': _L2_gnn_in['biases'], 'L3_gnn_W': _L3_gnn_in['W'], 'L3_gnn_attn_l': _L3_gnn_in['attn_l'], 'L3_gnn_attn_r': _L3_gnn_in['attn_r'], 'L3_gnn_gat_bias': _L3_gnn_in['gat_bias'], 'L3_gnn_lin_W': _L3_gnn_in['lin_W'], 'L3_gnn_lin_b': _L3_gnn_in['lin_b']}

def reference(x, src, dst, edge_type_8, edge_weight, node_vec, L0_gnn_W1, L0_gnn_b1, L0_gnn_W2, L0_gnn_b2, L0_gnn_W3, L0_gnn_b3, L0_gnn_W4, L0_gnn_b4, L1_gnn_gat_w, L1_gnn_gat_a_src, L1_gnn_gat_a_tgt, L1_gnn_gat_b, L1_gnn_ln_local_g, L1_gnn_ln_local_b, L1_gnn_ln_global_g, L1_gnn_ln_global_b, L1_gnn_ln2_g, L1_gnn_ln2_b, L1_gnn_in_proj_w, L1_gnn_conv_w, L1_gnn_conv_b, L1_gnn_x_proj_w, L1_gnn_dt_proj_w, L1_gnn_dt_proj_b, L1_gnn_A_log, L1_gnn_D_param, L1_gnn_out_proj_w, L1_gnn_wl, L1_gnn_wg, L1_gnn_ff1_w, L1_gnn_ff1_b, L1_gnn_ff2_w, L1_gnn_ff2_b, L2_gnn_weights, L2_gnn_roots, L2_gnn_biases, L3_gnn_W, L3_gnn_attn_l, L3_gnn_attn_r, L3_gnn_gat_bias, L3_gnn_lin_W, L3_gnn_lin_b):
    import jax
    import jax.numpy as jnp

    def _L0_gnn_ref(x, edge_index, edge_weights, W1, b1, W2, b2, W3, b3, W4, b4):
        import jax, jax.numpy as jnp
        import numpy as np
        N = 3125

        def _gcn_norm(edge_index, num_nodes):
            src = jnp.concatenate([edge_index[0], jnp.arange(num_nodes, dtype=edge_index.dtype)])
            dst = jnp.concatenate([edge_index[1], jnp.arange(num_nodes, dtype=edge_index.dtype)])
            w = jnp.ones(src.shape[0], dtype=jnp.float32)
            deg = jax.ops.segment_sum(w, dst, num_segments=num_nodes)
            dinv = jnp.where(deg > 0, jax.lax.rsqrt(deg), 0.0)
            norm = dinv[src] * w * dinv[dst]
            return (src, dst, norm)

        def _gcn_conv(h, src, dst, norm, W, b, num_nodes):
            h = h @ W
            msg = norm[:, None] * h[src]
            agg = jax.ops.segment_sum(msg, dst, num_segments=num_nodes)
            return agg + b
        src, dst, norm = _gcn_norm(edge_index, N)
        h = _gcn_conv(x, src, dst, norm, W1, b1, N)
        h = _gcn_conv(h, src, dst, norm, W2, b2, N)
        h = jax.nn.sigmoid(h)
        h = _gcn_conv(h, src, dst, norm, W3, b3, N)
        h = _gcn_conv(h, src, dst, norm, W4, b4, N)
        return jax.nn.relu(h)

    def _L1_gnn_ref(x, edge_index, edge_prob, deg_noise, gat_w, gat_a_src, gat_a_tgt, gat_b, ln_local_g, ln_local_b, ln_global_g, ln_global_b, ln2_g, ln2_b, in_proj_w, conv_w, conv_b, x_proj_w, dt_proj_w, dt_proj_b, A_log, D_param, out_proj_w, wl, wg, ff1_w, ff1_b, ff2_w, ff2_b):
        import jax, jax.numpy as jnp
        import numpy as np
        from jax import lax
        N, E, D = (512, 16384, 256)
        NH, FOUT = (4, 64)
        D_STATE, D_CONV, DT_RANK = (16, 4, 16)

        def _layer_norm(x, g, b, eps=1e-05):
            mu = jnp.mean(x, -1, keepdims=True)
            var = jnp.var(x, -1, keepdims=True)
            return (x - mu) * lax.rsqrt(var + eps) * g + b

        def _mamba(xs, in_proj_w, conv_w, conv_b, x_proj_w, dt_proj_w, dt_proj_b, A_log, D_param, out_proj_w):
            n = xs.shape[0]
            xz = xs @ in_proj_w.T
            xc, z = jnp.split(xz, 2, axis=-1)
            K = conv_w.shape[1]
            xp = jnp.pad(xc, ((K - 1, 0), (0, 0)))
            xc = sum((xp[k:k + n] * conv_w[:, k] for k in range(K))) + conv_b
            xc = jax.nn.silu(xc)
            dbc = xc @ x_proj_w.T
            dt = jax.nn.softplus(dbc[:, :DT_RANK] @ dt_proj_w.T + dt_proj_b)
            Bm = dbc[:, DT_RANK:DT_RANK + D_STATE]
            Cm = dbc[:, DT_RANK + D_STATE:]
            A = -jnp.exp(A_log)
            dA = jnp.exp(dt[:, :, None] * A)
            dBx = (dt * xc)[:, :, None] * Bm[:, None, :]

            def step(h, t):
                dA_t, dBx_t, C_t = t
                h = dA_t * h + dBx_t
                return (h, h @ C_t)
            _, y = lax.scan(step, jnp.zeros((xc.shape[1], D_STATE), xs.dtype), (dA, dBx, Cm))
            y = y + xc * D_param
            y = y * jax.nn.silu(z)
            return y @ out_proj_w.T

        def _forward(x, edge_index, deg_noise, gat_w, gat_a_src, gat_a_tgt, gat_b, ln_local_g, ln_local_b, ln_global_g, ln_global_b, ln2_g, ln2_b, in_proj_w, conv_w, conv_b, x_proj_w, dt_proj_w, dt_proj_b, A_log, D_param, out_proj_w, wl, wg, ff1_w, ff1_b, ff2_w, ff2_b):
            n = x.shape[0]
            src, tgt = (edge_index[0], edge_index[1])
            proj = (x @ gat_w.T).reshape(n, NH, FOUT)
            s_src = jnp.sum(proj * gat_a_src, -1)
            s_tgt = jnp.sum(proj * gat_a_tgt, -1)
            e = jax.nn.leaky_relu(s_src[src] + s_tgt[tgt], 0.2)
            exp_e = jnp.exp(e - jnp.max(e))
            denom = jax.ops.segment_sum(exp_e, tgt, num_segments=n)
            attn = exp_e / (denom[tgt] + 1e-16)
            agg = jax.ops.segment_sum(proj[src] * attn[:, :, None], tgt, num_segments=n)
            h_local = jax.nn.elu((agg + x.reshape(n, NH, FOUT)).reshape(n, NH * FOUT) + gat_b)
            h_local = _layer_norm(h_local, ln_local_g, ln_local_b)
            deg = jax.ops.segment_sum(jnp.ones((src.shape[0],), x.dtype), src, num_segments=n)
            perm = jnp.argsort(deg + deg_noise, stable=True)
            inv = jnp.argsort(perm)
            y = _mamba(x[perm], in_proj_w, conv_w, conv_b, x_proj_w, dt_proj_w, dt_proj_b, A_log, D_param, out_proj_w)
            h_attn = _layer_norm(x + y[inv], ln_global_g, ln_global_b)
            gate = jax.nn.sigmoid(h_local @ wl.T + h_attn @ wg.T)
            h = gate * h_local + (1.0 - gate) * h_attn
            ff = jax.nn.relu(h @ ff1_w.T + ff1_b) @ ff2_w.T + ff2_b
            return _layer_norm(h + ff, ln2_g, ln2_b)
        return _forward(x, edge_index, deg_noise, gat_w, gat_a_src, gat_a_tgt, gat_b, ln_local_g, ln_local_b, ln_global_g, ln_global_b, ln2_g, ln2_b, in_proj_w, conv_w, conv_b, x_proj_w, dt_proj_w, dt_proj_b, A_log, D_param, out_proj_w, wl, wg, ff1_w, ff1_b, ff2_w, ff2_b)

    def _L2_gnn_ref(x, weights, roots, biases, edge_index, edge_type):
        import jax, jax.numpy as jnp
        import numpy as np
        N_NODES = 3125
        N_EDGES = 18750
        N_REL = 8
        D = 256
        N_LAYERS = 3

        def _rgcn_layer(x, W, root, bias, src, dst, seg):
            agg = jax.ops.segment_sum(x[src], seg, num_segments=N_REL * N_NODES)
            agg = agg.reshape(N_REL, N_NODES, -1)
            return jnp.einsum('rnd,rde->ne', agg, W) + x @ root + bias
        src, dst = (edge_index[0], edge_index[1])
        seg = edge_type * N_NODES + dst
        h = x
        for l in range(N_LAYERS - 1):
            h = jax.nn.relu(_rgcn_layer(h, weights[l], roots[l], biases[l], src, dst, seg))
        h = jax.nn.sigmoid(_rgcn_layer(h, weights[-1], roots[-1], biases[-1], src, dst, seg))
        return h

    def _L3_gnn_ref(feat, src, dst, W, attn_l, attn_r, gat_bias, lin_W, lin_b):
        import jax, jax.numpy as jnp
        import numpy as np
        N_NODES = 6250
        N_EDGES = 100000
        IN_DIM = 256
        HID = 64
        HEADS = 2
        OUT_DIM = 256
        NEG_SLOPE = 0.2
        N = feat.shape[0]
        H, D = attn_l.shape
        h = (feat @ W).reshape(N, H, D)
        el = jnp.sum(h * attn_l[None], axis=-1)
        er = jnp.sum(h * attn_r[None], axis=-1)
        e = jax.nn.leaky_relu(el[src] + er[dst], NEG_SLOPE)
        m = jax.ops.segment_max(e, dst, num_segments=N)
        ee = jnp.exp(e - m[dst])
        s = jax.ops.segment_sum(ee, dst, num_segments=N)
        alpha = ee / s[dst]
        out = jax.ops.segment_sum(alpha[:, :, None] * h[src], dst, num_segments=N)
        out = out + gat_bias.reshape(1, H, D)
        out = jax.nn.relu(out.reshape(N, H * D))
        return jax.nn.relu(out @ lin_W + lin_b)
    edge_index = jnp.stack([src, dst])
    x = _layernorm(x + _L0_gnn_ref(x, edge_index, edge_weight, L0_gnn_W1, L0_gnn_b1, L0_gnn_W2, L0_gnn_b2, L0_gnn_W3, L0_gnn_b3, L0_gnn_W4, L0_gnn_b4), axis=-1)
    x = _layernorm(x + _L1_gnn_ref(x, edge_index, edge_weight, node_vec, L1_gnn_gat_w, L1_gnn_gat_a_src, L1_gnn_gat_a_tgt, L1_gnn_gat_b, L1_gnn_ln_local_g, L1_gnn_ln_local_b, L1_gnn_ln_global_g, L1_gnn_ln_global_b, L1_gnn_ln2_g, L1_gnn_ln2_b, L1_gnn_in_proj_w, L1_gnn_conv_w, L1_gnn_conv_b, L1_gnn_x_proj_w, L1_gnn_dt_proj_w, L1_gnn_dt_proj_b, L1_gnn_A_log, L1_gnn_D_param, L1_gnn_out_proj_w, L1_gnn_wl, L1_gnn_wg, L1_gnn_ff1_w, L1_gnn_ff1_b, L1_gnn_ff2_w, L1_gnn_ff2_b), axis=-1)
    x = _layernorm(x + _L2_gnn_ref(x, L2_gnn_weights, L2_gnn_roots, L2_gnn_biases, edge_index, edge_type_8), axis=-1)
    x = _layernorm(x + _L3_gnn_ref(x, src, dst, L3_gnn_W, L3_gnn_attn_l, L3_gnn_attn_r, L3_gnn_gat_bias, L3_gnn_lin_W, L3_gnn_lin_b), axis=-1)
    return x

_drawn_inputs = setup_inputs


def setup_inputs(seed=0):
    import zlib

    import numpy as np

    out = dict(_drawn_inputs(seed))
    spreads = {'L0_gnn_b1': (0.0, 0.377),
     'L0_gnn_b2': (0.0, 0.1),
     'L0_gnn_b3': (0.0, 0.1),
     'L0_gnn_b4': (0.0, 0.1),
     'L1_gnn_gat_b': (0.0, 0.1),
     'L1_gnn_ln_local_g': (1.0, 0.2),
     'L1_gnn_ln_local_b': (0.0, 0.1),
     'L1_gnn_ln_global_g': (1.0, 0.2),
     'L1_gnn_ln_global_b': (0.0, 0.1),
     'L1_gnn_ln2_g': (1.0, 0.2),
     'L1_gnn_ln2_b': (0.0, 0.1),
     'L1_gnn_conv_b': (0.0, 0.562),
     'L1_gnn_D_param': (1.0, 0.6),
     'L1_gnn_ff1_b': (0.0, 0.1),
     'L1_gnn_ff2_b': (0.0, 0.1),
     'L2_gnn_biases': (0.0, 0.1),
     'L3_gnn_gat_bias': (0.0, 0.335),
     'L3_gnn_lin_b': (0.0, 0.1)}
    factors = {'L0_gnn_W1': 8.0,
     'L1_gnn_gat_a_tgt': 7.546,
     'L1_gnn_x_proj_w': 8.0,
     'L1_gnn_dt_proj_w': 8.0,
     'L1_gnn_dt_proj_b': 8.0,
     'L1_gnn_A_log': 8.0,
     'L3_gnn_attn_l': 4.719,
     'L3_gnn_attn_r': 8.0}
    for name, (base, spread) in spreads.items():
        noise = np.random.default_rng([zlib.crc32(name.encode()), seed]).standard_normal(out[name].shape)
        drawn = base * np.exp(spread * noise) if base else spread * noise
        out[name] = jnp.asarray(drawn.astype(out[name].dtype))
    for name, factor in factors.items():
        out[name] = (out[name] * factor).astype(out[name].dtype)
    return out
```

```python
from contextlib import ExitStack

import concourse.bass as bass
from concourse import mybir

F32, BF16, F16, I32 = mybir.dt.float32, mybir.dt.bfloat16, mybir.dt.float16, mybir.dt.int32
ALU, ACT, AX = mybir.AluOpType, mybir.ActivationFunctionType, mybir.AxisListType

P = 128
N = 3125
D = 256
T = -(-N // P)
NP = T * P
E = 100000
C = -(-E // P)
CT = -(-C // P)
G = 4
NG = -(-C // G)
PAD = NP - 1
HALF = NP // 2
REL = 8
BANK = 512
BANKS = [(b, min(b + BANK, NP)) for b in range(0, NP, BANK)]
NEG = -2.0 ** 100
EPS = 1e-5
J = 400
NJ = NP // J


class Shared:
    pass


class Tick:

    def __init__(self, sem, eng=None):
        self.sem, self.eng, self.n, self.i, self.per, self.base = sem, eng, 0, None, 0, 0

    def loop(self, i, per):
        self.base, self.n, self.i, self.per = self.n, 0, i, per

    def end(self, turns):
        assert self.n == self.per, (self.n, self.per)
        self.n, self.i = self.base + turns * self.per, None

    def value(self):
        return self.n if self.i is None else self.i * self.per + (self.base + self.n)

    def __call__(self, ins):
        ins.then_inc(self.sem, 1)
        self.n += 1
        self.eng.wait_ge(self.sem, self.value())


class Phase:

    def __init__(self, nc, name):
        self.nc, self.name, self.ctx = nc, name, ExitStack()

    def __enter__(self):
        self.ctx.__enter__()
        return self

    def __exit__(self, *e):
        return self.ctx.__exit__(*e)

    def sb(self, name, shape, dt=F32):
        return self.ctx.enter_context(self.nc.sbuf_tensor(f"{self.name}_{name}", shape, dt))

    def ps(self, name, shape, dt=F32):
        return self.ctx.enter_context(self.nc.psum_tensor(f"{self.name}_{name}", shape, dt))

    def sem(self, name):
        return self.ctx.enter_context(self.nc.semaphore(f"{self.name}_{name}"))

    def sems(self, *names):
        return [self.sem(n) for n in names]

    def pool_sems(self, g, n):
        return [g.pool_sems.pop(0) for _ in range(n)]

    def block(self):
        return self.ctx.enter_context(self.nc.Block())


def constants(nc, g):
    with Phase(nc, "const") as ph:
        s_fill, s_sel = ph.sems("fill", "sel")
        num = ph.sb("num", [P, NP], I32)
        s_iota, s_cast = ph.sems("iota", "cast")
        block = ph.block()

        @block.gpsimd
        def _(pool):
            nc.gpsimd.memset(g.ident[:, :], 1.0).then_inc(s_fill, 1)
            nc.gpsimd.memset(g.ones[:, :], 1.0)
            nc.gpsimd.memset(g.zeros[:, :], 0.0)
            pool.wait_ge(s_fill, 1)
            nc.gpsimd.affine_select(out=g.ident[:, :], in_=g.ident[:, :], compare_op=ALU.is_equal, fill=0.0,
                                    base=0, pattern=[[-1, P]], channel_multiplier=1).then_inc(s_sel, 1)
            nc.gpsimd.iota(num[:, :], [[1, NP]], base=-HALF, channel_multiplier=0).then_inc(s_iota, 1)

        @block.vector
        def _(dve):
            dve.wait_ge(s_iota, 1)
            nc.vector.tensor_copy(g.numbers[:, :], num[:, :]).then_inc(s_cast, 1)


def edge_tables(nc, g, src, dst, kind):
    full = E // P
    tail = E - full * P
    R = CT - 1
    with Phase(nc, "edge") as ph:
        raw = ph.sb("raw", [P, 3, CT, P], I32)
        val = ph.sb("val", [P, 3, CT, P])
        node = ph.sb("node", [P, CT, P])
        ends = ph.sb("ends", [P, 2 * CT])
        endsT = ph.sb("endsT", [2 * CT, P])
        row = ph.sb("row", [32, 2, CT * P])
        gmin = ph.sb("gmin", [32, NG])
        gmax = ph.sb("gmax", [32, NG])
        gnum = ph.sb("gnum", [32, NG])
        gnumi = ph.sb("gnumi", [32, NG], I32)
        hit = ph.sb("hit", [32, NG])
        low = ph.sb("low", [32, NG])
        tmp = ph.sb("tmp", [32, NG])
        edge0 = ph.sb("edge0", [32, 2])
        edge0i = ph.sb("edge0i", [32, 2], I32)
        span = ph.sb("span", [32, 2])
        flat = ph.sb("flat", [1, 4, 32])
        psum = [ph.ps(f"t{k}", [P, CT * P]) for k in range(3)]
        pend = ph.ps("pend", [2 * CT, P])
        dram_ends = nc.dram_tensor("ends_rows", (2, CT * P), F32).ap()
        dram_span = nc.dram_tensor("span_rows", (2, 32), F32).ap()
        s_fill, s_in, s_val, s_end, s_T, s_Tc, s_st, s_row, s_v, s_io, s_sp, s_fl = ph.sems(
            "fill", "in", "val", "end", "T", "Tc", "st", "row", "v", "io", "sp", "fl")
        block = ph.block()

        @block.gpsimd
        def _(pool):
            nc.gpsimd.memset(raw[:, :, R, :], PAD).then_inc(s_fill, 1)
            nc.gpsimd.iota(gnumi[:, :], [[1, NG]], base=0, channel_multiplier=0).then_inc(s_io, 1)
            nc.gpsimd.iota(edge0i[:, :], [[P, 2]], base=0, channel_multiplier=P).then_inc(s_io, 1)

        @block.sync
        def _(sp):
            sp.wait_ge(s_fill, 1)
            for k, a in enumerate((src, dst, kind)):
                sp.dma_start(raw[:, k, 0:R, :], a[0:R * P * P].rearrange("(r c e) -> c r e", c=P, e=P)).then_inc(s_in, 16)
                sp.dma_start(raw[0:full - R * P, k, R, :],
                             a[R * P * P:full * P].rearrange("(c e) -> c e", e=P)).then_inc(s_in, 16)
                sp.dma_start(raw[full - R * P:full - R * P + 1, k, R, 0:tail],
                             a[full * P:E].rearrange("(c e) -> c e", c=1)).then_inc(s_in, 16)
            sp.wait_ge(s_Tc, 1)
            sp.dma_start(dram_ends.rearrange("k (r p) -> (k r) p", p=P), endsT[:, :]).then_inc(s_st, 16)
            sp.wait_ge(s_st, 16)
            sp.dma_start(row[:, :, :].rearrange("p k n -> p (k n)"),
                         dram_ends.rearrange("k n -> (k n)").partition_broadcast(32)).then_inc(s_row, 16)
            sp.wait_ge(s_sp, 1)
            with nc.allow_non_contiguous_dma(reason="64 numbers"):
                sp.dma_start(dram_span.rearrange("k t -> t k"), span[:, :]).then_inc(s_st, 16)
            sp.wait_ge(s_st, 32)
            sp.dma_start(flat[:, 0:2, :].rearrange("o k t -> o (k t)"),
                         dram_span.rearrange("k t -> (k t)").rearrange("(o n) -> o n", o=1)).then_inc(s_fl, 16)

        @block.tensor
        def _(pe):
            pe.wait_ge(s_val, 1)
            for k, a in enumerate((val[:, 0], val[:, 1], node[:, :, :])):
                for r in range(CT):
                    last = nc.tensor.transpose(psum[k][:, r * P:(r + 1) * P], a[:, r, :], g.ident[:, :])
            last.then_inc(s_T, 1)
            pe.wait_ge(s_end, 1)
            nc.tensor.transpose(pend[:, :], ends[:, :], g.ident[:, :]).then_inc(s_T, 1)

        @block.vector
        def _(dve):
            v = Tick(s_v, dve)
            dve.wait_ge(s_in, 9 * 16)
            v(nc.vector.tensor_copy(val[:, :, :, :], raw[:, :, :, :]))
            v(nc.vector.tensor_scalar(node[:, R, :], val[:, 2, R, :], float(REL - 1), None, ALU.min))
            v(nc.vector.tensor_copy(val[:, 2, R, :], node[:, R, :]))
            nc.vector.scalar_tensor_tensor(node[:, :, :], val[:, 2], float(NP), val[:, 0], ALU.mult, ALU.add).then_inc(s_val, 1)
            v(nc.vector.tensor_reduce(ends[:, 0:CT], val[:, 1], AX.X, ALU.min))
            nc.vector.tensor_reduce(ends[:, CT:], val[:, 1], AX.X, ALU.max).then_inc(s_end, 1)
            dve.wait_ge(s_T, 1)
            nc.vector.tensor_scalar(g.srcs[:, :], psum[0][:, :], -float(HALF), None, ALU.add)
            nc.vector.tensor_scalar(g.dsts[:, :], psum[1][:, :], -float(HALF), None, ALU.add)
            nc.vector.tensor_copy(g.rows[:, :], psum[2][:, :])
            dve.wait_ge(s_T, 2)
            nc.vector.tensor_copy(endsT[:, :], pend[:, :]).then_inc(s_Tc, 1)
            dve.wait_ge(s_io, 2)
            nc.vector.tensor_copy(gnum[:, :], gnumi[:, :])
            nc.vector.tensor_copy(edge0[:, :], edge0i[:, :])
            dve.wait_ge(s_row, 16)
            nc.vector.tensor_reduce(gmin[:, :], row[:, 0, 0:NG * G].rearrange("p (n g) -> p n g", g=G), AX.X, ALU.min)
            v(nc.vector.tensor_reduce(gmax[:, :], row[:, 1, 0:NG * G].rearrange("p (n g) -> p n g", g=G), AX.X, ALU.max))
            v(nc.vector.tensor_scalar(tmp[:, :], gmin[:, :], edge0[:, 1:2], None, ALU.is_lt))
            v(nc.vector.scalar_tensor_tensor(hit[:, :], gmax[:, :], edge0[:, 0:1], tmp[:, :], ALU.is_ge, ALU.mult))
            v(nc.vector.scalar_tensor_tensor(low[:, :], hit[:, :], -1e6, gnum[:, :], ALU.mult, ALU.add))
            v(nc.vector.tensor_scalar(low[:, :], low[:, :], 1e6, float(NG - 1), ALU.add, ALU.min))
            v(nc.vector.scalar_tensor_tensor(tmp[:, :], gnum[:, :], 1.0, hit[:, :], ALU.add, ALU.mult))
            v(nc.vector.tensor_reduce(span[:, 0:1], low[:, :], AX.X, ALU.min))
            v(nc.vector.tensor_reduce(span[:, 1:2], tmp[:, :], AX.X, ALU.max))
            v(nc.vector.tensor_tensor(span[:, 1:2], span[:, 1:2], span[:, 0:1], ALU.subtract))
            nc.vector.tensor_scalar(span[:, 1:2], span[:, 1:2], 1.0, None, ALU.max).then_inc(s_sp, 1)
            dve.wait_ge(s_fl, 16)
            v(nc.vector.memset(flat[:, 3, :], 1.0))
            v(nc.vector.tensor_tensor_scan(flat[:, 2, :], flat[:, 3, :], flat[:, 1, :], 0.0, ALU.mult, ALU.add))
            v(nc.vector.tensor_tensor(flat[:, 2, :], flat[:, 2, :], flat[:, 1, :], ALU.subtract))
            nc.vector.tensor_copy(g.spans[:, :, :], flat[:, 0:3, :])


def span_of(eng, g, t):
    first = eng.value_load(g.spans[0:1, 0, bass.ds(t, 1)], min_val=0, max_val=NG - 1)
    count = eng.value_load(g.spans[0:1, 1, bass.ds(t, 1)], min_val=1, max_val=NG)
    before = eng.value_load(g.spans[0:1, 2, bass.ds(t, 1)], min_val=0, max_val=T * NG)
    return first, count, before


def group_start(nc, group):
    return nc.s_assert_within(group * G, 0, (NG - 1) * G, skip_runtime_bounds_check_because="spans end at NG")


def adjacency(nc, g):
    with Phase(nc, "adj") as ph:
        to = ph.sb("to", [P, 2, P], BF16)
        frm = ph.sb("frm", [P, 2, NP], BF16)
        counts = ph.sb("counts", [P, NP])
        miss = ph.sb("miss", [P, NP], BF16)
        outsum = ph.sb("outsum", [P, NP])
        turned = ph.sb("turned", [P, T, P])
        acc = ph.ps("acc", [P, NP])
        tp = ph.ps("tp", [P, BANK])
        s_hot, s_used, s_sum, s_copied, s_masked, s_miss, s_adj, s_tp, s_tpc, s_ab, s_out, s_bc, s_z = ph.sems(
            "hot", "used", "sum", "copied", "masked", "miss", "adjst", "tp", "tpc", "ab", "out", "bc", "z")
        s_v = ph.sem("v")
        rounds = [range(r, min(r + 4, T)) for r in range(0, T, 4)]
        block = ph.block()

        @block.vector
        def _(dve):
            nc.vector.memset(outsum[:, :], 0.0).then_inc(s_v, 1)
            with dve.Fori(0, T, 1) as t:
                first, count, before = span_of(dve, g, t)
                with dve.Fori(0, count, 1) as j:
                    c0 = group_start(nc, first + j)
                    for u in range(G):
                        c = c0 + u
                        dve.wait_ge(s_used, (before + j) * G + (u + 1))
                        nc.vector.tensor_scalar(to[:, u % 2, :], g.numbers[:, bass.ds(t * P, P)],
                                                g.dsts[:, bass.ds(c, 1)], None, ALU.is_equal)
                        nc.vector.tensor_scalar(frm[:, u % 2, :], g.numbers[:, :],
                                                g.srcs[:, bass.ds(c, 1)], None, ALU.is_equal).then_inc(s_hot, 1)
                dve.wait_ge(s_copied, t + 1)
                dve.wait_ge(s_miss, t * 16)
                nc.vector.tensor_scalar(miss[:, :], counts[:, :], 0.0, NEG, ALU.is_equal, ALU.mult).then_inc(s_masked, 1)
                dve.wait_ge(s_v, t + 1)
                nc.vector.tensor_tensor(outsum[:, :], outsum[:, :], counts[:, :], ALU.add).then_inc(s_v, 1)
            dve.wait_ge(s_bc, 1)
            nc.vector.tensor_copy(g.outdeg[:, :], acc[:, :])

        @block.tensor
        def _(pe):
            pe.sem_inc(s_used, 2)
            with pe.Fori(0, T, 1) as t:
                first, count, before = span_of(pe, g, t)
                pe.wait_ge(s_copied, t)
                for a, b in BANKS:
                    nc.tensor.matmul(acc[:, a:b], g.zeros[:, 0:P], g.zeros[:, 0:b - a], start=True, stop=False)
                with pe.Fori(0, count, 1) as j:
                    for u in range(G):
                        pe.wait_ge(s_hot, (before + j) * G + (u + 1))
                        for a, b in BANKS:
                            last = nc.tensor.matmul(acc[:, a:b], to[:, u % 2, :], frm[:, u % 2, a:b], start=False, stop=False)
                        last.then_inc(s_used, 1)
                for a, b in BANKS:
                    last = nc.tensor.matmul(acc[:, a:b], g.zeros[:, 0:P], g.zeros[:, 0:b - a], start=False, stop=True)
                last.then_inc(s_sum, 1)
                pe.wait_ge(s_copied, t + 1)
                for k, rnd in enumerate(rounds):
                    pe.wait_ge(s_tpc, t * len(rounds) + k)
                    for n, s in enumerate(rnd):
                        last = nc.tensor.transpose(tp[:, n * P:(n + 1) * P], counts[:, s * P:(s + 1) * P], g.ident[:, :])
                    last.then_inc(s_tp, 1)
            pe.wait_ge(s_v, T + 1)
            for a, b in BANKS:
                last = nc.tensor.matmul(acc[:, a:b], g.ones[:, :], outsum[:, a:b], start=True, stop=True)
            last.then_inc(s_bc, 1)

        @block.scalar
        def _(act):
            with act.Fori(0, T, 1) as t:
                act.wait_ge(s_sum, t + 1)
                act.wait_ge(s_tp, t * len(rounds))
                act.wait_ge(s_v, t + 1)
                nc.scalar.activation(counts[:, :], acc[:, :], ACT.Copy,
                                     accum_out=g.indeg[:, bass.ds(t, 1)]).then_inc(s_copied, 1)
                act.wait_ge(s_adj, t * 16)
                for k, rnd in enumerate(rounds):
                    act.wait_ge(s_tp, t * len(rounds) + (k + 1))
                    nc.scalar.copy(turned[:, rnd[0]:rnd[-1] + 1, :].rearrange("p a b -> p (a b)"),
                                   tp[:, 0:len(rnd) * P]).then_inc(s_tpc, 1)

        @block.sync
        def _(sp):
            with sp.Fori(0, T, 1) as t:
                a = sp.snap(t * P)
                masked, turned_ = sp.snap(t + 1), sp.snap((t + 1) * len(rounds))
                sp.wait_ge(s_masked, masked)
                sp.sem_inc(g.waited, 1)
                sp.dma_start(g.absent[bass.ds(a, P), :], miss[:, :]).then_inc(s_miss, 16)
                sp.wait_ge(s_tpc, turned_)
                sp.sem_inc(g.waited, 1)
                sp.dma_start(g.adj[:, bass.ds(a, P)].rearrange("(s p) d -> p s d", p=P),
                             turned[:, :, :]).then_inc(s_adj, 16)
            sp.wait_ge(s_miss, T * 16)
            sp.wait_ge(s_adj, T * 16)


def turned_weights(nc, name, g, jobs):
    blocks = []
    for n, (w, out) in enumerate(jobs):
        O, I = w.shape
        for o in range(0, O, P):
            for k in range(0, I, P):
                blocks.append((n, o, min(P, O - o), k, min(P, I - k)))
    with Phase(nc, name) as ph:
        raw = [ph.sb(f"raw{n}", [min(P, w.shape[0]), -(-w.shape[0] // P), w.shape[1]]) for n, (w, _) in enumerate(jobs)]
        tp = [ph.ps(f"tp{k}", [P, P]) for k in range(4)]
        s_in, s_t, s_c = ph.sems("in", "t", "c")
        block = ph.block()

        @block.sync
        def _(sp):
            for (w, _), r in zip(jobs, raw):
                sp.dma_start(r[:, :, :], w.rearrange("(a p) i -> p a i", p=min(P, w.shape[0]))).then_inc(s_in, 16)

        @block.tensor
        def _(pe):
            pe.wait_ge(s_in, 16 * len(jobs))
            for b, (n, o, no, k, ni) in enumerate(blocks):
                if b >= 4:
                    pe.wait_ge(s_c, b - 3)
                nc.tensor.transpose(tp[b % 4][0:ni, 0:no], raw[n][0:no, o // P, k:k + ni], g.ident[0:no, 0:no]).then_inc(s_t, 1)

        @block.scalar
        def _(act):
            for b, (n, o, no, k, ni) in enumerate(blocks):
                act.wait_ge(s_t, b + 1)
                nc.scalar.copy(jobs[n][1][0:ni, k // P, o:o + no], tp[b % 4][0:ni, 0:no]).then_inc(s_c, 1)


def project(nc, name, g, x, weights, width, store, scale=None, extra=None, ones_at=None):
    chunks = [(a, min(a + BANK, width)) for a in range(0, width, BANK)]
    heads = ones_at or 0
    out_width = width + heads
    with Phase(nc, name) as ph:
        tile = [ph.sb(f"tile{u}", [P, D]) for u in range(2)]
        turned = [ph.sb(f"turned{u}", [P, 2, P]) for u in range(2)]
        res = [ph.sb(f"res{u}", [P, out_width]) for u in range(2)]
        tp = ph.ps("tp", [P, D])
        mm = [ph.ps(f"mm{n}", [P, BANK]) for n in range(len(chunks))]
        s_in = ph.sems("in0", "in1")
        s_st = ph.pool_sems(g, 2)
        s_free, s_tp, s_turn, s_mm, s_done, s_one = ph.sems("free", "tp", "turn", "mm", "done", "one")
        nst = len(store(0))
        block = ph.block()

        def turns(eng, step):
            with eng.Fori(0, T // 2, 1) as i:
                step(2 * i, i, 0)
                step(2 * i + 1, i, 1)
            step(T - 1, T // 2, 0)

        @block.sync
        def _(sp):
            def step(t, i, u):
                a = sp.snap(t * P) if not isinstance(t, int) else t * P
                need = sp.snap(t + 1) if not isinstance(t, int) else t + 1
                sp.wait_ge(s_free, need)
                sp.sem_inc(g.waited, 1)
                sp.dma_start(tile[u][:, :], x[bass.ds(a, P), :]).then_inc(s_in[u], 16)
            turns(sp, step)

        @block.tensor
        def _(pe):
            pe.sem_inc(s_free, 2)

            def step(t, i, u):
                pe.wait_ge(s_in[u], (i + 1) * 16)
                pe.wait_ge(s_turn, t)
                for k in range(2):
                    last = nc.tensor.transpose(tp[:, k * P:(k + 1) * P], tile[u][:, k * P:(k + 1) * P], g.ident[:, :])
                last.then_inc(s_tp, 1)
                pe.wait_ge(s_turn, t + 1)
                pe.wait_ge(s_done, t)
                for n, (a, b) in enumerate(chunks):
                    for k in range(2):
                        last = nc.tensor.matmul(mm[n][:, 0:b - a], turned[u][:, k, :], weights[:, k, a:b],
                                                start=k == 0, stop=k == 1)
                last.then_inc(s_mm, 1)
                pe.sem_inc(s_free, 1)
            turns(pe, step)

        @block.scalar
        def _(act):
            def step(t, i, u):
                act.wait_ge(s_tp, t + 1)
                nc.scalar.copy(turned[u][:, :, :].rearrange("p k n -> p (k n)"), tp[:, :]).then_inc(s_turn, 1)
            turns(act, step)

        @block.vector
        def _(dve):
            if heads:
                for u in range(2):
                    nc.vector.memset(res[u][:, 0:heads * 65], 1.0).then_inc(s_one, 1)
                dve.wait_ge(s_one, 2)

            def step(t, i, u):
                dve.wait_ge(s_mm, t + 1)
                dve.wait_ge(s_st[u], i * (16 * nst))
                for n, (a, b) in enumerate(chunks):
                    if heads:
                        nc.vector.tensor_copy(res[u][:, 0:heads * 65].rearrange("p (h c) -> p h c", c=65)[:, :, 0:64],
                                              mm[n][:, 0:heads * 64].rearrange("p (h c) -> p h c", c=64))
                        nc.vector.tensor_copy(extra[:, bass.ds(t, 1), :].rearrange("p a c -> p (a c)"),
                                              mm[n][:, heads * 64:width])
                        last = nc.vector.tensor_copy(res[u][:, heads * 65:], mm[n][:, heads * 64:width])
                    elif scale is not None:
                        last = nc.vector.tensor_scalar(res[u][:, a:b], mm[n][:, 0:b - a], scale[:, bass.ds(t, 1)], None, ALU.mult)
                    else:
                        last = nc.vector.tensor_copy(res[u][:, a:b], mm[n][:, 0:b - a])
                last.then_inc(s_done, 1)
            turns(dve, step)

        @block.gpsimd
        def _(pool):
            def step(t, i, u):
                jobs = store(t)
                pool.wait_ge(s_done, t + 1)
                for to, (a, b) in jobs:
                    pool.dma_start(to, res[u][:, a:b]).then_inc(s_st[u], 16)
            turns(pool, step)
            pool.wait_ge(s_st[0], (T - T // 2) * 16 * nst)
            pool.wait_ge(s_st[1], (T // 2) * 16 * nst)


def aggregate(nc, name, g, F, y_dram, out):
    with Phase(nc, name) as ph:
        rows = [ph.sb(f"rows{u}", [P, NP]) for u in range(2)]
        ys = [ph.sb(f"ys{u}", [P, F]) for u in range(2)]
        sums = ph.sb("sums", [F, NP])
        per = BANK // F
        s_in = ph.sems("in0", "in1")
        s_free, s_done, s_c, s_t, s_o = ph.sems("free", "done", "c", "t", "o")
        with ExitStack() as own:
            acc = own.enter_context(nc.psum_tensor(f"{name}_acc", [F, NP], F32))
            tp = own.enter_context(nc.psum_tensor(f"{name}_tp", [P, BANK], F32))
            rounds = [range(a, min(a + per, T)) for a in range(0, T, per)]
            with nc.Block() as block:
                @block.sync
                def _(sp):
                    def step(t, i, u):
                        a = sp.snap(t * P) if not isinstance(t, int) else t * P
                        need = sp.snap(t + 1) if not isinstance(t, int) else t + 1
                        sp.wait_ge(s_free, need)
                        sp.sem_inc(g.waited, 1)
                        sp.dma_start(rows[u][:, :], g.adj[bass.ds(a, P), :]).then_inc(s_in[u], 16)
                        sp.dma_start(ys[u][:, :], y_dram[bass.ds(a, P), :]).then_inc(s_in[u], 16)
                    with sp.Fori(0, T // 2, 1) as i:
                        step(2 * i, i, 0)
                        step(2 * i + 1, i, 1)
                    step(T - 1, T // 2, 0)

                @block.tensor
                def _(pe):
                    pe.sem_inc(s_free, 2)
                    for a, b in BANKS:
                        nc.tensor.matmul(acc[:, a:b], g.zeros[:, 0:F], g.zeros[:, 0:b - a], start=True, stop=False)

                    def step(i, u, stop):
                        pe.wait_ge(s_in[u], (i + 1) * 32)
                        for a, b in BANKS:
                            last = nc.tensor.matmul(acc[:, a:b], ys[u][:, :], rows[u][:, a:b], start=False, stop=stop)
                        last.then_inc(s_free, 1)
                    with pe.Fori(0, T // 2, 1) as i:
                        step(i, 0, False)
                        step(i, 1, False)
                    step(T // 2, 0, True)
                    for k, rnd in enumerate(rounds):
                        pe.wait_ge(s_c, min(len(BANKS), rnd[-1] * P // BANK + 1))
                        if k:
                            pe.wait_ge(s_o, k)
                        for n, t in enumerate(rnd):
                            last = nc.tensor.transpose(tp[:, n * F:(n + 1) * F], sums[:, t * P:(t + 1) * P], g.ident[0:F, 0:F])
                        last.then_inc(s_t, 1)

                @block.scalar
                def _(act):
                    act.wait_ge(s_free, T + 2)
                    for a, b in BANKS:
                        nc.scalar.copy(sums[:, a:b], acc[:, a:b]).then_inc(s_c, 1)

                @block.vector
                def _(dve):
                    for k, rnd in enumerate(rounds):
                        dve.wait_ge(s_t, k + 1)
                        nc.vector.tensor_copy(out[:, rnd[0]:rnd[-1] + 1, :].rearrange("p t f -> p (t f)"),
                                              tp[:, 0:len(rnd) * F]).then_inc(s_o, 1)


class Norm:

    def __init__(self, ph, name, scratch, width=D):
        self.w, self.width = scratch, width
        self.mean, self.var, self.std, self.eps = (ph.sb(f"{name}_{n}", [P, T]) for n in ("mean", "var", "std", "eps"))
        self.s_var, self.s_std = ph.sems(f"{name}_var", f"{name}_std")

    def dve(self, nc, dve, v, x, gain=None, shift=None):
        wide = lambda a: a[:, :].unsqueeze(2).to_broadcast([P, T, self.width])
        v(nc.vector.memset(self.eps[:, :], EPS))
        v(nc.vector.tensor_reduce(self.mean[:, :], x[:, :, :], AX.X, ALU.add))
        v(nc.vector.tensor_scalar(self.mean[:, :], self.mean[:, :], 1.0 / self.width, None, ALU.mult))
        v(nc.vector.tensor_tensor(x[:, :, :], x[:, :, :], wide(self.mean), ALU.subtract))
        v(nc.vector.tensor_tensor(self.w[:, :, :], x[:, :, :], x[:, :, :], ALU.mult))
        nc.vector.tensor_reduce(self.var[:, :], self.w[:, :, :], AX.X, ALU.add).then_inc(self.s_var, 1)
        dve.wait_ge(self.s_std, 1)
        v(nc.vector.reciprocal(self.std[:, :], self.std[:, :]))
        v(nc.vector.tensor_tensor(x[:, :, :], x[:, :, :], wide(self.std), ALU.mult))
        if gain is not None:
            along = lambda a: a[:, :].unsqueeze(1).to_broadcast([P, T, self.width])
            v(nc.vector.tensor_tensor(x[:, :, :], x[:, :, :], along(gain), ALU.mult))
            v(nc.vector.tensor_tensor(x[:, :, :], x[:, :, :], along(shift), ALU.add))

    def act(self, nc, act):
        act.wait_ge(self.s_var, 1)
        nc.scalar.activation(self.std[:, :], self.var[:, :], ACT.Sqrt, bias=self.eps[:, 0:1],
                             scale=1.0 / self.width).then_inc(self.s_std, 1)


def nodes(a):
    return a.rearrange("(t p) f -> p t f", p=P)


def row(a):
    return a.partition_broadcast(P)


def load_x(nc, g, x, x_dram):
    with Phase(nc, "loadx") as ph:
        buf = ph.sb("buf", [P, T, D])
        s_z, s_in, s_st, s_v, s_d = ph.sems("z", "in", "st", "v", "d")
        whole = N // P
        block = ph.block()

        @block.vector
        def _(dve):
            nc.vector.memset(buf[:, whole, :], 0.0).then_inc(s_z, 1)
            nc.vector.tensor_scalar(g.dinv[:, :], g.indeg[:, :], 1.0, None, ALU.add).then_inc(s_v, 1)
            dve.wait_ge(s_d, 1)
            nc.vector.reciprocal(g.dinv[:, :], g.dinv[:, :])

        @block.scalar
        def _(act):
            act.wait_ge(s_v, 1)
            nc.scalar.activation(g.dinv[:, :], g.dinv[:, :], ACT.Sqrt).then_inc(s_d, 1)

        @block.sync
        def _(sp):
            sp.wait_ge(s_z, 1)
            sp.dma_start(buf[:, 0:whole, :], nodes(x[0:whole * P, :])).then_inc(s_in, 16)
            sp.dma_start(buf[0:N - whole * P, whole, :], x[whole * P:N, :]).then_inc(s_in, 16)
            sp.wait_ge(s_in, 32)
            sp.dma_start(nodes(x_dram), buf[:, :, :]).then_inc(s_st, 16)
            sp.wait_ge(s_st, 16)


def gcn_stack(nc, g, x_dram, W1, b1, W2, b2, W3, b3, W4, b4, x_out):
    F = 64
    with Phase(nc, "gcn") as top:
        w12 = top.sb("w12", [P, 2, F])
        w34 = top.sb("w34", [F + 1, D])
        b1w2 = top.sb("b1w2", [P, F])
        b2r = top.sb("b2r", [P, F])
        b4r = top.sb("b4r", [P, D])
        y_dram = nc.dram_tensor("gcn_y", (NP, F), F32).ap()
        y1_dram = nc.dram_tensor("gcn_y1", (NP, F + 1), F32).ap()
        with Phase(nc, "gcnw") as ph:
            w1 = ph.sb("w1", [P, 2, P])
            w1T = ph.sb("w1T", [P, D])
            w2 = ph.sb("w2", [P, F])
            w3b = ph.sb("w3b", [F + 1, P])
            w3bT = ph.sb("w3bT", [P, F + 1])
            w4 = ph.sb("w4", [P, D])
            b1c = ph.sb("b1c", [P, 1])
            b1b = ph.sb("b1b", [P, P])
            tp = ph.ps("tp", [P, BANK])
            mm = ph.ps("mm", [P, BANK])
            s_in, s_t, s_tc, s_m, s_b = ph.sems("in", "t", "tc", "m", "b")
            block = ph.block()

            @block.sync
            def _(sp):
                for to, a in ((w1[:, :, :], W1.rearrange("(k p) n -> p k n", p=P)), (w2[:, :], W2), (w3b[0:F, :], W3),
                              (w3b[F:F + 1, :], b3.rearrange("(o n) -> o n", o=1)), (w4[:, :], W4),
                              (b1c[:, :], b1.rearrange("(n o) -> n o", o=1)), (b2r[:, :], row(b2)), (b4r[:, :], row(b4))):
                    sp.dma_start(to, a).then_inc(s_in, 16)

            @block.tensor
            def _(pe):
                pe.wait_ge(s_in, 8 * 16)
                for k in range(2):
                    nc.tensor.transpose(tp[:, k * P:(k + 1) * P], w1[:, k, :], g.ident[:, :])
                nc.tensor.transpose(tp[:, D:D + F + 1], w3b[:, :], g.ident[0:F + 1, 0:F + 1]).then_inc(s_t, 1)
                pe.wait_ge(s_tc, 1)
                for k in range(2):
                    nc.tensor.matmul(mm[:, k * F:(k + 1) * F], w1T[:, k * P:(k + 1) * P], w2[:, :], start=True, stop=True)
                nc.tensor.matmul(mm[:, P:P + F], b1b[:, :], w2[:, :], start=True, stop=True)
                nc.tensor.matmul(mm[0:F + 1, D:2 * D], w3bT[:, :], w4[:, :], start=True, stop=True).then_inc(s_m, 1)

            @block.vector
            def _(dve):
                dve.wait_ge(s_in, 8 * 16)
                nc.vector.tensor_copy(b1b[:, :], b1c[:, 0:1].to_broadcast([P, P]))
                dve.wait_ge(s_t, 1)
                nc.vector.tensor_copy(w1T[:, :], tp[:, 0:D])
                nc.vector.tensor_copy(w3bT[:, :], tp[:, D:D + F + 1]).then_inc(s_tc, 1)
                dve.wait_ge(s_m, 1)
                nc.vector.tensor_copy(w12[:, :, :].rearrange("p k n -> p (k n)"), mm[:, 0:P])
                nc.vector.tensor_copy(b1w2[:, :], mm[:, P:P + F])
                nc.vector.tensor_copy(w34[:, :], mm[0:F + 1, D:2 * D])

        project(nc, "gcnp", g, x_dram, w12, F, lambda t: [(y_dram[bass.ds(t * P, P), :], (0, F))], scale=g.dinv)
        with Phase(nc, "gcns") as st:
            y = st.sb("y", [P, T, F + 1])
            a64 = st.sb("a64", [P, T, F])
            a65 = st.sb("a65", [P, T, F + 1])
            y64 = st.sb("y64", [P, T, F])
            for n in range(4):
                a, yy = (a64, y64) if n < 2 else (a65, y)
                width = F if n < 2 else F + 1
                aggregate(nc, f"agg{n}", g, width, y_dram if n < 2 else y1_dram, a)
                if n == 3:
                    break
                with Phase(nc, f"gcnc{n}") as ph:
                    s_in, s_v, s_a, s_b, s_st = ph.sems("in", "v", "a", "b", "st")
                    block = ph.block()
                    wide = lambda w: g.dinv[:, :].unsqueeze(2).to_broadcast([P, T, w])
                    along = lambda r: r[:, :].unsqueeze(1).to_broadcast([P, T, F])

                    @block.sync
                    def _(sp):
                        if n == 0:
                            sp.dma_start(y64[:, :, :], nodes(y_dram)).then_inc(s_in, 16)
                        sp.wait_ge(s_b, 1)
                        if n == 0:
                            sp.dma_start(nodes(y_dram), y64[:, :, :]).then_inc(s_st, 16)
                        else:
                            sp.dma_start(nodes(y1_dram), y[:, :, :]).then_inc(s_st, 16)
                        sp.wait_ge(s_st, 16)

                    @block.vector
                    def _(dve):
                        v = Tick(s_v, dve)
                        if n == 0:
                            dve.wait_ge(s_in, 16)
                        v(nc.vector.tensor_tensor(a[:, :, :], a[:, :, :], yy[:, :, :], ALU.add))
                        v(nc.vector.tensor_tensor(a[:, :, :], a[:, :, :], wide(width), ALU.mult))
                        if n == 0:
                            v(nc.vector.tensor_tensor(a[:, :, :], a[:, :, :], along(b1w2), ALU.add))
                            nc.vector.tensor_tensor(y64[:, :, :], a[:, :, :], wide(F), ALU.mult).then_inc(s_b, 1)
                        elif n == 1:
                            nc.vector.tensor_tensor(a[:, :, :], a[:, :, :], along(b2r), ALU.add).then_inc(s_a, 1)
                            v(nc.vector.memset(y[:, :, F:F + 1], 1.0))
                            dve.wait_ge(s_a, 2)
                            nc.vector.tensor_tensor(y[:, :, :], y[:, :, :], wide(F + 1), ALU.mult).then_inc(s_b, 1)
                        else:
                            v(nc.vector.memset(a[:, :, F:F + 1], 1.0))
                            nc.vector.tensor_tensor(y[:, :, :], a[:, :, :], wide(F + 1), ALU.mult).then_inc(s_b, 1)

                    @block.scalar
                    def _(act):
                        if n == 1:
                            act.wait_ge(s_a, 1)
                            nc.scalar.activation(y[:, :, 0:F], a[:, :, :], ACT.Sigmoid).then_inc(s_a, 1)
            with Phase(nc, "gcno") as ph:
                x = ph.sb("x", [P, T, D])
                w = ph.sb("w", [P, T, D])
                turned = [ph.sb(f"turned{u}", [F + 1, 2 * P]) for u in range(2)]
                norm = Norm(ph, "n", w)
                tp = [ph.ps(f"tp{u}", [F + 1, BANK]) for u in range(2)]
                mm = [ph.ps(f"mm{u}", [P, BANK]) for u in range(2)]
                s_in, s_v, s_a, s_t, s_c, s_m, s_r, s_o, s_st = ph.sems("in", "v", "a", "t", "c", "m", "r", "o", "st")
                pairs = [range(a, min(a + 2, T)) for a in range(0, T, 2)]
                block = ph.block()

                @block.sync
                def _(sp):
                    sp.dma_start(x[:, :, :], nodes(x_dram)).then_inc(s_in, 16)
                    sp.wait_ge(s_o, 1)
                    sp.dma_start(nodes(x_out), x[:, :, :]).then_inc(s_st, 16)
                    sp.wait_ge(s_st, 16)

                @block.tensor
                def _(pe):
                    pe.wait_ge(s_a, 1)
                    for k, pr in enumerate(pairs):
                        if k > 1:
                            pe.wait_ge(s_c, k - 1)
                        for n, t in enumerate(pr):
                            last = nc.tensor.transpose(tp[k % 2][:, n * P:(n + 1) * P], a65[:, t, :], g.ident[:, :])
                        last.then_inc(s_t, 1)
                        pe.wait_ge(s_c, k + 1)
                        if k > 1:
                            pe.wait_ge(s_r, k - 1)
                        for n, t in enumerate(pr):
                            last = nc.tensor.matmul(mm[k % 2][:, n * D:(n + 1) * D], turned[k % 2][:, n * P:(n + 1) * P], w34[:, :],
                                                    start=True, stop=True)
                        last.then_inc(s_m, 1)

                @block.scalar
                def _(act):
                    for k, pr in enumerate(pairs):
                        act.wait_ge(s_t, k + 1)
                        nc.scalar.copy(turned[k % 2][:, 0:len(pr) * P], tp[k % 2][:, 0:len(pr) * P]).then_inc(s_c, 1)
                    norm.act(nc, act)

                @block.vector
                def _(dve):
                    v = Tick(s_v, dve)
                    wide = g.dinv[:, :].unsqueeze(2).to_broadcast([P, T, F + 1])
                    v(nc.vector.tensor_tensor(a65[:, :, :], a65[:, :, :], y[:, :, :], ALU.add))
                    nc.vector.tensor_tensor(a65[:, :, :], a65[:, :, :], wide, ALU.mult).then_inc(s_a, 1)
                    for k, pr in enumerate(pairs):
                        dve.wait_ge(s_m, k + 1)
                        nc.vector.tensor_tensor(w[:, pr[0]:pr[-1] + 1, :],
                                                mm[k % 2][:, 0:len(pr) * D].rearrange("p (t d) -> p t d", d=D),
                                                b4r[:, :].unsqueeze(1).to_broadcast([P, len(pr), D]), ALU.add).then_inc(s_r, 1)
                    dve.wait_ge(s_r, len(pairs))
                    dve.wait_ge(s_in, 16)
                    v(nc.vector.scalar_tensor_tensor(x[:, :, :], w[:, :, :], 0.0, x[:, :, :], ALU.max, ALU.add))
                    norm.dve(nc, dve, v, x)
                    dve.sem_inc(s_o, 1)


def rank_nodes(nc, g, noise, outdeg):
    with Phase(nc, "rank") as ph:
        key = ph.sb("key", [P, NP])
        nrow = ph.sb("nrow", [P, N])
        keyc = ph.sb("keyc", [P, T])
        own = ph.sb("own", [P, T])
        owni = ph.sb("owni", [P, T], I32)
        before = ph.sb("before", [P, NP], BF16)
        same = ph.sb("same", [P, NP], BF16)
        less = ph.sb("less", [P, NP], BF16)
        rank = ph.sb("rank", [P, T])
        key_dram = nc.dram_tensor("key_row", (1, NP), F32).ap()
        s_in, s_v, s_k, s_st, s_kc, s_io = ph.sems("in", "v", "k", "st", "kc", "io")
        block = ph.block()

        @block.gpsimd
        def _(pool):
            nc.gpsimd.iota(owni[:, :], [[P, T]], base=-HALF, channel_multiplier=1).then_inc(s_io, 1)

        @block.sync
        def _(sp):
            sp.dma_start(nrow[:, :], row(noise)).then_inc(s_in, 16)
            sp.wait_ge(s_k, 1)
            sp.dma_start(key_dram, key[0:1, :]).then_inc(s_st, 16)
            sp.wait_ge(s_st, 16)
            with nc.allow_non_contiguous_dma(reason="one key for each node"):
                sp.dma_start(keyc[:, :], key_dram.rearrange("o (t p) -> p (o t)", p=P)).then_inc(s_kc, 16)

        @block.vector
        def _(dve):
            v = Tick(s_v, dve)
            dve.wait_ge(s_in, 16)
            v(nc.vector.memset(key[:, N:NP], 1e30))
            nc.vector.tensor_tensor(key[:, 0:N], outdeg[:, 0:N], nrow[:, :], ALU.add).then_inc(s_k, 1)
            dve.wait_ge(s_io, 1)
            v(nc.vector.tensor_copy(own[:, :], owni[:, :]))
            dve.wait_ge(s_kc, 16)
            with dve.Fori(0, T, 1) as t:
                v.loop(t, 4)
                at = bass.ds(t, 1)
                v(nc.vector.tensor_scalar(before[:, :], g.numbers[:, :], own[:, at], None, ALU.is_lt))
                v(nc.vector.scalar_tensor_tensor(same[:, :], key[:, :], keyc[:, at], before[:, :], ALU.is_equal, ALU.mult))
                v(nc.vector.scalar_tensor_tensor(less[:, :], key[:, :], keyc[:, at], same[:, :], ALU.is_lt, ALU.add))
                v(nc.vector.tensor_reduce(rank[:, at], less[:, :], AX.X, ALU.add))
            v.end(T)
            nc.vector.tensor_copy(g.rank[:, :], rank[:, :])


def score_rows(nc, name, g, H, extra, row_dram, col0=0):
    W = extra.shape[2]
    half = [(0, 13), (13, T)]
    with Phase(nc, name) as ph:
        rows = [ph.sb(f"rows{k}", [13 * W, P]) for k in range(2)]
        tp = [ph.ps(f"tp{k}", [13 * W, P]) for k in range(2)]
        s_t, s_c, s_st = ph.sems("t", "c", "st")
        block = ph.block()

        @block.tensor
        def _(pe):
            for k, (a, b) in enumerate(half):
                nc.tensor.transpose(tp[k][0:(b - a) * W, :], extra[:, a:b, :].rearrange("p t c -> p (t c)"), g.ident[:, :]).then_inc(s_t, 1)

        @block.vector
        def _(dve):
            for k, (a, b) in enumerate(half):
                dve.wait_ge(s_t, k + 1)
                nc.vector.tensor_copy(rows[k][0:(b - a) * W, :], tp[k][0:(b - a) * W, :]).then_inc(s_c, 1)

        @block.sync
        def _(sp):
            for k, (a, b) in enumerate(half):
                sp.wait_ge(s_c, k + 1)
                for t in range(a, b):
                    sp.dma_start(row_dram[:, t * P:(t + 1) * P], rows[k][(t - a) * W:(t - a + 1) * W, :]).then_inc(s_st, 16)
            sp.wait_ge(s_st, 16 * T)


def attention(nc, name, g, H, pr_dram, scores, agg_dram, by_target):
    with Phase(nc, name) as top:
        rows_dram = nc.dram_tensor(f"{name}_scores", (2 * H, NP), F32).ap()
        m_dram = nc.dram_tensor(f"{name}_best", (H, NP), F32).ap()
        score_rows(nc, f"{name}s", g, H, scores, rows_dram)
        top_m = top.sb("m", [P, T, H])
        with Phase(nc, f"{name}m") as ph:
            srow = ph.sb("srow", [P, H, NP])
            gone = [ph.sb(f"gone{u}", [P, NP], BF16) for u in range(2)]
            junk = ph.sb("junk", [P, H, NP], BF16)
            top4 = ph.sb("top4", [P, 2, H])
            best = ph.sb("best", [P, T, H])
            s_row, s_used, s_v, s_x = ph.sems("row", "used", "v", "x")
            s_in = ph.sems("in0", "in1")
            block = ph.block()

            @block.sync
            def _(sp):
                sp.dma_start(srow[:, :, :].rearrange("p h n -> p (h n)"),
                             row(rows_dram[0:H, :].rearrange("h n -> (h n)"))).then_inc(s_row, 16)

                def step(t, i, u):
                    a = sp.snap(t * P) if not isinstance(t, int) else t * P
                    need = sp.snap(t + 1) if not isinstance(t, int) else t + 1
                    sp.wait_ge(s_used, need)
                    sp.sem_inc(g.waited, 1)
                    sp.dma_start(gone[u][:, :], g.absent[bass.ds(a, P), :]).then_inc(s_in[u], 16)
                with sp.Fori(0, T // 2, 1) as i:
                    step(2 * i, i, 0)
                    step(2 * i + 1, i, 1)
                step(T - 1, T // 2, 0)

            @block.vector
            def _(dve):
                dve.wait_ge(s_row, 16)
                dve.sem_inc(s_used, 2)

                def step(t, i, u):
                    dve.wait_ge(s_in[u], (i + 1) * 16)
                    dve.sem_inc(g.waited, 1)
                    for h in range(H):
                        last = nc.vector.tensor_tensor_reduce(out=junk[:, h, :], in0=gone[u][:, :], in1=srow[:, h, :], scale=1.0,
                                                              scalar=-3e38, op0=ALU.add, op1=ALU.max,
                                                              accum_out=top4[:, u, h:h + 1])
                    last.then_inc(s_x, 1)
                    dve.wait_ge(s_x, t + 1)
                    nc.vector.tensor_copy(best[:, bass.ds(t, 1), :].rearrange("p a h -> p (a h)"), top4[:, u, :]).then_inc(s_used, 1)
                with dve.Fori(0, T // 2, 1) as i:
                    step(2 * i, i, 0)
                    step(2 * i + 1, i, 1)
                step(T - 1, T // 2, 0)
                v = Tick(s_v, dve)
                dve.wait_ge(s_used, T + 2)
                if by_target:
                    v(nc.vector.tensor_scalar(top_m[:, :, :], best[:, :, :], 0.5 * NEG, -NEG, ALU.is_lt, ALU.mult))
                    v(nc.vector.tensor_tensor(best[:, :, :], best[:, :, :], top_m[:, :, :], ALU.add))
                v(nc.vector.tensor_tensor(best[:, :, :], best[:, :, :], scores[:, :, H:2 * H], ALU.add))
                v(nc.vector.scalar_tensor_tensor(top_m[:, :, :], best[:, :, :], 0.2, best[:, :, :], ALU.mult, ALU.max))
        score_rows(nc, f"{name}t", g, H, top_m, m_dram)
        with Phase(nc, f"{name}x") as ph:
            t1 = ph.sb("t1", [P, H, NP])
            t2 = ph.sb("t2", [P, H, NP])
            s08 = ph.sb("s08", [P, T, H])
            s02 = ph.sb("s02", [P, T, H])
            allm = ph.sb("allm", [P, 1])
            adj = [ph.sb(f"adj{u}", [P, J]) for u in range(2)]
            feat = [ph.sb(f"feat{u}", [P, H * 65]) for u in range(2)]
            z = [ph.sb(f"z{u}", [P, H, J]) for u in range(2)]
            e = [ph.sb(f"e{u}", [P, H, J]) for u in range(2)]
            w = [ph.sb(f"w{u}", [P, H, J]) for u in range(2)]
            agg = ph.sb("agg", [65, H, J])
            acc = [ph.ps(f"acc{h}", [65, J]) for h in range(H)]
            s_row, s_v, s_ready = ph.sems("row", "v", "ready")
            s_in = ph.sems("in0", "in1")
            s_z, s_e, s_w, s_used, s_out = ph.sems("z", "e", "w", "used", "out")
            (s_st,) = ph.pool_sems(g, 1)
            block = ph.block()

            def turns(eng, step, begin, end):
                with eng.Fori(0, NJ, 1) as j:
                    begin(j)
                    with eng.Fori(0, T // 2, 1) as i:
                        step(j, 2 * i, j * T + 2 * i, j * (T // 2 + 1) + i, 0)
                        step(j, 2 * i + 1, j * T + 2 * i + 1, j * (T // 2) + i, 1)
                    step(j, T - 1, j * T + (T - 1), j * (T // 2 + 1) + T // 2, 0)
                    end(j)

            nothing = lambda j: None

            @block.sync
            def _(sp):
                sp.dma_start(t1[:, :, :].rearrange("p h n -> p (h n)"),
                             row(rows_dram[H:2 * H, :].rearrange("h n -> (h n)"))).then_inc(s_row, 16)
                sp.dma_start(t2[:, :, :].rearrange("p h n -> p (h n)"),
                             row(m_dram.rearrange("h n -> (h n)"))).then_inc(s_row, 16)

                def begin(j):
                    need = sp.snap(j * T + 1)
                    sp.wait_ge(s_used, need)
                    sp.sem_inc(g.waited, 1)

                def step(j, s, q, n, u):
                    a = sp.snap(s * P)
                    c = sp.snap(j * J)
                    need = sp.snap(q)
                    sp.wait_ge(s_used, need)
                    sp.sem_inc(g.waited, 1)
                    sp.dma_start(adj[u][:, :], g.adj[bass.ds(a, P), bass.ds(c, J)]).then_inc(s_in[u], 16)
                    sp.dma_start(feat[u][:, :], pr_dram[bass.ds(a, P), 0:H * 65]).then_inc(s_in[u], 16)
                turns(sp, step, begin, nothing)

            @block.vector
            def _(dve):
                v = Tick(s_v, dve)
                dve.wait_ge(s_row, 32)
                if by_target:
                    v(nc.vector.tensor_tensor(t1[:, :, :], t1[:, :, :], t2[:, :, :], ALU.subtract))
                    v(nc.vector.tensor_scalar(t2[:, :, :], t2[:, :, :], -0.8, None, ALU.mult))
                    v(nc.vector.scalar_tensor_tensor(t2[:, :, :], t1[:, :, :], 0.2, t2[:, :, :], ALU.mult, ALU.add))
                    v(nc.vector.tensor_scalar(s02[:, :, :], scores[:, :, 0:H], 0.2, None, ALU.mult))
                else:
                    v(nc.vector.tensor_reduce(allm[:, :], t2[:, :, 0:N], AX.XY, ALU.max))
                    v(nc.vector.tensor_scalar(t2[:, :, :], t1[:, :, :], 0.2, None, ALU.mult))
                    v(nc.vector.tensor_scalar(s02[:, :, :], scores[:, :, 0:H], 0.2, allm[:, 0:1], ALU.mult, ALU.subtract))
                v(nc.vector.tensor_scalar(s08[:, :, :], scores[:, :, 0:H], 0.8, None, ALU.mult))
                dve.sem_inc(s_ready, 1)
                dve.sem_inc(s_w, 1)

                def scores_of(j, s, u):
                    c = dve.snap(j * J)
                    for h in range(H):
                        last = nc.vector.scalar_tensor_tensor(z[u][:, h, :], t1[:, h, bass.ds(c, J)],
                                                              s08[:, bass.ds(s, 1), h], t2[:, h, bass.ds(c, J)],
                                                              ALU.add, ALU.max)
                    last.then_inc(s_z, 1)

                def weights_of(q, n, u):
                    dve.wait_ge(s_in[u], (n + 1) * 32)
                    dve.wait_ge(s_used, q)
                    dve.wait_ge(s_e, q + 1)
                    nc.vector.scalar_tensor_tensor(w[u][:, :, :], e[u][:, :, :], 1.0,
                                                   adj[u][:, :].unsqueeze(1).to_broadcast([P, H, J]),
                                                   ALU.min, ALU.mult).then_inc(s_w, 1)

                with dve.Fori(0, NJ, 1) as j:
                    dve.wait_ge(s_used, j * T + 1)
                    scores_of(j, 0, 0)
                    with dve.Fori(0, T // 2, 1) as i:
                        scores_of(j, 2 * i + 1, 1)
                        weights_of(j * T + 2 * i, j * (T // 2 + 1) + i, 0)
                        scores_of(j, 2 * i + 2, 0)
                        weights_of(j * T + 2 * i + 1, j * (T // 2) + i, 1)
                    weights_of(j * T + (T - 1), j * (T // 2 + 1) + T // 2, 0)

            @block.scalar
            def _(act):
                act.wait_ge(s_ready, 1)

                def step(j, s, q, n, u):
                    act.wait_ge(s_z, q + 1)
                    act.wait_ge(s_w, q)
                    for h in range(H):
                        last = nc.scalar.activation(e[u][:, h, :], z[u][:, h, :], ACT.Exp, bias=s02[:, bass.ds(s, 1), h])
                    last.then_inc(s_e, 1)

                def end(j):
                    act.wait_ge(s_used, (j + 1) * T + 1)
                    act.wait_ge(s_st, j * 16)
                    for h in range(H):
                        last = nc.scalar.copy(agg[:, h, :], acc[h][:, :])
                    last.then_inc(s_out, 1)

                def begin(j):
                    act.wait_ge(s_w, j * T + 1)
                turns(act, step, begin, end)

            @block.tensor
            def _(pe):
                pe.sem_inc(s_used, 1)

                def begin(j):
                    pe.wait_ge(s_out, j)
                    for h in range(H):
                        nc.tensor.matmul(acc[h][:, :], g.zeros[:, 0:65], g.zeros[:, 0:J], start=True, stop=False)

                def step(j, s, q, n, u):
                    stop = isinstance(s, int)
                    pe.wait_ge(s_in[u], (n + 1) * 32)
                    pe.wait_ge(s_w, q + 2)
                    for h in range(H):
                        last = nc.tensor.matmul(acc[h][:, :], feat[u][:, h * 65:(h + 1) * 65], w[u][:, h, :], start=False, stop=stop)
                    last.then_inc(s_used, 1)
                turns(pe, step, begin, nothing)

            @block.gpsimd
            def _(pool):
                with pool.Fori(0, NJ, 1) as j:
                    pool.wait_ge(s_out, j + 1)
                    pool.dma_start(agg_dram[:, :, bass.ds(j * J, J)].rearrange("h c n -> c h n"), agg[:, :, :]).then_inc(s_st, 16)
                pool.wait_ge(s_st, NJ * 16)


def heads_to_nodes(nc, name, g, H, agg_dram, out, floor):
    with Phase(nc, name) as ph:
        part = [ph.sb(f"part{u}", [65, H, P]) for u in range(2)]
        den = ph.sb("den", [P, H])
        tp = [ph.ps(f"tp{u}", [P, BANK]) for u in range(2)]
        s_in = ph.sems("in0", "in1")
        s_t, s_o, s_v = ph.sems("t", "o", "v")
        block = ph.block()

        def turns(eng, step):
            with eng.Fori(0, T // 2, 1) as i:
                step(2 * i, i, 0)
                step(2 * i + 1, i, 1)
            step(T - 1, T // 2, 0)

        @block.sync
        def _(sp):
            def step(t, i, u):
                a = sp.snap(t * P) if not isinstance(t, int) else t * P
                need = sp.snap(t + 1) if not isinstance(t, int) else t + 1
                sp.wait_ge(s_t, need)
                sp.sem_inc(g.waited, 1)
                sp.dma_start(part[u][:, :, :], agg_dram[:, :, bass.ds(a, P)].rearrange("h c n -> c h n")).then_inc(s_in[u], 16)
            turns(sp, step)

        @block.tensor
        def _(pe):
            pe.sem_inc(s_t, 2)

            def step(t, i, u):
                pe.wait_ge(s_in[u], (i + 1) * 16)
                pe.wait_ge(s_o, t)
                for h in range(H):
                    last = nc.tensor.transpose(tp[u][:, h * 65:(h + 1) * 65], part[u][:, h, :], g.ident[0:65, 0:65])
                last.then_inc(s_t, 1)
            turns(pe, step)

        @block.vector
        def _(dve):
            def step(t, i, u):
                dve.wait_ge(s_t, t + 3)
                heads = tp[u][:, 0:H * 65].rearrange("p (h c) -> p h c", c=65)
                nc.vector.tensor_scalar(den[:, :].unsqueeze(2), heads[:, :, 64:65], floor[1], None, floor[0]).then_inc(s_v, 1)
                dve.wait_ge(s_v, 2 * t + 1)
                nc.vector.reciprocal(den[:, :], den[:, :]).then_inc(s_v, 1)
                dve.wait_ge(s_v, 2 * t + 2)
                nc.vector.tensor_tensor(out[:, bass.ds(t, 1), :].rearrange("p a (h c) -> p (a h) c", c=64), heads[:, :, 0:64],
                                        den[:, :].unsqueeze(2).to_broadcast([P, H, 64]), ALU.mult).then_inc(s_o, 1)
            turns(dve, step)


def score_weights(nc, name, g, W, turned, a_src, a_tgt, H, out):
    K = H * 64 // P
    with Phase(nc, name) as ph:
        diag = ph.sb("diag", [P, K, 2 * H])
        mm = ph.ps("mm", [P, 2 * 2 * H])
        s_z, s_in, s_m = ph.sems("z", "in", "m")
        block = ph.block()

        @block.vector
        def _(dve):
            nc.vector.memset(diag[:, :, :], 0.0).then_inc(s_z, 1)
            dve.wait_ge(s_m, 1)
            nc.vector.tensor_copy(out[:, :, H * 64:H * 66], mm[:, :].rearrange("p (k c) -> p k c", k=2))

        @block.sync
        def _(sp):
            sp.wait_ge(s_z, 1)
            for n, a in enumerate((a_src, a_tgt)):
                for h in range(H):
                    p = 64 * (h % 2)
                    with nc.allow_non_contiguous_dma(reason="64 numbers"):
                        sp.dma_start(diag[p:p + 64, h // 2, n * H + h:n * H + h + 1],
                                     a[h, :].rearrange("(c o) -> c o", o=1)).then_inc(s_in, 16)

        @block.tensor
        def _(pe):
            pe.wait_ge(s_in, 2 * H * 16)
            for k in range(2):
                for o in range(K):
                    last = nc.tensor.matmul(mm[:, k * 2 * H:(k + 1) * 2 * H], turned[:, o, k * P:(k + 1) * P], diag[:, o, :],
                                            start=o == 0, stop=o == K - 1)
            last.then_inc(s_m, 1)


def local_branch(nc, g, x_dram, gat_w, a_src, a_tgt, gat_b, gain, shift, hl_dram):
    H = 4
    pr_dram = nc.dram_tensor("local_rows", (NP, H * 65 + 2 * H), F32).ap()
    agg_dram = nc.dram_tensor("local_agg", (H, 65, NP), F32).ap()
    with Phase(nc, "loc") as top:
        scores = top.sb("scores", [P, T, 2 * H])
        with Phase(nc, "locw") as ph:
            weights = ph.sb("weights", [P, 2, H * 64 + 2 * H])
            raw = ph.sb("raw", [P, 2, D])
            turned_weights(nc, "locwt", g, [(gat_w, weights)])
            load_all(nc, "locwl", [(raw[:, :, :], gat_w.rearrange("(k p) i -> p k i", p=P))])
            score_weights(nc, "locws", g, None, raw, a_src, a_tgt, H, weights)
            project(nc, "locp", g, x_dram, weights, H * 66, lambda t: [(pr_dram[bass.ds(t * P, P), :], (0, H * 67))],
                    extra=scores, ones_at=H)
        attention(nc, "gat", g, H, pr_dram, scores, agg_dram, False)
        with Phase(nc, "loco") as ph:
            h = ph.sb("h", [P, T, D])
            x = ph.sb("x", [P, T, D])
            w = ph.sb("w", [P, T, D])
            rows = ph.sb("rows", [P, 3, D])
            norm = Norm(ph, "n", w)
            heads_to_nodes(nc, "loch", g, H, agg_dram, h, (ALU.add, 1e-16))
            s_in, s_v, s_a, s_e, s_o, s_st = ph.sems("in", "v", "a", "e", "o", "st")
            block = ph.block()

            @block.sync
            def _(sp):
                sp.dma_start(x[:, :, :], nodes(x_dram)).then_inc(s_in, 16)
                for k, a in enumerate((gat_b, gain, shift)):
                    sp.dma_start(rows[:, k, :], row(a)).then_inc(s_in, 16)
                sp.wait_ge(s_o, 1)
                sp.dma_start(nodes(hl_dram), h[:, :, :]).then_inc(s_st, 16)
                sp.wait_ge(s_st, 16)

            @block.vector
            def _(dve):
                v = Tick(s_v, dve)
                dve.wait_ge(s_in, 64)
                v(nc.vector.tensor_tensor(h[:, :, :], h[:, :, :], x[:, :, :], ALU.add))
                v(nc.vector.tensor_tensor(h[:, :, :], h[:, :, :], rows[:, 0, :].unsqueeze(1).to_broadcast([P, T, D]), ALU.add))
                nc.vector.tensor_scalar(w[:, :, :], h[:, :, :], 0.0, None, ALU.min).then_inc(s_a, 1)
                dve.wait_ge(s_e, 1)
                v(nc.vector.tensor_scalar(h[:, :, :], h[:, :, :], 0.0, -1.0, ALU.max, ALU.add))
                v(nc.vector.tensor_tensor(h[:, :, :], h[:, :, :], w[:, :, :], ALU.add))
                norm.dve(nc, dve, v, h, rows[:, 1, :], rows[:, 2, :])
                dve.sem_inc(s_o, 1)

            @block.scalar
            def _(act):
                act.wait_ge(s_a, 1)
                nc.scalar.activation(w[:, :, :], w[:, :, :], ACT.Exp).then_inc(s_e, 1)
                norm.act(nc, act)


def load_all(nc, name, jobs):
    with Phase(nc, name) as ph:
        s_in = ph.sem("in")
        block = ph.block()

        @block.sync
        def _(sp):
            for to, a in jobs:
                with nc.allow_non_contiguous_dma(reason="small parameters"):
                    sp.dma_start(to, a).then_inc(s_in, 16)
            sp.wait_ge(s_in, 16 * len(jobs))


def features_first(nc, name, g, x_dram, out):
    with Phase(nc, name) as ph:
        tile = [ph.sb(f"tile{u}", [P, D]) for u in range(2)]
        tp = [ph.ps(f"tp{u}", [P, D]) for u in range(2)]
        s_in = ph.sems("in0", "in1")
        s_t, s_c = ph.sems("t", "c")
        block = ph.block()

        def turns(eng, step):
            with eng.Fori(0, T // 2, 1) as i:
                step(2 * i, i, 0)
                step(2 * i + 1, i, 1)
            step(T - 1, T // 2, 0)

        @block.sync
        def _(sp):
            def step(t, i, u):
                a = sp.snap(t * P) if not isinstance(t, int) else t * P
                need = sp.snap(t + 1) if not isinstance(t, int) else t + 1
                sp.wait_ge(s_t, need)
                sp.sem_inc(g.waited, 1)
                sp.dma_start(tile[u][:, :], x_dram[bass.ds(a, P), :]).then_inc(s_in[u], 16)
            turns(sp, step)

        @block.tensor
        def _(pe):
            pe.sem_inc(s_t, 2)
            pe.sem_inc(s_c, 1)

            def step(t, i, u):
                pe.wait_ge(s_in[u], (i + 1) * 16)
                pe.wait_ge(s_c, t)
                for k in range(2):
                    last = nc.tensor.transpose(tp[u][:, k * P:(k + 1) * P], tile[u][:, k * P:(k + 1) * P], g.ident[:, :])
                last.then_inc(s_t, 1)
            turns(pe, step)

        @block.scalar
        def _(act):
            def step(t, i, u):
                act.wait_ge(s_t, t + 3)
                nc.scalar.copy(out[:, :, bass.ds(t * P, P)], tp[u][:, :].rearrange("p (k n) -> p k n", k=2)).then_inc(s_c, 1)
            turns(act, step)


def moved_rows(nc, name, g, table, buf, scatter):
    with Phase(nc, name) as ph:
        (s_m,) = ph.pool_sems(g, 1)
        block = ph.block()

        @block.gpsimd
        def _(pool):
            for t in range(T):
                at = bass.IndirectOffsetOnAxis(ap=g.rank[:, t:t + 1], axis=0)
                if scatter:
                    pool.indirect_dma_start(table, at, buf[:, t, :], None).then_inc(s_m, 16)
                else:
                    pool.indirect_dma_start(buf[:, t, :], None, table, at).then_inc(s_m, 16)
            pool.wait_ge(s_m, 16 * T)


def banked_products(nc, ph, name, block, jobs, evict):
    mm = [ph.ps(f"{name}_mm{k}", [P, BANK]) for k in range(4)]
    s_mm, s_ev = ph.sems(f"{name}_mm", f"{name}_ev")
    todo = [(n, a, b) for n in range(len(jobs)) for a, b in BANKS]

    @block.tensor
    def _(pe):
        for q, (n, a, b) in enumerate(todo):
            if q >= 4:
                pe.wait_ge(s_ev, q - 3)
            rows, terms = jobs[n]
            for k, (w, x) in enumerate(terms):
                last = nc.tensor.matmul(mm[q % 4][0:rows, 0:b - a], w, x[:, a:b], start=k == 0, stop=k == len(terms) - 1)
            last.then_inc(s_mm, 1)

    @block.scalar
    def _(act):
        for q, (n, a, b) in enumerate(todo):
            act.wait_ge(s_mm, q + 1)
            evict(n, a, b, mm[q % 4][0:jobs[n][0], 0:b - a]).then_inc(s_ev, 1)


def mamba(nc, g, x_dram, in_w, conv_w, conv_b, x_w, dt_w, dt_b, A_log, D_par, out_w, ym_dram):
    S, R, K = 16, 16, 4
    xs_dram = nc.dram_tensor("sorted_x", (NP, D), F32).ap()
    dbc_dram = nc.dram_tensor("dbc", (R + 2 * S, NP), F32).ap()
    xc_dram = nc.dram_tensor("conv_x", (2, P, NP), F32).ap()
    z_dram = nc.dram_tensor("silu_z", (2, P, NP), F32).ap()
    with Phase(nc, "mamx") as ph:
        buf = ph.sb("buf", [P, T, D])
        load_all(nc, "mamxl", [(buf[:, :, :], nodes(x_dram))])
        moved_rows(nc, "mamxs", g, xs_dram, buf, True)
    with Phase(nc, "mam") as top:
        inT = top.sb("inT", [P, 2, 2 * D])
        xT = top.sb("xT", [P, 2, R + 2 * S])
        dtT = top.sb("dtT", [P, 1, D])
        outT = top.sb("outT", [P, 2, D])
        cw = top.sb("cw", [P, 2, K])
        cols = top.sb("cols", [P, 3, 2])
        A = top.sb("A", [P, 2, S])
        one = top.sb("one", [P, 1])
        turned_weights(nc, "mamwt", g, [(in_w, inT), (x_w, xT), (dt_w, dtT), (out_w, outT)])
        by_part = lambda a: a.rearrange("(k p) -> p k", p=P)
        load_all(nc, "mamwl", [(cw[:, :, :], conv_w.rearrange("(k p) c -> p k c", p=P)), (cols[:, 0, :], by_part(conv_b)),
                               (cols[:, 1, :], by_part(dt_b)), (cols[:, 2, :], by_part(D_par)),
                               (A[:, :, :], A_log.rearrange("(k p) s -> p k s", p=P))])
        dt = top.sb("dt", [P, 2, NP])
        u = top.sb("u", [P, 2, NP])
        with Phase(nc, "mama") as ph:
            xsT = ph.sb("xsT", [P, 2, NP])
            raw = ph.sb("raw", [P, 2, K - 1 + NP])
            features_first(nc, "mamaf", g, xs_dram, xsT)
            with Phase(nc, "mamap") as pp:
                s_z, s_st, s_v, s_e = pp.sems("z", "st", "v", "e")
                block = pp.block()

                def evict(n, a, b, psum):
                    if n < 2:
                        return nc.scalar.copy(raw[:, n, K - 1 + a:K - 1 + b], psum)
                    return nc.scalar.activation(u[:, n - 2, a:b], psum, ACT.Silu)
                banked_products(nc, pp, "mamap", block,
                                [(P, [(inT[:, k, n * P:(n + 1) * P], xsT[:, k, :]) for k in range(2)]) for n in range(4)], evict)

                @block.vector
                def _(dve):
                    nc.vector.memset(raw[:, :, 0:K - 1], 0.0)
            with Phase(nc, "mamac") as pp:
                s_st, s_v, s_c = pp.sems("st", "v", "c")
                block = pp.block()

                @block.vector
                def _(dve):
                    v = Tick(s_v, dve)
                    for k in range(2):
                        v(nc.vector.tensor_scalar(xsT[:, k, :], raw[:, k, 0:NP], cw[:, k, 0:1], None, ALU.mult))
                        for c in range(1, K):
                            ins = nc.vector.scalar_tensor_tensor(xsT[:, k, :], raw[:, k, c:c + NP], cw[:, k, c:c + 1],
                                                                 xsT[:, k, :], ALU.mult, ALU.add)
                            v(ins)
                        dve.sem_inc(s_c, 1)

                @block.scalar
                def _(act):
                    for k in range(2):
                        act.wait_ge(s_c, k + 1)
                        nc.scalar.activation(xsT[:, k, :], xsT[:, k, :], ACT.Silu, bias=cols[:, 0, k:k + 1])

                @block.sync
                def _(sp):
                    sp.dma_start(z_dram.rearrange("k p n -> p k n"), u[:, :, :]).then_inc(s_st, 16)
                    sp.wait_ge(s_st, 16)
            with Phase(nc, "mamad") as pp:
                dbc = pp.sb("dbc", [R + 2 * S, NP])
                s_st = pp.sem("st")
                with Phase(nc, "mamae") as pq:
                    s_st = pq.sem("st")
                    block = pq.block()
                    banked_products(nc, pq, "mamae", block,
                                    [(R + 2 * S, [(xT[:, k, :], xsT[:, k, :]) for k in range(2)])],
                                    lambda n, a, b, psum: nc.scalar.copy(dbc[:, a:b], psum))

                    @block.sync
                    def _(sp):
                        sp.dma_start(xc_dram.rearrange("k p n -> p k n"), xsT[:, :, :]).then_inc(s_st, 16)
                        sp.wait_ge(s_st, 16)
                with Phase(nc, "mamag") as pq:
                    s_st = pq.sem("st")
                    block = pq.block()
                    banked_products(nc, pq, "mamag", block,
                                    [(P, [(dtT[0:R, 0, n * P:(n + 1) * P], dbc[0:R, :])]) for n in range(2)],
                                    lambda n, a, b, psum: nc.scalar.activation(dt[:, n, a:b], psum, ACT.Identity, bias=cols[:, 1, n:n + 1]))

                    @block.sync
                    def _(sp):
                        sp.dma_start(dbc_dram, dbc[:, :]).then_inc(s_st, 16)
                        sp.wait_ge(s_st, 16)
            with Phase(nc, "mamas") as pp:
                s_v, s_a, s_b = pp.sems("v", "a", "b")
                block = pp.block()

                @block.scalar
                def _(act):
                    a = Tick(s_a, act)
                    a(nc.scalar.activation(u[:, :, :], dt[:, :, :], ACT.Abs))
                    a(nc.scalar.activation(u[:, :, :], u[:, :, :], ACT.Exp, scale=-1.0))
                    act.wait_ge(s_v, 1)
                    a(nc.scalar.activation(u[:, :, :], u[:, :, :], ACT.Ln, bias=one[:, 0:1]))
                    nc.scalar.activation(A[:, :, :], A[:, :, :], ACT.Exp).then_inc(s_a, 1)

                @block.vector
                def _(dve):
                    v = Tick(s_v, dve)
                    v(nc.vector.memset(one[:, :], 1.0))
                    dve.wait_ge(s_a, 4)
                    v(nc.vector.scalar_tensor_tensor(dt[:, :, :], dt[:, :, :], 0.0, u[:, :, :], ALU.max, ALU.add))
                    v(nc.vector.tensor_tensor(u[:, :, :], dt[:, :, :], xsT[:, :, :], ALU.mult))
                    v(nc.vector.tensor_scalar(A[:, :, :], A[:, :, :], -1.0, None, ALU.mult))
        with Phase(nc, "mamb") as mid:
            yT = mid.sb("yT", [P, 2, NP])
            for ct in range(2):
                with Phase(nc, f"mamb{ct}") as ph:
                    ident = g.ident
                    rowb = ph.sb("rowb", [1, 2, NP])
                    bc = [ph.sb(f"bc{k}", [P, NP]) for k in range(2)]
                    dA = ph.sb("dA", [P, NP])
                    st = ph.sb("st", [P, NP])
                    hs = ph.sb("hs", [P, NP])
                    hc = ph.sb("hc", [P, NP])
                    acc = ph.ps("acc", [P, NP])
                    s_B, s_C, s_bb, s_bC, s_dA, s_x, s_h, s_hc, s_y = ph.sems("B", "C", "bb", "bC", "dA", "x", "h", "hc", "y")
                    block = ph.block()

                    @block.sync
                    def _(sp):
                        with sp.Fori(0, S, 1) as s:
                            a = sp.snap(s + R)
                            c = sp.snap(s + (R + S))
                            need = sp.snap(s)
                            sp.wait_ge(s_bb, need)
                            sp.sem_inc(g.waited, 1)
                            sp.dma_start(rowb[0:1, 0, :], dbc_dram[bass.ds(a, 1), :]).then_inc(s_B, 16)
                            sp.wait_ge(s_bC, need)
                            sp.sem_inc(g.waited, 1)
                            sp.dma_start(rowb[0:1, 1, :], dbc_dram[bass.ds(c, 1), :]).then_inc(s_C, 16)

                    @block.gpsimd
                    def _(pool):
                        with pool.Fori(0, S, 1) as s:
                            pool.wait_ge(s_B, (s + 1) * 16)
                            pool.wait_ge(s_x, s)
                            pool.sem_inc(g.waited, 1)
                            nc.gpsimd.partition_broadcast(bc[0][:, :], rowb[0:1, 0, :]).then_inc(s_bb, 1)
                            pool.wait_ge(s_C, (s + 1) * 16)
                            pool.wait_ge(s_hc, s)
                            pool.sem_inc(g.waited, 1)
                            nc.gpsimd.partition_broadcast(bc[1][:, :], rowb[0:1, 1, :]).then_inc(s_bC, 1)

                    @block.scalar
                    def _(act):
                        with act.Fori(0, S, 1) as s:
                            act.wait_ge(s_h, s)
                            nc.scalar.activation(dA[:, :], dt[:, ct, :], ACT.Exp, scale=A[:, ct, bass.ds(s, 1)]).then_inc(s_dA, 1)
                        act.wait_ge(s_y, S)
                        for a, b in BANKS:
                            nc.scalar.copy(yT[:, ct, a:b], acc[:, a:b])

                    @block.vector
                    def _(dve):
                        with dve.Fori(0, S, 1) as s:
                            dve.wait_ge(s_bb, s + 1)
                            nc.vector.tensor_tensor(st[:, :], u[:, ct, :], bc[0][:, :], ALU.mult).then_inc(s_x, 1)
                            dve.wait_ge(s_x, s + 1)
                            dve.wait_ge(s_dA, s + 1)
                            nc.vector.tensor_tensor_scan(hs[:, :], dA[:, :], st[:, :], 0.0, ALU.mult, ALU.add).then_inc(s_h, 1)
                            dve.wait_ge(s_h, s + 1)
                            dve.wait_ge(s_bC, s + 1)
                            dve.wait_ge(s_y, s)
                            nc.vector.tensor_tensor(hc[:, :], hs[:, :], bc[1][:, :], ALU.mult).then_inc(s_hc, 1)

                    @block.tensor
                    def _(pe):
                        for a, b in BANKS:
                            nc.tensor.matmul(acc[:, a:b], g.zeros[:, 0:P], g.zeros[:, 0:b - a], start=True, stop=False)
                        with pe.Fori(0, S - 1, 1) as s:
                            pe.wait_ge(s_hc, s + 1)
                            for a, b in BANKS:
                                last = nc.tensor.matmul(acc[:, a:b], ident[:, :], hc[:, a:b], start=False, stop=False)
                            last.then_inc(s_y, 1)
                        pe.wait_ge(s_hc, S)
                        for a, b in BANKS:
                            last = nc.tensor.matmul(acc[:, a:b], ident[:, :], hc[:, a:b], start=False, stop=True)
                        last.then_inc(s_y, 1)
            with Phase(nc, "mamo") as ph:
                xc = ph.sb("xc", [P, 2, NP])
                z = u
                out = dt
                outv = out[:, :, :].rearrange("p k n -> p (k n)").rearrange("p (t d) -> p t d", d=D)
                mm = [ph.ps(f"mm{k}", [P, BANK]) for k in range(2)]
                s_in, s_v, s_r, s_m, s_e, s_st = ph.sems("in", "v", "r", "m", "e", "st")
                pairs = [range(a, min(a + 2, T)) for a in range(0, T, 2)]
                block = ph.block()

                @block.sync
                def _(sp):
                    sp.dma_start(xc[:, :, :], xc_dram.rearrange("k p n -> p k n")).then_inc(s_in, 16)
                    sp.dma_start(z[:, :, :], z_dram.rearrange("k p n -> p k n")).then_inc(s_in, 16)
                    sp.wait_ge(s_e, len(pairs))
                    sp.dma_start(nodes(ym_dram), outv).then_inc(s_st, 16)
                    sp.wait_ge(s_st, 16)

                @block.vector
                def _(dve):
                    v = Tick(s_v, dve)
                    dve.wait_ge(s_in, 32)
                    for k in range(2):
                        v(nc.vector.scalar_tensor_tensor(yT[:, k, :], xc[:, k, :], cols[:, 2, k:k + 1], yT[:, k, :], ALU.mult, ALU.add))
                        v(nc.vector.tensor_tensor(yT[:, k, :], yT[:, k, :], z[:, k, :], ALU.mult))
                    dve.sem_inc(s_r, 1)

                @block.tensor
                def _(pe):
                    pe.wait_ge(s_r, 1)
                    for q, pr in enumerate(pairs):
                        if q > 1:
                            pe.wait_ge(s_e, q - 1)
                        for n, t in enumerate(pr):
                            for k in range(2):
                                last = nc.tensor.matmul(mm[q % 2][:, n * D:(n + 1) * D], yT[:, k, t * P:(t + 1) * P], outT[:, k, :],
                                                        start=k == 0, stop=k == 1)
                        last.then_inc(s_m, 1)

                @block.scalar
                def _(act):
                    for q, pr in enumerate(pairs):
                        act.wait_ge(s_m, q + 1)
                        nc.scalar.copy(outv[:, pr[0]:pr[-1] + 1, :].rearrange("p t d -> p (t d)"), mm[q % 2][:, 0:len(pr) * D]).then_inc(s_e, 1)


def mixed_branches(nc, g, x_dram, hl_dram, ym_dram, gg, gb, wl, wg, f1w, f1b, f2w, f2b, ng, nb, x_out):
    ha_dram = nc.dram_tensor("h_attn", (NP, D), F32).ap()
    s_dram = nc.dram_tensor("h_and_ff", (NP, D), F32).ap()
    with Phase(nc, "mixa") as ph:
        y = ph.sb("y", [P, T, D])
        x = ph.sb("x", [P, T, D])
        rows = ph.sb("rows", [P, 2, D])
        moved_rows(nc, "mixag", g, ym_dram, y, False)
        norm = Norm(ph, "n", x)
        s_in, s_v, s_o, s_st = ph.sems("in", "v", "o", "st")
        block = ph.block()

        @block.sync
        def _(sp):
            sp.dma_start(x[:, :, :], nodes(x_dram)).then_inc(s_in, 16)
            for k, a in enumerate((gg, gb)):
                sp.dma_start(rows[:, k, :], row(a)).then_inc(s_in, 16)
            sp.wait_ge(s_o, 1)
            sp.dma_start(nodes(ha_dram), y[:, :, :]).then_inc(s_st, 16)
            sp.wait_ge(s_st, 16)

        @block.vector
        def _(dve):
            v = Tick(s_v, dve)
            dve.wait_ge(s_in, 48)
            v(nc.vector.tensor_tensor(y[:, :, :], y[:, :, :], x[:, :, :], ALU.add))
            norm.dve(nc, dve, v, y, rows[:, 0, :], rows[:, 1, :])
            dve.sem_inc(s_o, 1)

        @block.scalar
        def _(act):
            norm.act(nc, act)
    with Phase(nc, "mixb") as top:
        lT = top.sb("lT", [P, 2, D])
        gT = top.sb("gT", [P, 2, D])
        f1T = top.sb("f1T", [P, 2, 2 * D])
        f2T = top.sb("f2T", [P, 4, D])
        f1c = top.sb("f1c", [P, 4])
        f2r = top.sb("f2r", [P, D])
        turned_weights(nc, "mixbt", g, [(wl, lT), (wg, gT), (f1w, f1T), (f2w, f2T)])
        load_all(nc, "mixbl", [(f1c[:, :], f1b.rearrange("(c p) -> p c", p=P)), (f2r[:, :], row(f2b))])
        with Phase(nc, "mixc") as ph:
            both = [ph.sb(f"both{u}", [P, 2, D]) for u in range(2)]
            bothT = ph.sb("bothT", [P, 4, P])
            gate = ph.sb("gate", [P, D])
            dif = ph.sb("dif", [P, D])
            h = ph.sb("h", [P, D])
            hT = ph.sb("hT", [P, 2, P])
            hid = ph.sb("hid", [P, 4, P])
            res = [ph.sb(f"res{u}", [P, D]) for u in range(2)]
            tp = ph.ps("tp", [P, BANK])
            ga = ph.ps("ga", [P, D])
            tq = ph.ps("tq", [P, D])
            mh = ph.ps("mh", [P, BANK])
            mo = ph.ps("mo", [P, D])
            s_in = ph.sems("in0", "in1")
            s_st = ph.pool_sems(g, 2)
            s_t, s_tc, s_g, s_gs, s_h, s_q, s_qc, s_m, s_mr, s_o, s_r, s_v = ph.sems(
                "t", "tc", "g", "gs", "h", "q", "qc", "m", "mr", "o", "r", "v")
            block = ph.block()

            def turns(eng, step):
                with eng.Fori(0, T // 2, 1) as i:
                    step(2 * i, i, 0)
                    step(2 * i + 1, i, 1)
                step(T - 1, T // 2, 0)

            @block.sync
            def _(sp):
                def step(t, i, u):
                    a = sp.snap(t * P) if not isinstance(t, int) else t * P
                    need = sp.snap(t + 1) if not isinstance(t, int) else t + 1
                    sp.wait_ge(s_r, need)
                    sp.sem_inc(g.waited, 1)
                    sp.dma_start(both[u][:, 0, :], hl_dram[bass.ds(a, P), :]).then_inc(s_in[u], 16)
                    sp.dma_start(both[u][:, 1, :], ha_dram[bass.ds(a, P), :]).then_inc(s_in[u], 16)
                turns(sp, step)

            @block.tensor
            def _(pe):
                def step(t, i, u):
                    pe.wait_ge(s_in[u], (i + 1) * 32)
                    for c in range(4):
                        last = nc.tensor.transpose(tp[:, c * P:(c + 1) * P], both[u][:, c // 2, (c % 2) * P:(c % 2 + 1) * P], g.ident[:, :])
                    last.then_inc(s_t, 1)
                    pe.wait_ge(s_tc, t + 1)
                    for c in range(4):
                        last = nc.tensor.matmul(ga[:, :], bothT[:, c, :], (lT if c < 2 else gT)[:, c % 2, :], start=c == 0, stop=c == 3)
                    last.then_inc(s_g, 1)
                    pe.wait_ge(s_h, t + 1)
                    for k in range(2):
                        last = nc.tensor.transpose(tq[:, k * P:(k + 1) * P], h[:, k * P:(k + 1) * P], g.ident[:, :])
                    last.then_inc(s_q, 1)
                    pe.wait_ge(s_qc, t + 1)
                    for c in range(4):
                        for k in range(2):
                            last = nc.tensor.matmul(mh[:, c * P:(c + 1) * P], f1T[:, k, c * P:(c + 1) * P], hT[:, k, :], start=k == 0, stop=k == 1)
                    last.then_inc(s_m, 1)
                    pe.wait_ge(s_mr, t + 1)
                    for c in range(4):
                        last = nc.tensor.matmul(mo[:, :], hid[:, c, :], f2T[:, c, :], start=c == 0, stop=c == 3)
                    last.then_inc(s_o, 1)
                turns(pe, step)

            @block.scalar
            def _(act):
                def step(t, i, u):
                    act.wait_ge(s_t, t + 1)
                    nc.scalar.copy(bothT[:, :, :].rearrange("p c n -> p (c n)"), tp[:, :]).then_inc(s_tc, 1)
                    act.wait_ge(s_g, t + 1)
                    act.wait_ge(s_h, t)
                    nc.scalar.activation(gate[:, :], ga[:, :], ACT.Sigmoid).then_inc(s_gs, 1)
                    act.wait_ge(s_q, t + 1)
                    nc.scalar.copy(hT[:, :, :].rearrange("p c n -> p (c n)"), tq[:, :]).then_inc(s_qc, 1)
                    act.wait_ge(s_m, t + 1)
                    for c in range(4):
                        last = nc.scalar.activation(hid[:, c, :], mh[:, c * P:(c + 1) * P], ACT.Relu, bias=f1c[:, c:c + 1])
                    last.then_inc(s_mr, 1)
                turns(act, step)

            @block.vector
            def _(dve):
                v = Tick(s_v, dve)
                dve.sem_inc(s_r, 2)

                def step(t, i, u):
                    dve.wait_ge(s_in[u], (i + 1) * 32)
                    dve.wait_ge(s_qc, t)
                    v(nc.vector.tensor_tensor(dif[:, :], both[u][:, 0, :], both[u][:, 1, :], ALU.subtract))
                    dve.wait_ge(s_gs, t + 1)
                    v(nc.vector.tensor_tensor(dif[:, :], dif[:, :], gate[:, :], ALU.mult))
                    nc.vector.tensor_tensor(h[:, :], dif[:, :], both[u][:, 1, :], ALU.add).then_inc(s_h, 1)
                    dve.wait_ge(s_h, t + 1)
                    dve.wait_ge(s_st[u], i * 16)
                    v(nc.vector.tensor_tensor(res[u][:, :], h[:, :], f2r[:, :], ALU.add))
                    dve.wait_ge(s_o, t + 1)
                    nc.vector.tensor_tensor(res[u][:, :], res[u][:, :], mo[:, :], ALU.add).then_inc(s_r, 1)
                with dve.Fori(0, T // 2, 1) as i:
                    v.loop(i, 6)
                    step(2 * i, i, 0)
                    step(2 * i + 1, i, 1)
                v.end(T // 2)
                step(T - 1, T // 2, 0)

            @block.gpsimd
            def _(pool):
                def step(t, i, u):
                    pool.wait_ge(s_r, t + 3)
                    pool.dma_start(s_dram[bass.ds(t * P, P), :], res[u][:, :]).then_inc(s_st[u], 16)
                turns(pool, step)
                pool.wait_ge(s_st[0], (T - T // 2) * 16)
                pool.wait_ge(s_st[1], (T // 2) * 16)
    residual_norm(nc, "mixn", x_dram, s_dram, x_out, ng, nb)


def residual_norm(nc, name, x_dram, h_dram, x_out, gain=None, shift=None):
    with Phase(nc, name) as ph:
        h = ph.sb("h", [P, T, D])
        x = ph.sb("x", [P, T, D])
        w = ph.sb("w", [P, T, D])
        rows = ph.sb("rows", [P, 2, D])
        inner = Norm(ph, "a", w)
        outer = Norm(ph, "b", w)
        s_in, s_v, s_o, s_st = ph.sems("in", "v", "o", "st")
        block = ph.block()
        jobs = [(x[:, :, :], nodes(x_dram)), (h[:, :, :], nodes(h_dram))]
        if gain is not None:
            jobs += [(rows[:, 0, :], row(gain)), (rows[:, 1, :], row(shift))]
        if x_out.shape[0] == NP:
            parts = [(nodes(x_out), x[:, :, :])]
        else:
            whole = N // P
            parts = [(nodes(x_out[0:whole * P, :]), x[:, 0:whole, :]), (x_out[whole * P:N, :], x[0:N - whole * P, whole, :])]

        @block.sync
        def _(sp):
            for to, a in jobs:
                sp.dma_start(to, a).then_inc(s_in, 16)
            sp.wait_ge(s_o, 1)
            for to, a in parts:
                sp.dma_start(to, a).then_inc(s_st, 16)
            sp.wait_ge(s_st, 16 * len(parts))

        @block.vector
        def _(dve):
            v = Tick(s_v, dve)
            dve.wait_ge(s_in, 16 * len(jobs))
            if gain is not None:
                inner.dve(nc, dve, v, h, rows[:, 0, :], rows[:, 1, :])
            v(nc.vector.tensor_tensor(x[:, :, :], x[:, :, :], h[:, :, :], ALU.add))
            outer.dve(nc, dve, v, x)
            dve.sem_inc(s_o, 1)

        @block.scalar
        def _(act):
            if gain is not None:
                inner.act(nc, act)
            outer.act(nc, act)


def relational_stack(nc, g, x_dram, weights, roots, biases, x_out):
    L = 3
    table = nc.dram_tensor("rel_table", (REL * NP, D), F32).ap()
    own = nc.dram_tensor("rel_own", (NP, D), F32).ap()
    hs = [nc.dram_tensor(f"rel_h{n}", (NP, D), F32).ap() for n in range(L)]
    for n in range(L):
        with Phase(nc, f"rel{n}w") as ph:
            w = ph.sb("w", [P, 2, (REL + 1) * D])
            load_all(nc, f"rel{n}l",
                     [(w[:, :, r * D:(r + 1) * D], weights[n, r].rearrange("(k p) e -> p k e", p=P)) for r in range(REL)] +
                     [(w[:, :, REL * D:], roots[n].rearrange("(k p) e -> p k e", p=P))])
            project(nc, f"rel{n}p", g, hs[n - 1] if n else x_dram, w, (REL + 1) * D,
                    lambda t: [(table[bass.ds(t * P + r * NP, P), :], (r * D, (r + 1) * D)) for r in range(REL)] +
                    [(own[bass.ds(t * P, P), :], (REL * D, (REL + 1) * D))])
        gather_sum(nc, f"rel{n}s", g, table, own, biases[n], ACT.Relu if n < L - 1 else ACT.Sigmoid, hs[n])
    residual_norm(nc, "reln", x_dram, hs[L - 1], x_out)


def gather_sum(nc, name, g, table, own, bias, func, out):
    with Phase(nc, name) as ph:
        rows = [ph.sb(f"rows{u}", [P, D]) for u in range(G)]
        at = [ph.sb(f"at{u}", [P, 1], I32) for u in range(G)]
        hot = [ph.sb(f"hot{u}", [P, P]) for u in range(G)]
        mine = ph.sb("mine", [P, D])
        bias_row = ph.sb("bias_row", [P, D])
        total = ph.sb("total", [P, D])
        res = ph.sb("res", [P, D])
        acc = ph.ps("acc", [P, D])
        s_in = ph.pool_sems(g, G)
        s_at, s_hot, s_used, s_sum, s_own, s_bias, s_v, s_tot, s_res, s_st = ph.sems(
            "at", "hot", "used", "sum", "own", "bias", "v", "tot", "res", "st")
        block = ph.block()

        @block.vector
        def _(dve):
            dve.wait_ge(s_bias, 16)
            with dve.Fori(0, T, 1) as t:
                first, count, before = span_of(dve, g, t)
                with dve.Fori(0, count, 1) as j:
                    c0 = group_start(nc, first + j)
                    for u in range(G):
                        dve.wait_ge(s_in[u], (before + j) * 16)
                        nc.vector.tensor_copy(at[u][:, :], g.rows[:, bass.ds(c0 + u, 1)]).then_inc(s_at, 1)
                    for u in range(G):
                        dve.wait_ge(s_used, (before + j) * G + (u + 1))
                        nc.vector.tensor_scalar(hot[u][:, :], g.numbers[:, bass.ds(t * P, P)],
                                                g.dsts[:, bass.ds(c0 + u, 1)], None, ALU.is_equal).then_inc(s_hot, 1)
                dve.wait_ge(s_own, (t + 1) * 16)
                dve.wait_ge(s_sum, t + 1)
                nc.vector.tensor_tensor(total[:, :], acc[:, :], mine[:, :], ALU.add).then_inc(s_v, 1)
                dve.wait_ge(s_v, t + 1)
                dve.wait_ge(s_res, t)
                nc.vector.tensor_tensor(total[:, :], total[:, :], bias_row[:, :], ALU.add).then_inc(s_tot, 1)
                dve.wait_ge(s_tot, t + 1)

        @block.gpsimd
        def _(pool):
            with pool.Fori(0, T, 1) as t:
                first, count, before = span_of(pool, g, t)
                with pool.Fori(0, count, 1) as j:
                    for u in range(G):
                        pool.wait_ge(s_at, (before + j) * G + (u + 1))
                        pool.wait_ge(s_used, (before + j) * G + (u + 1))
                        pool.sem_inc(g.waited, 1)
                        pool.indirect_dma_start(rows[u][:, :], None, table,
                                                bass.IndirectOffsetOnAxis(ap=at[u][:, 0:1], axis=0)).then_inc(s_in[u], 16)

        @block.tensor
        def _(pe):
            pe.sem_inc(s_used, G)
            with pe.Fori(0, T, 1) as t:
                first, count, before = span_of(pe, g, t)
                pe.wait_ge(s_v, t)
                nc.tensor.matmul(acc[:, :], g.zeros[:, 0:P], g.zeros[:, 0:D], start=True, stop=False)
                with pe.Fori(0, count, 1) as j:
                    for u in range(G):
                        pe.wait_ge(s_hot, (before + j) * G + (u + 1))
                        pe.wait_ge(s_in[u], (before + j) * 16 + 16)
                        nc.tensor.matmul(acc[:, :], hot[u][:, :], rows[u][:, :], start=False, stop=False).then_inc(s_used, 1)
                nc.tensor.matmul(acc[:, :], g.zeros[:, 0:P], g.zeros[:, 0:D], start=False, stop=True).then_inc(s_sum, 1)

        @block.scalar
        def _(act):
            with act.Fori(0, T, 1) as t:
                act.wait_ge(s_tot, t + 1)
                act.wait_ge(s_st, t * 16)
                nc.scalar.activation(res[:, :], total[:, :], func).then_inc(s_res, 1)

        @block.sync
        def _(sp):
            sp.dma_start(bias_row[:, :], row(bias)).then_inc(s_bias, 16)
            with sp.Fori(0, T, 1) as t:
                a, need, done = sp.snap(t * P), sp.snap(t), sp.snap(t + 1)
                sp.wait_ge(s_v, need)
                sp.sem_inc(g.waited, 1)
                sp.dma_start(mine[:, :], own[bass.ds(a, P), :]).then_inc(s_own, 16)
                sp.wait_ge(s_res, done)
                sp.sem_inc(g.waited, 1)
                sp.dma_start(out[bass.ds(a, P), :], res[:, :]).then_inc(s_st, 16)
            sp.wait_ge(s_st, 16 * T)


def last_attention(nc, g, x_dram, W, a_l, a_r, bias, lin_w, lin_b, out):
    H = 2
    F = H * 64
    pr_dram = nc.dram_tensor("last_rows", (NP, H * 65 + 2 * H), F32).ap()
    agg_dram = nc.dram_tensor("last_agg", (H, 65, NP), F32).ap()
    h_dram = nc.dram_tensor("last_h", (NP, D), F32).ap()
    with Phase(nc, "las") as top:
        scores = top.sb("scores", [P, T, 2 * H])
        with Phase(nc, "lasw") as ph:
            weights = ph.sb("weights", [P, 2, F + 2 * H])
            WT = ph.sb("WT", [P, 1, D])
            load_all(nc, "laswl", [(weights[:, :, 0:F], W.rearrange("(k p) n -> p k n", p=P))])
            turned_weights(nc, "laswt", g, [(W, WT)])
            score_weights(nc, "lasws", g, None, WT, a_l, a_r, H, weights)
            project(nc, "lasp", g, x_dram, weights, F + 2 * H, lambda t: [(pr_dram[bass.ds(t * P, P), :], (0, H * 67))],
                    extra=scores, ones_at=H)
        attention(nc, "lat", g, H, pr_dram, scores, agg_dram, True)
        with Phase(nc, "laso") as ph:
            h = ph.sb("h", [P, T, F])
            o = ph.sb("o", [P, T, D])
            lw = ph.sb("lw", [P, D])
            br = ph.sb("br", [P, F])
            lr = ph.sb("lr", [P, D])
            turned = [ph.sb(f"turned{u}", [P, 2 * P]) for u in range(2)]
            heads_to_nodes(nc, "lash", g, H, agg_dram, h, (ALU.max, 1e-30))
            tp = [ph.ps(f"tp{u}", [P, BANK]) for u in range(2)]
            mm = [ph.ps(f"mm{u}", [P, BANK]) for u in range(2)]
            s_in, s_v, s_a, s_t, s_c, s_m, s_r, s_o, s_st = ph.sems("in", "v", "a", "t", "c", "m", "r", "o", "st")
            pairs = [range(a, min(a + 2, T)) for a in range(0, T, 2)]
            block = ph.block()

            @block.sync
            def _(sp):
                for to, a in ((lw[:, :], lin_w), (br[:, :], row(bias)), (lr[:, :], row(lin_b))):
                    sp.dma_start(to, a).then_inc(s_in, 16)
                sp.wait_ge(s_o, 1)
                sp.dma_start(nodes(h_dram), o[:, :, :]).then_inc(s_st, 16)
                sp.wait_ge(s_st, 16)

            @block.tensor
            def _(pe):
                pe.wait_ge(s_a, 1)
                for k, pr in enumerate(pairs):
                    if k > 1:
                        pe.wait_ge(s_c, k - 1)
                    for n, t in enumerate(pr):
                        last = nc.tensor.transpose(tp[k % 2][:, n * P:(n + 1) * P], h[:, t, :], g.ident[:, :])
                    last.then_inc(s_t, 1)
                    pe.wait_ge(s_c, k + 1)
                    if k > 1:
                        pe.wait_ge(s_r, k - 1)
                    for n, t in enumerate(pr):
                        last = nc.tensor.matmul(mm[k % 2][:, n * D:(n + 1) * D], turned[k % 2][:, n * P:(n + 1) * P], lw[:, :],
                                                start=True, stop=True)
                    last.then_inc(s_m, 1)

            @block.scalar
            def _(act):
                for k, pr in enumerate(pairs):
                    act.wait_ge(s_t, k + 1)
                    nc.scalar.copy(turned[k % 2][:, 0:len(pr) * P], tp[k % 2][:, 0:len(pr) * P]).then_inc(s_c, 1)

            @block.vector
            def _(dve):
                v = Tick(s_v, dve)
                dve.wait_ge(s_in, 48)
                v(nc.vector.tensor_tensor(h[:, :, :], h[:, :, :], br[:, :].unsqueeze(1).to_broadcast([P, T, F]), ALU.add))
                nc.vector.tensor_scalar(h[:, :, :], h[:, :, :], 0.0, None, ALU.max).then_inc(s_a, 1)
                for k, pr in enumerate(pairs):
                    dve.wait_ge(s_m, k + 1)
                    nc.vector.tensor_tensor(o[:, pr[0]:pr[-1] + 1, :],
                                            mm[k % 2][:, 0:len(pr) * D].rearrange("p (t d) -> p t d", d=D),
                                            lr[:, :].unsqueeze(1).to_broadcast([P, len(pr), D]), ALU.add).then_inc(s_r, 1)
                dve.wait_ge(s_r, len(pairs))
                v(nc.vector.tensor_scalar(o[:, :, :], o[:, :, :], 0.0, None, ALU.max))
                dve.sem_inc(s_o, 1)
    residual_norm(nc, "lasn", x_dram, h_dram, out)


def program(nc, x, src, dst, kind, noise, gcn, local, ssm, mix, rel, last, out):
    ctx = ExitStack()
    with ctx:
        g = Shared()

        def sb(name, shape, dt=F32):
            return ctx.enter_context(nc.sbuf_tensor(f"g_{name}", shape, dt))

        def dram(name, shape, dt=F32):
            return nc.dram_tensor(name, shape, dt).ap()

        g.ident = sb("ident", [P, P])
        g.ones = sb("ones", [P, P])
        g.zeros = sb("zeros", [P, BANK], BF16)
        g.numbers = sb("numbers", [P, NP], F16)
        g.srcs = sb("srcs", [P, CT * P])
        g.dsts = sb("dsts", [P, CT * P])
        g.rows = sb("rows", [P, CT * P], I32)
        g.spans = sb("spans", [1, 3, 32], I32)
        g.indeg = sb("indeg", [P, T])
        g.dinv = sb("dinv", [P, T])
        g.rank = sb("rank", [P, T], I32)
        g.adj = dram("adj", (NP, NP))
        g.absent = dram("absent", (NP, NP), BF16)
        xs = [dram(f"x{n}", (NP, D)) for n in range(4)]
        hl, ym = dram("h_local", (NP, D)), dram("y_sorted", (NP, D))
        g.waited = ctx.enter_context(nc.semaphore("waited"))
        g.pool_sems = [ctx.enter_context(nc.semaphore(f"pool_dma{n}")) for n in range(30)]

        def stage(f, *args):
            f(nc, g, *args)
            free = nc.free_semaphores
            nc.all_engine_barrier(sems_to_clear=range(min(free), max(free) + 1))

        def graph(nc, g):
            constants(nc, g)
            edge_tables(nc, g, src, dst, kind)
            with Phase(nc, "deg") as ph:
                g.outdeg = ph.sb("outdeg", [P, NP])
                adjacency(nc, g)
                rank_nodes(nc, g, noise, g.outdeg)

        stage(graph)
        load_x(nc, g, x, xs[0])
        stage(gcn_stack, xs[0], *gcn, xs[1])
        stage(local_branch, xs[1], *local, hl)
        stage(mamba, xs[1], *ssm, ym)
        stage(mixed_branches, xs[1], hl, ym, *mix, xs[2])
        stage(relational_stack, xs[2], *rel, xs[3])
        last_attention(nc, g, xs[3], *last, out)

_FIRST = ['x', 'src', 'dst', 'edge_type_8', 'node_vec']
_GCN = ['L0_gnn_W1', 'L0_gnn_b1', 'L0_gnn_W2', 'L0_gnn_b2', 'L0_gnn_W3', 'L0_gnn_b3', 'L0_gnn_W4', 'L0_gnn_b4']
_LOCAL = ['L1_gnn_gat_w', 'L1_gnn_gat_a_src', 'L1_gnn_gat_a_tgt', 'L1_gnn_gat_b', 'L1_gnn_ln_local_g', 'L1_gnn_ln_local_b']
_SSM = ['L1_gnn_in_proj_w', 'L1_gnn_conv_w', 'L1_gnn_conv_b', 'L1_gnn_x_proj_w', 'L1_gnn_dt_proj_w', 'L1_gnn_dt_proj_b', 'L1_gnn_A_log', 'L1_gnn_D_param', 'L1_gnn_out_proj_w']
_MIX = ['L1_gnn_ln_global_g', 'L1_gnn_ln_global_b', 'L1_gnn_wl', 'L1_gnn_wg', 'L1_gnn_ff1_w', 'L1_gnn_ff1_b', 'L1_gnn_ff2_w', 'L1_gnn_ff2_b', 'L1_gnn_ln2_g', 'L1_gnn_ln2_b']
_REL = ['L2_gnn_weights', 'L2_gnn_roots', 'L2_gnn_biases']
_LAST = ['L3_gnn_W', 'L3_gnn_attn_l', 'L3_gnn_attn_r', 'L3_gnn_gat_bias', 'L3_gnn_lin_W', 'L3_gnn_lin_b']


def kernel(**inputs):
    import numpy as _np
    import concourse.bacc as _bacc
    from concourse import mybir as _mybir
    from concourse.bass_utils import run_bass_kernel_spmd as _run

    nc = _bacc.Bacc("TRN2", target_bir_lowering=False, num_devices=1)
    arrays = {}

    def given(names):
        aps = []
        for name in names:
            a = _np.ascontiguousarray(inputs[name])
            arrays[f"in_{name}"] = a
            aps.append(nc.dram_tensor(f"in_{name}", a.shape, _mybir.dt.from_np(a.dtype), kind="ExternalInput").ap())
        return aps

    first = given(_FIRST)
    rest = [given(names) for names in (_GCN, _LOCAL, _SSM, _MIX, _REL, _LAST)]
    out = nc.dram_tensor("out", (N, D), F32, kind="ExternalOutput").ap()
    program(nc, *first, *rest, out)
    r = _run(nc, [arrays], core_ids=[0])
    return r.results[0]["out"]
```

```python
from contextlib import ExitStack

import concourse.bass as bass
from concourse import mybir

F32, BF16, F16, I32 = mybir.dt.float32, mybir.dt.bfloat16, mybir.dt.float16, mybir.dt.int32
ALU, ACT, AX = mybir.AluOpType, mybir.ActivationFunctionType, mybir.AxisListType

P = 128
N = 3125
D = 256
T = -(-N // P)
NP = T * P
E = 100000
C = -(-E // P)
CT = -(-C // P)
G_ADJ, G_SUM = 4, 6
SPANS = [G_ADJ, G_SUM]
PAD = NP - 1
HALF = NP // 2
REL = 8
BANK = 512
BANKS = [(b, min(b + BANK, NP)) for b in range(0, NP, BANK)]
NEG = -2.0 ** 100
EPS = 1e-5
J = 400
NJ = NP // J


class Shared:
    pass


class Tick:

    def __init__(self, sem, eng=None):
        self.sem, self.eng, self.n, self.i, self.per, self.base = sem, eng, 0, None, 0, 0

    def loop(self, i, per):
        self.base, self.n, self.i, self.per = self.n, 0, i, per

    def end(self, turns):
        assert self.n == self.per, (self.n, self.per)
        self.n, self.i = self.base + turns * self.per, None

    def value(self):
        return self.n if self.i is None else self.i * self.per + (self.base + self.n)

    def __call__(self, ins):
        ins.then_inc(self.sem, 1)
        self.n += 1
        self.eng.wait_ge(self.sem, self.value())


class Phase:

    def __init__(self, nc, name):
        self.nc, self.name, self.ctx = nc, name, ExitStack()

    def __enter__(self):
        self.ctx.__enter__()
        return self

    def __exit__(self, *e):
        return self.ctx.__exit__(*e)

    def sb(self, name, shape, dt=F32):
        return self.ctx.enter_context(self.nc.sbuf_tensor(f"{self.name}_{name}", shape, dt))

    def ps(self, name, shape, dt=F32):
        return self.ctx.enter_context(self.nc.psum_tensor(f"{self.name}_{name}", shape, dt))

    def sem(self, name):
        return self.ctx.enter_context(self.nc.semaphore(f"{self.name}_{name}"))

    def sems(self, *names):
        return [self.sem(n) for n in names]

    def pool_sems(self, g, n):
        return [g.pool_sems.pop(0) for _ in range(n)]

    def block(self):
        return self.ctx.enter_context(self.nc.Block())


def constants(nc, g):
    with Phase(nc, "const") as ph:
        s_fill, s_sel = ph.sems("fill", "sel")
        num = ph.sb("num", [P, NP], I32)
        s_iota, s_cast = ph.sems("iota", "cast")
        block = ph.block()

        @block.gpsimd
        def _(pool):
            nc.gpsimd.memset(g.ident[:, :], 1.0).then_inc(s_fill, 1)
            nc.gpsimd.memset(g.ones[:, :], 1.0)
            nc.gpsimd.memset(g.zeros[:, :], 0.0)
            pool.wait_ge(s_fill, 1)
            nc.gpsimd.affine_select(out=g.ident[:, :], in_=g.ident[:, :], compare_op=ALU.is_equal, fill=0.0,
                                    base=0, pattern=[[-1, P]], channel_multiplier=1).then_inc(s_sel, 1)
            nc.gpsimd.iota(num[:, :], [[1, NP]], base=-HALF, channel_multiplier=0).then_inc(s_iota, 1)

        @block.vector
        def _(dve):
            dve.wait_ge(s_iota, 1)
            nc.vector.tensor_copy(g.numbers[:, :], num[:, :]).then_inc(s_cast, 1)


def edge_tables(nc, g, src, dst, kind):
    full = E // P
    tail = E - full * P
    R = CT - 1
    with Phase(nc, "edge") as ph:
        raw = ph.sb("raw", [P, 3, CT, P], I32)
        val = ph.sb("val", [P, 3, CT, P])
        node = ph.sb("node", [P, CT, P])
        ends = ph.sb("ends", [P, 2 * CT])
        endsT = ph.sb("endsT", [2 * CT, P])
        row = ph.sb("row", [32, 2, CT * P])
        cnum = ph.sb("cnum", [32, C])
        cnumi = ph.sb("cnumi", [32, C], I32)
        hit = ph.sb("hit", [32, C])
        low = ph.sb("low", [32, C])
        tmp = ph.sb("tmp", [32, C])
        edge0 = ph.sb("edge0", [32, 2])
        edge0i = ph.sb("edge0i", [32, 2], I32)
        span = ph.sb("span", [32, 2])
        steps = ph.sb("steps", [32, 1 + len(SPANS)])
        flat = ph.sb("flat", [1, 2 + 2 * len(SPANS), 32])
        psum = [ph.ps(f"t{k}", [P, CT * P]) for k in range(3)]
        pend = ph.ps("pend", [2 * CT, P])
        dram_ends = nc.dram_tensor("ends_rows", (2, CT * P), F32).ap()
        dram_span = nc.dram_tensor("span_rows", (1 + len(SPANS), 32), F32).ap()
        s_fill, s_in, s_val, s_end, s_T, s_Tc, s_st, s_row, s_v, s_io, s_sp, s_fl = ph.sems(
            "fill", "in", "val", "end", "T", "Tc", "st", "row", "v", "io", "sp", "fl")
        block = ph.block()

        @block.gpsimd
        def _(pool):
            nc.gpsimd.memset(raw[:, :, R, :], PAD).then_inc(s_fill, 1)
            nc.gpsimd.iota(cnumi[:, :], [[1, C]], base=0, channel_multiplier=0).then_inc(s_io, 1)
            nc.gpsimd.iota(edge0i[:, :], [[P, 2]], base=0, channel_multiplier=P).then_inc(s_io, 1)

        @block.sync
        def _(sp):
            sp.wait_ge(s_fill, 1)
            for k, a in enumerate((src, dst, kind)):
                sp.dma_start(raw[:, k, 0:R, :], a[0:R * P * P].rearrange("(r c e) -> c r e", c=P, e=P)).then_inc(s_in, 16)
                sp.dma_start(raw[0:full - R * P, k, R, :],
                             a[R * P * P:full * P].rearrange("(c e) -> c e", e=P)).then_inc(s_in, 16)
                sp.dma_start(raw[full - R * P:full - R * P + 1, k, R, 0:tail],
                             a[full * P:E].rearrange("(c e) -> c e", c=1)).then_inc(s_in, 16)
            sp.wait_ge(s_Tc, 1)
            sp.dma_start(dram_ends.rearrange("k (r p) -> (k r) p", p=P), endsT[:, :]).then_inc(s_st, 16)
            sp.wait_ge(s_st, 16)
            sp.dma_start(row[:, :, :].rearrange("p k n -> p (k n)"),
                         dram_ends.rearrange("k n -> (k n)").partition_broadcast(32)).then_inc(s_row, 16)
            sp.wait_ge(s_sp, 1)
            with nc.allow_non_contiguous_dma(reason="96 numbers"):
                sp.dma_start(dram_span.rearrange("k t -> t k"), steps[:, :]).then_inc(s_st, 16)
            sp.wait_ge(s_st, 32)
            sp.dma_start(flat[:, 0:1 + len(SPANS), :].rearrange("o k t -> o (k t)"),
                         dram_span.rearrange("k t -> (k t)").rearrange("(o n) -> o n", o=1)).then_inc(s_fl, 16)

        @block.tensor
        def _(pe):
            pe.wait_ge(s_val, 1)
            for k, a in enumerate((val[:, 0], val[:, 1], node[:, :, :])):
                for r in range(CT):
                    last = nc.tensor.transpose(psum[k][:, r * P:(r + 1) * P], a[:, r, :], g.ident[:, :])
            last.then_inc(s_T, 1)
            pe.wait_ge(s_end, 1)
            nc.tensor.transpose(pend[:, :], ends[:, :], g.ident[:, :]).then_inc(s_T, 1)

        @block.vector
        def _(dve):
            v = Tick(s_v, dve)
            dve.wait_ge(s_in, 9 * 16)
            v(nc.vector.tensor_copy(val[:, :, :, :], raw[:, :, :, :]))
            v(nc.vector.tensor_scalar(node[:, R, :], val[:, 2, R, :], float(REL - 1), None, ALU.min))
            v(nc.vector.tensor_copy(val[:, 2, R, :], node[:, R, :]))
            nc.vector.scalar_tensor_tensor(node[:, :, :], val[:, 2], float(NP), val[:, 0], ALU.mult, ALU.add).then_inc(s_val, 1)
            v(nc.vector.tensor_reduce(ends[:, 0:CT], val[:, 1], AX.X, ALU.min))
            nc.vector.tensor_reduce(ends[:, CT:], val[:, 1], AX.X, ALU.max).then_inc(s_end, 1)
            dve.wait_ge(s_T, 1)
            nc.vector.tensor_scalar(g.srcs[:, :], psum[0][:, :], -float(HALF), None, ALU.add)
            nc.vector.tensor_scalar(g.dsts[:, :], psum[1][:, :], -float(HALF), None, ALU.add)
            nc.vector.tensor_copy(g.rows[:, :], psum[2][:, :])
            dve.wait_ge(s_T, 2)
            nc.vector.tensor_copy(endsT[:, :], pend[:, :]).then_inc(s_Tc, 1)
            dve.wait_ge(s_io, 2)
            nc.vector.tensor_copy(cnum[:, :], cnumi[:, :])
            v(nc.vector.tensor_copy(edge0[:, :], edge0i[:, :]))
            dve.wait_ge(s_row, 16)
            v(nc.vector.tensor_scalar(tmp[:, :], row[:, 0, 0:C], edge0[:, 1:2], None, ALU.is_lt))
            v(nc.vector.scalar_tensor_tensor(hit[:, :], row[:, 1, 0:C], edge0[:, 0:1], tmp[:, :], ALU.is_ge, ALU.mult))
            v(nc.vector.scalar_tensor_tensor(low[:, :], hit[:, :], -1e6, cnum[:, :], ALU.mult, ALU.add))
            v(nc.vector.tensor_scalar(low[:, :], low[:, :], 1e6, float(C - 1), ALU.add, ALU.min))
            v(nc.vector.scalar_tensor_tensor(tmp[:, :], cnum[:, :], 1.0, hit[:, :], ALU.add, ALU.mult))
            v(nc.vector.tensor_reduce(span[:, 0:1], low[:, :], AX.X, ALU.min))
            v(nc.vector.tensor_reduce(span[:, 1:2], tmp[:, :], AX.X, ALU.max))
            v(nc.vector.tensor_tensor(span[:, 1:2], span[:, 1:2], span[:, 0:1], ALU.subtract))
            v(nc.vector.tensor_scalar(span[:, 1:2], span[:, 1:2], 1.0, None, ALU.max))
            v(nc.vector.tensor_copy(steps[:, 0:1], span[:, 0:1]))
            for k, size in enumerate(SPANS):
                v(nc.vector.tensor_scalar(tmp[:, :], cnum[:, :], float(size), span[:, 1:2], ALU.mult, ALU.is_lt))
                v(nc.vector.tensor_reduce(steps[:, 1 + k:2 + k], tmp[:, :], AX.X, ALU.add))
            dve.sem_inc(s_sp, 1)
            dve.wait_ge(s_fl, 16)
            K = len(SPANS)
            v(nc.vector.memset(flat[:, 1 + 2 * K, :], 1.0))
            for k in range(K):
                v(nc.vector.tensor_tensor_scan(flat[:, 1 + K + k, :], flat[:, 1 + 2 * K, :], flat[:, 1 + k, :], 0.0,
                                               ALU.mult, ALU.add))
                v(nc.vector.tensor_tensor(flat[:, 1 + K + k, :], flat[:, 1 + K + k, :], flat[:, 1 + k, :], ALU.subtract))
            nc.vector.tensor_copy(g.spans[:, :, :], flat[:, 0:1 + 2 * K, :])


def span_of(eng, g, t, size):
    k, K = SPANS.index(size), len(SPANS)
    most = -(-C // size)
    first = eng.value_load(g.spans[0:1, 0, bass.ds(t, 1)], min_val=0, max_val=C - 1)
    count = eng.value_load(g.spans[0:1, 1 + k, bass.ds(t, 1)], min_val=1, max_val=most)
    before = eng.value_load(g.spans[0:1, 1 + K + k, bass.ds(t, 1)], min_val=0, max_val=T * most)
    return first, count, before


def step_start(nc, chunk):
    return nc.s_assert_within(chunk, 0, C - 1, skip_runtime_bounds_check_because="spans end at C")


def adjacency(nc, g):
    G = G_ADJ
    NB = len(BANKS)
    with Phase(nc, "adj") as ph:
        to = ph.sb("to", [P, 4, P], BF16)
        frm = ph.sb("frm", [P, 4, NP], BF16)
        counts = ph.sb("counts", [P, NP])
        miss = ph.sb("miss", [P, NP], BF16)
        junk = ph.sb("junk", [P, NP], BF16)
        outsum = ph.sb("outsum", [P, NP])
        turned = ph.sb("turned", [P, NP])
        acc = ph.ps("acc", [P, NP])
        s_hot, s_used, s_sum, s_copied, s_masked, s_miss, s_adj, s_tp, s_tpc, s_bc = ph.sems(
            "hot", "used", "sum", "copied", "masked", "miss", "adjst", "tp", "tpc", "bc")
        s_v = ph.sem("v")
        s_in = ph.sem("indeg")
        block = ph.block()

        @block.vector
        def _(dve):
            with dve.Fori(0, T, 1) as t:
                first, count, before = span_of(dve, g, t, G)
                with dve.Fori(0, count, 1) as j:
                    c0 = step_start(nc, first + j * G)
                    for u in range(G):
                        dve.wait_ge(s_used, (before + j) * G + (u + 1))
                        nc.vector.tensor_scalar(to[:, u, :], g.numbers[:, bass.ds(t * P, P)],
                                                g.dsts[:, bass.ds(c0 + u, 1)], None, ALU.is_equal)
                        nc.vector.tensor_scalar(frm[:, u, :], g.numbers[:, :],
                                                g.srcs[:, bass.ds(c0 + u, 1)], None, ALU.is_equal).then_inc(s_hot, 1)
                dve.wait_ge(s_adj, t * 16)
                for n, (a, b) in enumerate(BANKS):
                    dve.wait_ge(s_tp, t * NB + (n + 1))
                    nc.vector.tensor_copy(turned[:, a:b], acc[:, a:b]).then_inc(s_tpc, 1)
                dve.wait_ge(s_copied, (t + 1) * NB)
                dve.wait_ge(s_miss, t * 16)
                nc.vector.tensor_scalar(miss[:, :], counts[:, :], 0.0, NEG, ALU.is_equal, ALU.mult).then_inc(s_masked, 1)
            dve.wait_ge(s_bc, 1)
            nc.vector.tensor_copy(g.outdeg[:, :], acc[:, :])

        @block.gpsimd
        def _(pool):
            nc.gpsimd.memset(outsum[:, :], 0.0).then_inc(s_v, 1)
            with pool.Fori(0, T, 1) as t:
                pool.wait_ge(s_copied, (t + 1) * NB)
                pool.wait_ge(s_v, t + 1)
                nc.gpsimd.tensor_tensor(outsum[:, :], outsum[:, :], counts[:, :], ALU.add).then_inc(s_v, 1)

        @block.tensor
        def _(pe):
            pe.sem_inc(s_used, 4)
            with pe.Fori(0, T, 1) as t:
                first, count, before = span_of(pe, g, t, G)
                for n, (a, b) in enumerate(BANKS):
                    if n == 0:
                        pe.wait_ge(s_tpc, t * NB)
                    nc.tensor.matmul(acc[:, a:b], g.zeros[:, 0:P], g.zeros[:, 0:b - a], start=True, stop=False)
                with pe.Fori(0, count, 1) as j:
                    for u in range(G):
                        pe.wait_ge(s_hot, (before + j) * G + (u + 1))
                        for a, b in BANKS:
                            last = nc.tensor.matmul(acc[:, a:b], to[:, u, :], frm[:, u, a:b], start=False, stop=False)
                        last.then_inc(s_used, 1)
                for a, b in BANKS:
                    nc.tensor.matmul(acc[:, a:b], g.zeros[:, 0:P], g.zeros[:, 0:b - a], start=False, stop=True).then_inc(s_sum, 1)
                for n, (a, b) in enumerate(BANKS):
                    pe.wait_ge(s_copied, t * NB + (n + 1))
                    for c in range(a, b, P):
                        last = nc.tensor.transpose(acc[:, c:c + P], counts[:, c:c + P], g.ident[:, :])
                    last.then_inc(s_tp, 1)
            pe.wait_ge(s_v, T + 1)
            pe.wait_ge(s_tpc, T * NB)
            for a, b in BANKS:
                last = nc.tensor.matmul(acc[:, a:b], g.ones[:, :], outsum[:, a:b], start=True, stop=True)
            last.then_inc(s_bc, 1)

        @block.scalar
        def _(act):
            with act.Fori(0, T, 1) as t:
                act.wait_ge(s_v, t + 1)
                act.wait_ge(s_masked, t)
                act.wait_ge(s_in, t)
                for n, (a, b) in enumerate(BANKS):
                    act.wait_ge(s_sum, t * NB + (n + 1))
                    nc.scalar.copy(counts[:, a:b], acc[:, a:b]).then_inc(s_copied, 1)
                act.wait_ge(s_copied, (t + 1) * NB)
                nc.scalar.activation(junk[:, :], counts[:, :], ACT.Copy, accum_out=g.indeg[:, bass.ds(t, 1)]).then_inc(s_in, 1)

        @block.sync
        def _(sp):
            with sp.Fori(0, T, 1) as t:
                a = sp.snap(t * P)
                masked, turned_ = sp.snap(t + 1), sp.snap((t + 1) * NB)
                sp.wait_ge(s_tpc, turned_)
                sp.sem_inc(g.waited, 1)
                sp.dma_start(g.adj[:, bass.ds(a, P)].rearrange("(s p) d -> p s d", p=P),
                             turned[:, :].rearrange("p (s d) -> p s d", d=P)).then_inc(s_adj, 16)
                sp.wait_ge(s_masked, masked)
                sp.sem_inc(g.waited, 1)
                sp.dma_start(g.absent[bass.ds(a, P), :], miss[:, :]).then_inc(s_miss, 16)
            sp.wait_ge(s_miss, T * 16)
            sp.wait_ge(s_adj, T * 16)


def turned_weights(nc, name, g, jobs):
    blocks = []
    for n, (w, out) in enumerate(jobs):
        O, I = w.shape
        for o in range(0, O, P):
            for k in range(0, I, P):
                blocks.append((n, o, min(P, O - o), k, min(P, I - k)))
    with Phase(nc, name) as ph:
        raw = [ph.sb(f"raw{n}", [min(P, w.shape[0]), -(-w.shape[0] // P), w.shape[1]]) for n, (w, _) in enumerate(jobs)]
        tp = [ph.ps(f"tp{k}", [P, P]) for k in range(4)]
        s_in, s_t, s_c = ph.sems("in", "t", "c")
        block = ph.block()

        @block.sync
        def _(sp):
            for (w, _), r in zip(jobs, raw):
                sp.dma_start(r[:, :, :], w.rearrange("(a p) i -> p a i", p=min(P, w.shape[0]))).then_inc(s_in, 16)

        @block.tensor
        def _(pe):
            pe.wait_ge(s_in, 16 * len(jobs))
            for b, (n, o, no, k, ni) in enumerate(blocks):
                if b >= 4:
                    pe.wait_ge(s_c, b - 3)
                nc.tensor.transpose(tp[b % 4][0:ni, 0:no], raw[n][0:no, o // P, k:k + ni], g.ident[0:no, 0:no]).then_inc(s_t, 1)

        @block.scalar
        def _(act):
            for b, (n, o, no, k, ni) in enumerate(blocks):
                act.wait_ge(s_t, b + 1)
                nc.scalar.copy(jobs[n][1][0:ni, k // P, o:o + no], tp[b % 4][0:ni, 0:no]).then_inc(s_c, 1)


def project(nc, name, g, x, weights, width, store, scale=None, extra=None, ones_at=None):
    chunks = [(a, min(a + BANK, width)) for a in range(0, width, BANK)]
    NC = len(chunks)
    heads = ones_at or 0
    with Phase(nc, name) as ph:
        tile = [ph.sb(f"tile{u}", [P, D]) for u in range(2)]
        turned = [ph.sb(f"turned{u}", [P, 2, P]) for u in range(2)]
        res = [ph.sb(f"res{u}", [P, width + heads]) for u in range(2)]
        tp = [ph.ps(f"tp{u}", [P, D]) for u in range(2)]
        mm = [ph.ps(f"mm{n}", [P, BANK]) for n in range(NC)]
        s_in = ph.sems("in0", "in1")
        s_st = ph.pool_sems(g, 2)
        s_tp, s_turn, s_mm, s_done, s_one = ph.sems("tp", "turn", "mm", "done", "one")
        nst = len(store(0, res[0]))
        block = ph.block()

        def turns(eng, step):
            with eng.Fori(0, T // 2, 1) as i:
                step(2 * i, i, 0)
                step(2 * i + 1, i, 1)
            step(T - 1, T // 2, 0)

        @block.sync
        def _(sp):
            def step(t, i, u):
                a = sp.snap(t * P) if not isinstance(t, int) else t * P
                need = sp.snap(t + 1) if not isinstance(t, int) else t + 1
                sp.wait_ge(s_tp, need)
                sp.sem_inc(g.waited, 1)
                sp.dma_start(tile[u][:, :], x[bass.ds(a, P), :]).then_inc(s_in[u], 16)
            turns(sp, step)

        @block.tensor
        def _(pe):
            pe.sem_inc(s_tp, 2)
            pe.sem_inc(s_done, NC)

            def turn(t, i, u):
                pe.wait_ge(s_in[u], (i + 1) * 16)
                for k in range(2):
                    last = nc.tensor.transpose(tp[u][:, k * P:(k + 1) * P], tile[u][:, k * P:(k + 1) * P], g.ident[:, :])
                last.then_inc(s_tp, 1)

            def multiply(t, u):
                pe.wait_ge(s_turn, t + 1)
                for n, (a, b) in enumerate(chunks):
                    pe.wait_ge(s_done, t * NC + (n + 1))
                    for k in range(2):
                        last = nc.tensor.matmul(mm[n][:, 0:b - a], turned[u][:, k, :], weights[:, k, a:b],
                                                start=k == 0, stop=k == 1)
                    last.then_inc(s_mm, 1)
            turn(0, 0, 0)
            with pe.Fori(0, T // 2, 1) as i:
                turn(2 * i + 1, i, 1)
                multiply(2 * i, 0)
                turn(2 * i + 2, i + 1, 0)
                multiply(2 * i + 1, 1)
            multiply(T - 1, 0)

        @block.scalar
        def _(act):
            def step(t, i, u):
                act.wait_ge(s_tp, t + 3)
                nc.scalar.copy(turned[u][:, :, :].rearrange("p k n -> p (k n)"), tp[u][:, :]).then_inc(s_turn, 1)
            turns(act, step)

        @block.vector
        def _(dve):
            if heads:
                for u in range(2):
                    nc.vector.memset(res[u][:, 0:heads * 65], 1.0).then_inc(s_one, 1)
                dve.wait_ge(s_one, 2)

            def step(t, i, u):
                dve.wait_ge(s_st[u], i * (16 * nst))
                for n, (a, b) in enumerate(chunks):
                    dve.wait_ge(s_mm, t * NC + (n + 1))
                    if heads:
                        nc.vector.tensor_copy(res[u][:, 0:heads * 65].rearrange("p (h c) -> p h c", c=65)[:, :, 0:64],
                                              mm[n][:, 0:heads * 64].rearrange("p (h c) -> p h c", c=64))
                        nc.vector.tensor_copy(extra[:, bass.ds(t, 1), :].rearrange("p a c -> p (a c)"),
                                              mm[n][:, heads * 64:width])
                        last = nc.vector.tensor_copy(res[u][:, heads * 65:], mm[n][:, heads * 64:width])
                    elif scale is not None:
                        last = nc.vector.tensor_scalar(res[u][:, a:b], mm[n][:, 0:b - a], scale[:, bass.ds(t, 1)], None, ALU.mult)
                    else:
                        last = nc.vector.tensor_copy(res[u][:, a:b], mm[n][:, 0:b - a])
                    last.then_inc(s_done, 1)
            turns(dve, step)

        @block.gpsimd
        def _(pool):
            def step(t, i, u):
                pool.wait_ge(s_done, (t + 2) * NC)
                for to, out in store(t, res[u]):
                    pool.dma_start(to, out).then_inc(s_st[u], 16)
            turns(pool, step)
            pool.wait_ge(s_st[0], (T - T // 2) * 16 * nst)
            pool.wait_ge(s_st[1], (T // 2) * 16 * nst)


def aggregate(nc, name, g, F, y_dram, out, beside=None):
    with Phase(nc, name) as ph:
        rows = [ph.sb(f"rows{u}", [P, NP]) for u in range(2)]
        ys = [ph.sb(f"ys{u}", [P, F]) for u in range(2)]
        sums = ph.sb("sums", [F, NP])
        per = BANK // F
        s_in = ph.sems("in0", "in1")
        s_free, s_done, s_c, s_t, s_o = ph.sems("free", "done", "c", "t", "o")
        with ExitStack() as own:
            acc = own.enter_context(nc.psum_tensor(f"{name}_acc", [F, NP], F32))
            tp = own.enter_context(nc.psum_tensor(f"{name}_tp", [P, BANK], F32))
            rounds = [range(a, min(a + per, T)) for a in range(0, T, per)]
            with nc.Block() as block:
                @block.sync
                def _(sp):
                    def step(t, i, u):
                        a = sp.snap(t * P) if not isinstance(t, int) else t * P
                        need = sp.snap(t + 1) if not isinstance(t, int) else t + 1
                        sp.wait_ge(s_free, need)
                        sp.sem_inc(g.waited, 1)
                        sp.dma_start(rows[u][:, :], g.adj[bass.ds(a, P), :]).then_inc(s_in[u], 16)
                        sp.dma_start(ys[u][:, :], y_dram[bass.ds(a, P), :]).then_inc(s_in[u], 16)
                    with sp.Fori(0, T // 2, 1) as i:
                        step(2 * i, i, 0)
                        step(2 * i + 1, i, 1)
                    step(T - 1, T // 2, 0)

                @block.tensor
                def _(pe):
                    pe.sem_inc(s_free, 2)
                    for a, b in BANKS:
                        nc.tensor.matmul(acc[:, a:b], g.zeros[:, 0:F], g.zeros[:, 0:b - a], start=True, stop=False)

                    def step(i, u, stop):
                        pe.wait_ge(s_in[u], (i + 1) * 32)
                        for a, b in BANKS:
                            last = nc.tensor.matmul(acc[:, a:b], ys[u][:, :], rows[u][:, a:b], start=False, stop=stop)
                        last.then_inc(s_free, 1)
                    with pe.Fori(0, T // 2, 1) as i:
                        step(i, 0, False)
                        step(i, 1, False)
                    step(T // 2, 0, True)
                    for k, rnd in enumerate(rounds):
                        pe.wait_ge(s_c, min(len(BANKS), rnd[-1] * P // BANK + 1))
                        if k:
                            pe.wait_ge(s_o, k)
                        for n, t in enumerate(rnd):
                            last = nc.tensor.transpose(tp[:, n * F:(n + 1) * F], sums[:, t * P:(t + 1) * P], g.ident[0:F, 0:F])
                        last.then_inc(s_t, 1)

                @block.scalar
                def _(act):
                    act.wait_ge(s_free, T + 2)
                    for a, b in BANKS:
                        nc.scalar.copy(sums[:, a:b], acc[:, a:b]).then_inc(s_c, 1)

                @block.vector
                def _(dve):
                    if beside:
                        beside(dve)
                    for k, rnd in enumerate(rounds):
                        dve.wait_ge(s_t, k + 1)
                        nc.vector.tensor_copy(out[:, rnd[0]:rnd[-1] + 1, :].rearrange("p t f -> p (t f)"),
                                              tp[:, 0:len(rnd) * F]).then_inc(s_o, 1)


class Norm:

    def __init__(self, ph, name):
        self.stats = ph.sb(f"{name}_stats", [P, T, 6])
        self.mv = ph.sb(f"{name}_mv", [P, T, 2])
        self.std, self.less, self.eps = (ph.sb(f"{name}_{n}", [P, T]) for n in ("std", "less", "eps"))
        self.s_var, self.s_std, self.s_rec, self.s_out = ph.sems(*(f"{name}_{n}" for n in ("var", "std", "rec", "out")))

    def dve(self, nc, dve, v, x, gain=None, shift=None):
        v(nc.vector.memset(self.eps[:, :], EPS))
        for t in range(T):
            last = nc.vector.bn_stats(self.stats[:, t, :], x[:, t, :])
        v(last)
        for t in range(T):
            last = nc.vector.bn_aggr(self.mv[:, t, :], self.stats[:, t, :])
        last.then_inc(self.s_var, 1)
        dve.wait_ge(self.s_std, 1)
        v(nc.vector.reciprocal(self.std[:, :], self.std[:, :]))
        nc.vector.scalar_tensor_tensor(self.less[:, :], self.mv[:, :, 0], -1.0, self.std[:, :], ALU.mult,
                                       ALU.mult).then_inc(self.s_rec, 1)
        dve.wait_ge(self.s_out, T)
        if gain is not None:
            along = lambda a: a[:, :].unsqueeze(1).to_broadcast([P, T, D])
            v(nc.vector.tensor_tensor(x[:, :, :], x[:, :, :], along(gain), ALU.mult))
            v(nc.vector.tensor_tensor(x[:, :, :], x[:, :, :], along(shift), ALU.add))

    def act(self, nc, act, x):
        act.wait_ge(self.s_var, 1)
        nc.scalar.activation(self.std[:, :], self.mv[:, :, 1], ACT.Sqrt, bias=self.eps[:, 0:1]).then_inc(self.s_std, 1)
        act.wait_ge(self.s_rec, 1)
        for t in range(T):
            nc.scalar.activation(x[:, t, :], x[:, t, :], ACT.Identity, bias=self.less[:, t:t + 1],
                                 scale=self.std[:, t:t + 1]).then_inc(self.s_out, 1)


def nodes(a):
    return a.rearrange("(t p) f -> p t f", p=P)


def row(a):
    return a.partition_broadcast(P)


def load_x(nc, g, x, x_dram):
    with Phase(nc, "loadx") as ph:
        buf = ph.sb("buf", [P, T, D])
        s_z, s_in, s_st, s_v, s_d = ph.sems("z", "in", "st", "v", "d")
        whole = N // P
        block = ph.block()

        @block.vector
        def _(dve):
            nc.vector.memset(buf[:, whole, :], 0.0).then_inc(s_z, 1)
            nc.vector.tensor_scalar(g.dinv[:, :], g.indeg[:, :], 1.0, None, ALU.add).then_inc(s_v, 1)
            dve.wait_ge(s_d, 1)
            nc.vector.reciprocal(g.dinv[:, :], g.dinv[:, :])

        @block.scalar
        def _(act):
            act.wait_ge(s_v, 1)
            nc.scalar.activation(g.dinv[:, :], g.dinv[:, :], ACT.Sqrt).then_inc(s_d, 1)

        @block.sync
        def _(sp):
            sp.wait_ge(s_z, 1)
            sp.dma_start(buf[:, 0:whole, :], nodes(x[0:whole * P, :])).then_inc(s_in, 16)
            sp.dma_start(buf[0:N - whole * P, whole, :], x[whole * P:N, :]).then_inc(s_in, 16)
            sp.wait_ge(s_in, 32)
            sp.dma_start(nodes(x_dram), buf[:, :, :]).then_inc(s_st, 16)
            sp.wait_ge(s_st, 16)


def gcn_stack(nc, g, x_dram, ranking, W1, b1, W2, b2, W3, b3, W4, b4, x_out):
    F = 64
    with Phase(nc, "gcn") as top:
        w12 = top.sb("w12", [P, 2, F])
        w34 = top.sb("w34", [F + 1, D])
        b1w2 = top.sb("b1w2", [P, F])
        b2r = top.sb("b2r", [P, F])
        b4r = top.sb("b4r", [P, D])
        y_dram = nc.dram_tensor("gcn_y", (NP, F), F32).ap()
        y1_dram = nc.dram_tensor("gcn_y1", (NP, F + 1), F32).ap()
        with Phase(nc, "gcnw") as ph:
            w1 = ph.sb("w1", [P, 2, P])
            w1T = ph.sb("w1T", [P, D])
            w2 = ph.sb("w2", [P, F])
            w3b = ph.sb("w3b", [F + 1, P])
            w3bT = ph.sb("w3bT", [P, F + 1])
            w4 = ph.sb("w4", [P, D])
            b1c = ph.sb("b1c", [P, 1])
            b1b = ph.sb("b1b", [P, P])
            tp = ph.ps("tp", [P, BANK])
            mm = ph.ps("mm", [P, BANK])
            s_in, s_t, s_tc, s_m, s_b = ph.sems("in", "t", "tc", "m", "b")
            block = ph.block()

            @block.sync
            def _(sp):
                for to, a in ((w1[:, :, :], W1.rearrange("(k p) n -> p k n", p=P)), (w2[:, :], W2), (w3b[0:F, :], W3),
                              (w3b[F:F + 1, :], b3.rearrange("(o n) -> o n", o=1)), (w4[:, :], W4),
                              (b1c[:, :], b1.rearrange("(n o) -> n o", o=1)), (b2r[:, :], row(b2)), (b4r[:, :], row(b4))):
                    sp.dma_start(to, a).then_inc(s_in, 16)

            @block.tensor
            def _(pe):
                pe.wait_ge(s_in, 8 * 16)
                for k in range(2):
                    nc.tensor.transpose(tp[:, k * P:(k + 1) * P], w1[:, k, :], g.ident[:, :])
                nc.tensor.transpose(tp[:, D:D + F + 1], w3b[:, :], g.ident[0:F + 1, 0:F + 1]).then_inc(s_t, 1)
                pe.wait_ge(s_tc, 1)
                for k in range(2):
                    nc.tensor.matmul(mm[:, k * F:(k + 1) * F], w1T[:, k * P:(k + 1) * P], w2[:, :], start=True, stop=True)
                nc.tensor.matmul(mm[:, P:P + F], b1b[:, :], w2[:, :], start=True, stop=True)
                nc.tensor.matmul(mm[0:F + 1, D:2 * D], w3bT[:, :], w4[:, :], start=True, stop=True).then_inc(s_m, 1)

            @block.vector
            def _(dve):
                dve.wait_ge(s_in, 8 * 16)
                nc.vector.tensor_copy(b1b[:, :], b1c[:, 0:1].to_broadcast([P, P]))
                dve.wait_ge(s_t, 1)
                nc.vector.tensor_copy(w1T[:, :], tp[:, 0:D])
                nc.vector.tensor_copy(w3bT[:, :], tp[:, D:D + F + 1]).then_inc(s_tc, 1)
                dve.wait_ge(s_m, 1)
                nc.vector.tensor_copy(w12[:, :, :].rearrange("p k n -> p (k n)"), mm[:, 0:P])
                nc.vector.tensor_copy(b1w2[:, :], mm[:, P:P + F])
                nc.vector.tensor_copy(w34[:, :], mm[0:F + 1, D:2 * D])

        project(nc, "gcnp", g, x_dram, w12, F, lambda t, out: [(y_dram[bass.ds(t * P, P), :], out[:, :])], scale=g.dinv)
        with Phase(nc, "gcns") as st:
            y = st.sb("y", [P, T, F + 1])
            a64 = st.sb("a64", [P, T, F])
            a65 = st.sb("a65", [P, T, F + 1])
            y64 = st.sb("y64", [P, T, F])
            for n in range(4):
                a, yy = (a64, y64) if n < 2 else (a65, y)
                width = F if n < 2 else F + 1
                aggregate(nc, f"agg{n}", g, width, y_dram if n < 2 else y1_dram, a, ranking.part(n) if n < 2 else None)
                if n == 3:
                    break
                with Phase(nc, f"gcnc{n}") as ph:
                    s_in, s_v, s_a, s_b, s_st = ph.sems("in", "v", "a", "b", "st")
                    block = ph.block()
                    wide = lambda w: g.dinv[:, :].unsqueeze(2).to_broadcast([P, T, w])
                    along = lambda r: r[:, :].unsqueeze(1).to_broadcast([P, T, F])

                    @block.sync
                    def _(sp):
                        if n == 0:
                            sp.dma_start(y64[:, :, :], nodes(y_dram)).then_inc(s_in, 16)
                        sp.wait_ge(s_b, 1)
                        if n == 0:
                            sp.dma_start(nodes(y_dram), y64[:, :, :]).then_inc(s_st, 16)
                        else:
                            sp.dma_start(nodes(y1_dram), y[:, :, :]).then_inc(s_st, 16)
                        sp.wait_ge(s_st, 16)

                    @block.vector
                    def _(dve):
                        v = Tick(s_v, dve)
                        if n == 0:
                            dve.wait_ge(s_in, 16)
                        v(nc.vector.tensor_tensor(a[:, :, :], a[:, :, :], yy[:, :, :], ALU.add))
                        v(nc.vector.tensor_tensor(a[:, :, :], a[:, :, :], wide(width), ALU.mult))
                        if n == 0:
                            v(nc.vector.tensor_tensor(a[:, :, :], a[:, :, :], along(b1w2), ALU.add))
                            nc.vector.tensor_tensor(y64[:, :, :], a[:, :, :], wide(F), ALU.mult).then_inc(s_b, 1)
                        elif n == 1:
                            nc.vector.tensor_tensor(a[:, :, :], a[:, :, :], along(b2r), ALU.add).then_inc(s_a, 1)
                            v(nc.vector.memset(y[:, :, F:F + 1], 1.0))
                            dve.wait_ge(s_a, 2)
                            nc.vector.tensor_tensor(y[:, :, :], y[:, :, :], wide(F + 1), ALU.mult).then_inc(s_b, 1)
                        else:
                            v(nc.vector.memset(a[:, :, F:F + 1], 1.0))
                            nc.vector.tensor_tensor(y[:, :, :], a[:, :, :], wide(F + 1), ALU.mult).then_inc(s_b, 1)

                    @block.scalar
                    def _(act):
                        if n == 1:
                            act.wait_ge(s_a, 1)
                            nc.scalar.activation(y[:, :, 0:F], a[:, :, :], ACT.Sigmoid).then_inc(s_a, 1)
            with Phase(nc, "gcno") as ph:
                x = ph.sb("x", [P, T, D])
                w = ph.sb("w", [P, T, D])
                turned = [ph.sb(f"turned{u}", [F + 1, 2 * P]) for u in range(2)]
                norm = Norm(ph, "n")
                tp = [ph.ps(f"tp{u}", [F + 1, BANK]) for u in range(2)]
                mm = [ph.ps(f"mm{u}", [P, BANK]) for u in range(2)]
                s_in, s_v, s_a, s_t, s_c, s_m, s_r, s_o, s_st = ph.sems("in", "v", "a", "t", "c", "m", "r", "o", "st")
                pairs = [range(a, min(a + 2, T)) for a in range(0, T, 2)]
                block = ph.block()

                @block.sync
                def _(sp):
                    sp.dma_start(x[:, :, :], nodes(x_dram)).then_inc(s_in, 16)
                    sp.wait_ge(s_o, 1)
                    sp.dma_start(nodes(x_out), x[:, :, :]).then_inc(s_st, 16)
                    sp.wait_ge(s_st, 16)

                @block.tensor
                def _(pe):
                    pe.wait_ge(s_a, 1)
                    for k, pr in enumerate(pairs):
                        if k > 1:
                            pe.wait_ge(s_c, k - 1)
                        for n, t in enumerate(pr):
                            last = nc.tensor.transpose(tp[k % 2][:, n * P:(n + 1) * P], a65[:, t, :], g.ident[:, :])
                        last.then_inc(s_t, 1)
                        pe.wait_ge(s_c, k + 1)
                        if k > 1:
                            pe.wait_ge(s_r, k - 1)
                        for n, t in enumerate(pr):
                            last = nc.tensor.matmul(mm[k % 2][:, n * D:(n + 1) * D], turned[k % 2][:, n * P:(n + 1) * P], w34[:, :],
                                                    start=True, stop=True)
                        last.then_inc(s_m, 1)

                @block.scalar
                def _(act):
                    for k, pr in enumerate(pairs):
                        act.wait_ge(s_t, k + 1)
                        nc.scalar.copy(turned[k % 2][:, 0:len(pr) * P], tp[k % 2][:, 0:len(pr) * P]).then_inc(s_c, 1)
                    norm.act(nc, act, x)

                @block.vector
                def _(dve):
                    v = Tick(s_v, dve)
                    wide = g.dinv[:, :].unsqueeze(2).to_broadcast([P, T, F + 1])
                    v(nc.vector.tensor_tensor(a65[:, :, :], a65[:, :, :], y[:, :, :], ALU.add))
                    nc.vector.tensor_tensor(a65[:, :, :], a65[:, :, :], wide, ALU.mult).then_inc(s_a, 1)
                    for k, pr in enumerate(pairs):
                        dve.wait_ge(s_m, k + 1)
                        nc.vector.tensor_tensor(w[:, pr[0]:pr[-1] + 1, :],
                                                mm[k % 2][:, 0:len(pr) * D].rearrange("p (t d) -> p t d", d=D),
                                                b4r[:, :].unsqueeze(1).to_broadcast([P, len(pr), D]), ALU.add).then_inc(s_r, 1)
                    dve.wait_ge(s_r, len(pairs))
                    dve.wait_ge(s_in, 16)
                    v(nc.vector.scalar_tensor_tensor(x[:, :, :], w[:, :, :], 0.0, x[:, :, :], ALU.max, ALU.add))
                    norm.dve(nc, dve, v, x)
                    dve.sem_inc(s_o, 1)


class Ranking:

    def __init__(self, nc, g, ph, noise):
        self.nc, self.g = nc, g
        self.key = ph.sb("key", [P, NP])
        self.keyc = ph.sb("keyc", [P, T])
        self.own = ph.sb("own", [P, T])
        self.before = ph.sb("before", [P, NP], BF16)
        self.same = ph.sb("same", [P, NP], BF16)
        self.less = ph.sb("less", [P, NP], BF16)
        self.rank = ph.sb("rank", [P, T])
        self.s_v, self.s_v2 = ph.sems("v", "v2")
        self.noise = noise

    def keys(self, outdeg):
        nc, key = self.nc, self.key
        with Phase(nc, "rankk") as ph:
            nrow = ph.sb("nrow", [P, N])
            owni = ph.sb("owni", [P, T], I32)
            key_dram = nc.dram_tensor("key_row", (1, NP), F32).ap()
            s_in, s_v, s_k, s_st, s_kc, s_io = ph.sems("in", "v", "k", "st", "kc", "io")
            block = ph.block()

            @block.gpsimd
            def _(pool):
                nc.gpsimd.iota(owni[:, :], [[P, T]], base=-HALF, channel_multiplier=1).then_inc(s_io, 1)

            @block.sync
            def _(sp):
                sp.dma_start(nrow[:, :], row(self.noise)).then_inc(s_in, 16)
                sp.wait_ge(s_k, 1)
                sp.dma_start(key_dram, key[0:1, :]).then_inc(s_st, 16)
                sp.wait_ge(s_st, 16)
                with nc.allow_non_contiguous_dma(reason="one key for each node"):
                    sp.dma_start(self.keyc[:, :], key_dram.rearrange("o (t p) -> p (o t)", p=P)).then_inc(s_kc, 16)
                sp.wait_ge(s_kc, 16)

            @block.vector
            def _(dve):
                v = Tick(s_v, dve)
                dve.wait_ge(s_in, 16)
                v(nc.vector.memset(key[:, N:NP], 1e30))
                nc.vector.tensor_tensor(key[:, 0:N], outdeg[:, 0:N], nrow[:, :], ALU.add).then_inc(s_k, 1)
                dve.wait_ge(s_io, 1)
                v(nc.vector.tensor_copy(self.own[:, :], owni[:, :]))

    def part(self, n):
        nc, key = self.nc, self.key
        start, end = ((0, 13), (13, T))[n]

        def work(dve):
            v = Tick((self.s_v, self.s_v2)[n], dve)
            with dve.Fori(0, end - start, 1) as i:
                v.loop(i, 4)
                at = bass.ds(i + start, 1)
                v(nc.vector.tensor_scalar(self.before[:, :], self.g.numbers[:, :], self.own[:, at], None, ALU.is_lt))
                v(nc.vector.scalar_tensor_tensor(self.same[:, :], key[:, :], self.keyc[:, at], self.before[:, :],
                                                 ALU.is_equal, ALU.mult))
                v(nc.vector.scalar_tensor_tensor(self.less[:, :], key[:, :], self.keyc[:, at], self.same[:, :],
                                                 ALU.is_lt, ALU.add))
                v(nc.vector.tensor_reduce(self.rank[:, at], self.less[:, :], AX.X, ALU.add))
            v.end(end - start)
            if end == T:
                nc.vector.tensor_copy(self.g.rank[:, :], self.rank[:, :])
        return work


def score_rows(nc, name, g, H, extra, row_dram, col0=0):
    W = extra.shape[2]
    half = [(0, 13), (13, T)]
    with Phase(nc, name) as ph:
        rows = [ph.sb(f"rows{k}", [13 * W, P]) for k in range(2)]
        tp = [ph.ps(f"tp{k}", [13 * W, P]) for k in range(2)]
        s_t, s_c, s_st = ph.sems("t", "c", "st")
        block = ph.block()

        @block.tensor
        def _(pe):
            for k, (a, b) in enumerate(half):
                nc.tensor.transpose(tp[k][0:(b - a) * W, :], extra[:, a:b, :].rearrange("p t c -> p (t c)"), g.ident[:, :]).then_inc(s_t, 1)

        @block.vector
        def _(dve):
            for k, (a, b) in enumerate(half):
                dve.wait_ge(s_t, k + 1)
                nc.vector.tensor_copy(rows[k][0:(b - a) * W, :], tp[k][0:(b - a) * W, :]).then_inc(s_c, 1)

        @block.sync
        def _(sp):
            for k, (a, b) in enumerate(half):
                sp.wait_ge(s_c, k + 1)
                for t in range(a, b):
                    sp.dma_start(row_dram[:, t * P:(t + 1) * P], rows[k][(t - a) * W:(t - a + 1) * W, :]).then_inc(s_st, 16)
            sp.wait_ge(s_st, 16 * T)


def attention(nc, name, g, H, pr_dram, scores, agg_dram, by_target):
    with Phase(nc, name) as top:
        rows_dram = nc.dram_tensor(f"{name}_scores", (2 * H, NP), F32).ap()
        m_dram = nc.dram_tensor(f"{name}_best", (H, NP), F32).ap()
        score_rows(nc, f"{name}s", g, H, scores, rows_dram)
        top_m = top.sb("m", [P, T, H])
        with Phase(nc, f"{name}m") as ph:
            srow = ph.sb("srow", [P, H, NP])
            gone = [ph.sb(f"gone{u}", [P, NP], BF16) for u in range(2)]
            junk = ph.sb("junk", [P, H, NP], BF16)
            top4 = ph.sb("top4", [P, 2, H])
            best = ph.sb("best", [P, T, H])
            s_row, s_used, s_v, s_x = ph.sems("row", "used", "v", "x")
            s_in = ph.sems("in0", "in1")
            block = ph.block()

            @block.sync
            def _(sp):
                sp.dma_start(srow[:, :, :].rearrange("p h n -> p (h n)"),
                             row(rows_dram[0:H, :].rearrange("h n -> (h n)"))).then_inc(s_row, 16)

                def step(t, i, u):
                    a = sp.snap(t * P) if not isinstance(t, int) else t * P
                    need = sp.snap(t + 1) if not isinstance(t, int) else t + 1
                    sp.wait_ge(s_used, need)
                    sp.sem_inc(g.waited, 1)
                    sp.dma_start(gone[u][:, :], g.absent[bass.ds(a, P), :]).then_inc(s_in[u], 16)
                with sp.Fori(0, T // 2, 1) as i:
                    step(2 * i, i, 0)
                    step(2 * i + 1, i, 1)
                step(T - 1, T // 2, 0)

            @block.vector
            def _(dve):
                dve.wait_ge(s_row, 16)
                dve.sem_inc(s_used, 2)

                def step(t, i, u):
                    dve.wait_ge(s_in[u], (i + 1) * 16)
                    dve.sem_inc(g.waited, 1)
                    for h in range(H):
                        last = nc.vector.tensor_tensor_reduce(out=junk[:, h, :], in0=gone[u][:, :], in1=srow[:, h, :], scale=1.0,
                                                              scalar=-3e38, op0=ALU.add, op1=ALU.max,
                                                              accum_out=top4[:, u, h:h + 1])
                    last.then_inc(s_x, 1)
                    dve.wait_ge(s_x, t + 1)
                    nc.vector.tensor_copy(best[:, bass.ds(t, 1), :].rearrange("p a h -> p (a h)"), top4[:, u, :]).then_inc(s_used, 1)
                with dve.Fori(0, T // 2, 1) as i:
                    step(2 * i, i, 0)
                    step(2 * i + 1, i, 1)
                step(T - 1, T // 2, 0)
                v = Tick(s_v, dve)
                dve.wait_ge(s_used, T + 2)
                if by_target:
                    v(nc.vector.tensor_scalar(top_m[:, :, :], best[:, :, :], 0.5 * NEG, -NEG, ALU.is_lt, ALU.mult))
                    v(nc.vector.tensor_tensor(best[:, :, :], best[:, :, :], top_m[:, :, :], ALU.add))
                v(nc.vector.tensor_tensor(best[:, :, :], best[:, :, :], scores[:, :, H:2 * H], ALU.add))
                v(nc.vector.scalar_tensor_tensor(top_m[:, :, :], best[:, :, :], 0.2, best[:, :, :], ALU.mult, ALU.max))
        score_rows(nc, f"{name}t", g, H, top_m, m_dram)
        with Phase(nc, f"{name}x") as ph:
            t1 = ph.sb("t1", [P, H, NP])
            t2 = ph.sb("t2", [P, H, NP])
            s08 = ph.sb("s08", [P, T, H])
            s02 = ph.sb("s02", [P, T, H])
            allm = ph.sb("allm", [P, 1])
            adj = [ph.sb(f"adj{u}", [P, J]) for u in range(3)]
            feat = [ph.sb(f"feat{u}", [P, H * 65]) for u in range(3)]
            z = [ph.sb(f"z{u}", [P, H, J]) for u in range(3)]
            e = [ph.sb(f"e{u}", [P, H, J]) for u in range(3)]
            w = [ph.sb(f"w{u}", [P, H, J]) for u in range(3)]
            agg = ph.sb("agg", [65, H, J])
            acc = [ph.ps(f"acc{h}", [65, J]) for h in range(H)]
            s_row, s_v, s_ready = ph.sems("row", "v", "ready")
            s_in = ph.sems("in0", "in1", "in2")
            s_z, s_e, s_w, s_used, s_out = ph.sems("z", "e", "w", "used", "out")
            (s_st,) = ph.pool_sems(g, 1)
            block = ph.block()

            def turns(eng, step, begin, end):
                with eng.Fori(0, NJ, 1) as j:
                    begin(j)
                    with eng.Fori(0, T // 2, 1) as i:
                        step(j, 2 * i, j * T + 2 * i, j * (T // 2) + i, 0)
                        step(j, 2 * i + 1, j * T + 2 * i + 1, j * (T // 2) + i, 1)
                    step(j, T - 1, j * T + (T - 1), j, 2)
                    end(j)

            nothing = lambda j: None

            @block.sync
            def _(sp):
                sp.dma_start(t1[:, :, :].rearrange("p h n -> p (h n)"),
                             row(rows_dram[H:2 * H, :].rearrange("h n -> (h n)"))).then_inc(s_row, 16)
                sp.dma_start(t2[:, :, :].rearrange("p h n -> p (h n)"),
                             row(m_dram.rearrange("h n -> (h n)"))).then_inc(s_row, 16)

                def step(j, s, q, n, u):
                    a = sp.snap(s * P)
                    c = sp.snap(j * J)
                    need = sp.snap(q)
                    sp.wait_ge(s_used, need)
                    sp.sem_inc(g.waited, 1)
                    sp.dma_start(adj[u][:, :], g.adj[bass.ds(a, P), bass.ds(c, J)]).then_inc(s_in[u], 16)
                    sp.dma_start(feat[u][:, :], pr_dram[bass.ds(a, P), 0:H * 65]).then_inc(s_in[u], 16)
                turns(sp, step, nothing, nothing)

            @block.vector
            def _(dve):
                v = Tick(s_v, dve)
                dve.wait_ge(s_row, 32)
                if by_target:
                    v(nc.vector.tensor_tensor(t1[:, :, :], t1[:, :, :], t2[:, :, :], ALU.subtract))
                    v(nc.vector.tensor_scalar(t2[:, :, :], t2[:, :, :], -0.8, None, ALU.mult))
                    v(nc.vector.scalar_tensor_tensor(t2[:, :, :], t1[:, :, :], 0.2, t2[:, :, :], ALU.mult, ALU.add))
                    v(nc.vector.tensor_scalar(s02[:, :, :], scores[:, :, 0:H], 0.2, None, ALU.mult))
                else:
                    v(nc.vector.tensor_reduce(allm[:, :], t2[:, :, 0:N], AX.XY, ALU.max))
                    v(nc.vector.tensor_scalar(t2[:, :, :], t1[:, :, :], 0.2, None, ALU.mult))
                    v(nc.vector.tensor_scalar(s02[:, :, :], scores[:, :, 0:H], 0.2, allm[:, 0:1], ALU.mult, ALU.subtract))
                v(nc.vector.tensor_scalar(s08[:, :, :], scores[:, :, 0:H], 0.8, None, ALU.mult))
                dve.sem_inc(s_ready, 1)
                dve.sem_inc(s_w, 1)

                def scores_of(j, s, u):
                    c = dve.snap(j * J)
                    for h in range(H):
                        last = nc.vector.scalar_tensor_tensor(z[u][:, h, :], t1[:, h, bass.ds(c, J)],
                                                              s08[:, bass.ds(s, 1), h], t2[:, h, bass.ds(c, J)],
                                                              ALU.add, ALU.max)
                    last.then_inc(s_z, 1)

                def weights_of(q, n, u):
                    dve.wait_ge(s_in[u], (n + 1) * 32)
                    dve.wait_ge(s_used, q)
                    dve.wait_ge(s_e, q + 1)
                    nc.vector.scalar_tensor_tensor(w[u][:, :, :], e[u][:, :, :], 1.0,
                                                   adj[u][:, :].unsqueeze(1).to_broadcast([P, H, J]),
                                                   ALU.min, ALU.mult).then_inc(s_w, 1)

                with dve.Fori(0, NJ, 1) as j:
                    scores_of(j, 0, 0)
                    with dve.Fori(0, T // 2 - 1, 1) as i:
                        scores_of(j, 2 * i + 1, 1)
                        weights_of(j * T + 2 * i, j * (T // 2) + i, 0)
                        scores_of(j, 2 * i + 2, 0)
                        weights_of(j * T + 2 * i + 1, j * (T // 2) + i, 1)
                    scores_of(j, T - 2, 1)
                    weights_of(j * T + (T - 3), j * (T // 2) + (T // 2 - 1), 0)
                    scores_of(j, T - 1, 2)
                    weights_of(j * T + (T - 2), j * (T // 2) + (T // 2 - 1), 1)
                    weights_of(j * T + (T - 1), j, 2)

            @block.scalar
            def _(act):
                act.wait_ge(s_ready, 1)

                def step(j, s, q, n, u):
                    act.wait_ge(s_z, q + 1)
                    act.wait_ge(s_w, q)
                    for h in range(H):
                        last = nc.scalar.activation(e[u][:, h, :], z[u][:, h, :], ACT.Exp, bias=s02[:, bass.ds(s, 1), h])
                    last.then_inc(s_e, 1)

                def end(j):
                    act.wait_ge(s_used, (j + 1) * T + 1)
                    act.wait_ge(s_st, j * 16)
                    for h in range(H):
                        last = nc.scalar.copy(agg[:, h, :], acc[h][:, :])
                    last.then_inc(s_out, 1)
                turns(act, step, nothing, end)

            @block.tensor
            def _(pe):
                pe.sem_inc(s_used, 1)

                def begin(j):
                    pe.wait_ge(s_out, j)
                    for h in range(H):
                        nc.tensor.matmul(acc[h][:, :], g.zeros[:, 0:65], g.zeros[:, 0:J], start=True, stop=False)

                def step(j, s, q, n, u):
                    stop = isinstance(s, int)
                    pe.wait_ge(s_in[u], (n + 1) * 32)
                    pe.wait_ge(s_w, q + 2)
                    for h in range(H):
                        last = nc.tensor.matmul(acc[h][:, :], feat[u][:, h * 65:(h + 1) * 65], w[u][:, h, :], start=False, stop=stop)
                    last.then_inc(s_used, 1)
                turns(pe, step, begin, nothing)

            @block.gpsimd
            def _(pool):
                with pool.Fori(0, NJ, 1) as j:
                    pool.wait_ge(s_out, j + 1)
                    pool.dma_start(agg_dram[:, :, bass.ds(j * J, J)].rearrange("h c n -> c h n"), agg[:, :, :]).then_inc(s_st, 16)
                pool.wait_ge(s_st, NJ * 16)


def heads_to_nodes(nc, name, g, H, agg_dram, out, floor):
    with Phase(nc, name) as ph:
        part = [ph.sb(f"part{u}", [65, H, P]) for u in range(2)]
        den = ph.sb("den", [P, H])
        tp = [ph.ps(f"tp{u}", [P, BANK]) for u in range(2)]
        s_in = ph.sems("in0", "in1")
        s_t, s_o, s_v = ph.sems("t", "o", "v")
        block = ph.block()

        def turns(eng, step):
            with eng.Fori(0, T // 2, 1) as i:
                step(2 * i, i, 0)
                step(2 * i + 1, i, 1)
            step(T - 1, T // 2, 0)

        @block.sync
        def _(sp):
            def step(t, i, u):
                a = sp.snap(t * P) if not isinstance(t, int) else t * P
                need = sp.snap(t + 1) if not isinstance(t, int) else t + 1
                sp.wait_ge(s_t, need)
                sp.sem_inc(g.waited, 1)
                sp.dma_start(part[u][:, :, :], agg_dram[:, :, bass.ds(a, P)].rearrange("h c n -> c h n")).then_inc(s_in[u], 16)
            turns(sp, step)

        @block.tensor
        def _(pe):
            pe.sem_inc(s_t, 2)

            def step(t, i, u):
                pe.wait_ge(s_in[u], (i + 1) * 16)
                pe.wait_ge(s_o, t)
                for h in range(H):
                    last = nc.tensor.transpose(tp[u][:, h * 65:(h + 1) * 65], part[u][:, h, :], g.ident[0:65, 0:65])
                last.then_inc(s_t, 1)
            turns(pe, step)

        @block.vector
        def _(dve):
            def step(t, i, u):
                dve.wait_ge(s_t, t + 3)
                heads = tp[u][:, 0:H * 65].rearrange("p (h c) -> p h c", c=65)
                nc.vector.tensor_scalar(den[:, :].unsqueeze(2), heads[:, :, 64:65], floor[1], None, floor[0]).then_inc(s_v, 1)
                dve.wait_ge(s_v, 2 * t + 1)
                nc.vector.reciprocal(den[:, :], den[:, :]).then_inc(s_v, 1)
                dve.wait_ge(s_v, 2 * t + 2)
                nc.vector.tensor_tensor(out[:, bass.ds(t, 1), :].rearrange("p a (h c) -> p (a h) c", c=64), heads[:, :, 0:64],
                                        den[:, :].unsqueeze(2).to_broadcast([P, H, 64]), ALU.mult).then_inc(s_o, 1)
            turns(dve, step)


def score_weights(nc, name, g, W, turned, a_src, a_tgt, H, out):
    K = H * 64 // P
    with Phase(nc, name) as ph:
        diag = ph.sb("diag", [P, K, 2 * H])
        mm = ph.ps("mm", [P, 2 * 2 * H])
        s_z, s_in, s_m = ph.sems("z", "in", "m")
        block = ph.block()

        @block.vector
        def _(dve):
            nc.vector.memset(diag[:, :, :], 0.0).then_inc(s_z, 1)
            dve.wait_ge(s_m, 1)
            nc.vector.tensor_copy(out[:, :, H * 64:H * 66], mm[:, :].rearrange("p (k c) -> p k c", k=2))

        @block.sync
        def _(sp):
            sp.wait_ge(s_z, 1)
            for n, a in enumerate((a_src, a_tgt)):
                for h in range(H):
                    p = 64 * (h % 2)
                    with nc.allow_non_contiguous_dma(reason="64 numbers"):
                        sp.dma_start(diag[p:p + 64, h // 2, n * H + h:n * H + h + 1],
                                     a[h, :].rearrange("(c o) -> c o", o=1)).then_inc(s_in, 16)

        @block.tensor
        def _(pe):
            pe.wait_ge(s_in, 2 * H * 16)
            for k in range(2):
                for o in range(K):
                    last = nc.tensor.matmul(mm[:, k * 2 * H:(k + 1) * 2 * H], turned[:, o, k * P:(k + 1) * P], diag[:, o, :],
                                            start=o == 0, stop=o == K - 1)
            last.then_inc(s_m, 1)


def local_branch(nc, g, x_dram, gat_w, a_src, a_tgt, gat_b, gain, shift, hl_dram):
    H = 4
    pr_dram = nc.dram_tensor("local_rows", (NP, H * 65 + 2 * H), F32).ap()
    agg_dram = nc.dram_tensor("local_agg", (H, 65, NP), F32).ap()
    with Phase(nc, "loc") as top:
        scores = top.sb("scores", [P, T, 2 * H])
        with Phase(nc, "locw") as ph:
            weights = ph.sb("weights", [P, 2, H * 64 + 2 * H])
            raw = ph.sb("raw", [P, 2, D])
            turned_weights(nc, "locwt", g, [(gat_w, weights)])
            load_all(nc, "locwl", [(raw[:, :, :], gat_w.rearrange("(k p) i -> p k i", p=P))])
            score_weights(nc, "locws", g, None, raw, a_src, a_tgt, H, weights)
            project(nc, "locp", g, x_dram, weights, H * 66, lambda t, out: [(pr_dram[bass.ds(t * P, P), :], out[:, :])],
                    extra=scores, ones_at=H)
        attention(nc, "gat", g, H, pr_dram, scores, agg_dram, False)
        with Phase(nc, "loco") as ph:
            h = ph.sb("h", [P, T, D])
            x = ph.sb("x", [P, T, D])
            w = ph.sb("w", [P, T, D])
            rows = ph.sb("rows", [P, 3, D])
            norm = Norm(ph, "n")
            heads_to_nodes(nc, "loch", g, H, agg_dram, h, (ALU.add, 1e-16))
            s_in, s_v, s_a, s_e, s_o, s_st = ph.sems("in", "v", "a", "e", "o", "st")
            block = ph.block()

            @block.sync
            def _(sp):
                sp.dma_start(x[:, :, :], nodes(x_dram)).then_inc(s_in, 16)
                for k, a in enumerate((gat_b, gain, shift)):
                    sp.dma_start(rows[:, k, :], row(a)).then_inc(s_in, 16)
                sp.wait_ge(s_o, 1)
                sp.dma_start(nodes(hl_dram), h[:, :, :]).then_inc(s_st, 16)
                sp.wait_ge(s_st, 16)

            @block.vector
            def _(dve):
                v = Tick(s_v, dve)
                dve.wait_ge(s_in, 64)
                v(nc.vector.tensor_tensor(h[:, :, :], h[:, :, :], x[:, :, :], ALU.add))
                v(nc.vector.tensor_tensor(h[:, :, :], h[:, :, :], rows[:, 0, :].unsqueeze(1).to_broadcast([P, T, D]), ALU.add))
                nc.vector.tensor_scalar(w[:, :, :], h[:, :, :], 0.0, None, ALU.min).then_inc(s_a, 1)
                dve.wait_ge(s_e, 1)
                v(nc.vector.tensor_scalar(h[:, :, :], h[:, :, :], 0.0, -1.0, ALU.max, ALU.add))
                v(nc.vector.tensor_tensor(h[:, :, :], h[:, :, :], w[:, :, :], ALU.add))
                norm.dve(nc, dve, v, h, rows[:, 1, :], rows[:, 2, :])
                dve.sem_inc(s_o, 1)

            @block.scalar
            def _(act):
                act.wait_ge(s_a, 1)
                nc.scalar.activation(w[:, :, :], w[:, :, :], ACT.Exp).then_inc(s_e, 1)
                norm.act(nc, act, h)


def load_all(nc, name, jobs):
    with Phase(nc, name) as ph:
        s_in = ph.sem("in")
        block = ph.block()

        @block.sync
        def _(sp):
            for to, a in jobs:
                with nc.allow_non_contiguous_dma(reason="small parameters"):
                    sp.dma_start(to, a).then_inc(s_in, 16)
            sp.wait_ge(s_in, 16 * len(jobs))


def features_first(nc, name, g, x_dram, out):
    with Phase(nc, name) as ph:
        tile = [ph.sb(f"tile{u}", [P, D]) for u in range(2)]
        tp = [ph.ps(f"tp{u}", [P, D]) for u in range(2)]
        s_in = ph.sems("in0", "in1")
        s_t, s_c = ph.sems("t", "c")
        block = ph.block()

        def turns(eng, step):
            with eng.Fori(0, T // 2, 1) as i:
                step(2 * i, i, 0)
                step(2 * i + 1, i, 1)
            step(T - 1, T // 2, 0)

        @block.sync
        def _(sp):
            def step(t, i, u):
                a = sp.snap(t * P) if not isinstance(t, int) else t * P
                need = sp.snap(t + 1) if not isinstance(t, int) else t + 1
                sp.wait_ge(s_t, need)
                sp.sem_inc(g.waited, 1)
                sp.dma_start(tile[u][:, :], x_dram[bass.ds(a, P), :]).then_inc(s_in[u], 16)
            turns(sp, step)

        @block.tensor
        def _(pe):
            pe.sem_inc(s_t, 2)
            pe.sem_inc(s_c, 1)

            def step(t, i, u):
                pe.wait_ge(s_in[u], (i + 1) * 16)
                pe.wait_ge(s_c, t)
                for k in range(2):
                    last = nc.tensor.transpose(tp[u][:, k * P:(k + 1) * P], tile[u][:, k * P:(k + 1) * P], g.ident[:, :])
                last.then_inc(s_t, 1)
            turns(pe, step)

        @block.scalar
        def _(act):
            def step(t, i, u):
                act.wait_ge(s_t, t + 3)
                nc.scalar.copy(out[:, :, bass.ds(t * P, P)], tp[u][:, :].rearrange("p (k n) -> p k n", k=2)).then_inc(s_c, 1)
            turns(act, step)


def moved_rows(nc, name, g, table, buf, scatter):
    with Phase(nc, name) as ph:
        (s_m,) = ph.pool_sems(g, 1)
        block = ph.block()

        @block.gpsimd
        def _(pool):
            for t in range(T):
                at = bass.IndirectOffsetOnAxis(ap=g.rank[:, t:t + 1], axis=0)
                if scatter:
                    pool.indirect_dma_start(table, at, buf[:, t, :], None).then_inc(s_m, 16)
                else:
                    pool.indirect_dma_start(buf[:, t, :], None, table, at).then_inc(s_m, 16)
            pool.wait_ge(s_m, 16 * T)


def banked_products(nc, ph, name, block, jobs, evict):
    mm = [ph.ps(f"{name}_mm{k}", [P, BANK]) for k in range(4)]
    s_mm, s_ev = ph.sems(f"{name}_mm", f"{name}_ev")
    todo = [(n, a, b) for n in range(len(jobs)) for a, b in BANKS]

    @block.tensor
    def _(pe):
        for q, (n, a, b) in enumerate(todo):
            if q >= 4:
                pe.wait_ge(s_ev, q - 3)
            rows, terms = jobs[n]
            for k, (w, x) in enumerate(terms):
                last = nc.tensor.matmul(mm[q % 4][0:rows, 0:b - a], w, x[:, a:b], start=k == 0, stop=k == len(terms) - 1)
            last.then_inc(s_mm, 1)

    @block.scalar
    def _(act):
        for q, (n, a, b) in enumerate(todo):
            act.wait_ge(s_mm, q + 1)
            evict(n, a, b, mm[q % 4][0:jobs[n][0], 0:b - a]).then_inc(s_ev, 1)


def mamba(nc, g, x_dram, in_w, conv_w, conv_b, x_w, dt_w, dt_b, A_log, D_par, out_w, ym_dram):
    S, R, K = 16, 16, 4
    xs_dram = nc.dram_tensor("sorted_x", (NP, D), F32).ap()
    dbc_dram = nc.dram_tensor("dbc", (R + 2 * S, NP), F32).ap()
    xc_dram = nc.dram_tensor("conv_x", (2, P, NP), F32).ap()
    z_dram = nc.dram_tensor("silu_z", (2, P, NP), F32).ap()
    with Phase(nc, "mamx") as ph:
        buf = ph.sb("buf", [P, T, D])
        load_all(nc, "mamxl", [(buf[:, :, :], nodes(x_dram))])
        moved_rows(nc, "mamxs", g, xs_dram, buf, True)
    with Phase(nc, "mam") as top:
        inT = top.sb("inT", [P, 2, 2 * D])
        xT = top.sb("xT", [P, 2, R + 2 * S])
        dtT = top.sb("dtT", [P, 1, D])
        outT = top.sb("outT", [P, 2, D])
        cw = top.sb("cw", [P, 2, K])
        cols = top.sb("cols", [P, 3, 2])
        A = top.sb("A", [P, 2, S])
        one = top.sb("one", [P, 1])
        turned_weights(nc, "mamwt", g, [(in_w, inT), (x_w, xT), (dt_w, dtT), (out_w, outT)])
        by_part = lambda a: a.rearrange("(k p) -> p k", p=P)
        load_all(nc, "mamwl", [(cw[:, :, :], conv_w.rearrange("(k p) c -> p k c", p=P)), (cols[:, 0, :], by_part(conv_b)),
                               (cols[:, 1, :], by_part(dt_b)), (cols[:, 2, :], by_part(D_par)),
                               (A[:, :, :], A_log.rearrange("(k p) s -> p k s", p=P))])
        dt = top.sb("dt", [P, 2, NP])
        u = top.sb("u", [P, 2, NP])
        with Phase(nc, "mama") as ph:
            xsT = ph.sb("xsT", [P, 2, NP])
            raw = ph.sb("raw", [P, 2, K - 1 + NP])
            features_first(nc, "mamaf", g, xs_dram, xsT)
            with Phase(nc, "mamap") as pp:
                s_z, s_st, s_v, s_e = pp.sems("z", "st", "v", "e")
                block = pp.block()

                def evict(n, a, b, psum):
                    if n < 2:
                        return nc.scalar.copy(raw[:, n, K - 1 + a:K - 1 + b], psum)
                    return nc.scalar.activation(u[:, n - 2, a:b], psum, ACT.Silu)
                banked_products(nc, pp, "mamap", block,
                                [(P, [(inT[:, k, n * P:(n + 1) * P], xsT[:, k, :]) for k in range(2)]) for n in range(4)], evict)

                @block.vector
                def _(dve):
                    nc.vector.memset(raw[:, :, 0:K - 1], 0.0)
            with Phase(nc, "mamac") as pp:
                s_st, s_v, s_c = pp.sems("st", "v", "c")
                block = pp.block()

                @block.vector
                def _(dve):
                    v = Tick(s_v, dve)
                    for k in range(2):
                        v(nc.vector.tensor_scalar(xsT[:, k, :], raw[:, k, 0:NP], cw[:, k, 0:1], None, ALU.mult))
                        for c in range(1, K):
                            ins = nc.vector.scalar_tensor_tensor(xsT[:, k, :], raw[:, k, c:c + NP], cw[:, k, c:c + 1],
                                                                 xsT[:, k, :], ALU.mult, ALU.add)
                            v(ins)
                        dve.sem_inc(s_c, 1)

                @block.scalar
                def _(act):
                    for k in range(2):
                        act.wait_ge(s_c, k + 1)
                        nc.scalar.activation(xsT[:, k, :], xsT[:, k, :], ACT.Silu, bias=cols[:, 0, k:k + 1])

                @block.sync
                def _(sp):
                    sp.dma_start(z_dram.rearrange("k p n -> p k n"), u[:, :, :]).then_inc(s_st, 16)
                    sp.wait_ge(s_st, 16)
            with Phase(nc, "mamad") as pp:
                dbc = pp.sb("dbc", [R + 2 * S, NP])
                s_st = pp.sem("st")
                with Phase(nc, "mamae") as pq:
                    s_st = pq.sem("st")
                    block = pq.block()
                    banked_products(nc, pq, "mamae", block,
                                    [(R + 2 * S, [(xT[:, k, :], xsT[:, k, :]) for k in range(2)])],
                                    lambda n, a, b, psum: nc.scalar.copy(dbc[:, a:b], psum))

                    @block.sync
                    def _(sp):
                        sp.dma_start(xc_dram.rearrange("k p n -> p k n"), xsT[:, :, :]).then_inc(s_st, 16)
                        sp.wait_ge(s_st, 16)
                with Phase(nc, "mamag") as pq:
                    s_st = pq.sem("st")
                    block = pq.block()
                    banked_products(nc, pq, "mamag", block,
                                    [(P, [(dtT[0:R, 0, n * P:(n + 1) * P], dbc[0:R, :])]) for n in range(2)],
                                    lambda n, a, b, psum: nc.scalar.activation(dt[:, n, a:b], psum, ACT.Identity, bias=cols[:, 1, n:n + 1]))

                    @block.sync
                    def _(sp):
                        sp.dma_start(dbc_dram, dbc[:, :]).then_inc(s_st, 16)
                        sp.wait_ge(s_st, 16)
            with Phase(nc, "mamas") as pp:
                s_v, s_a, s_b = pp.sems("v", "a", "b")
                block = pp.block()

                @block.scalar
                def _(act):
                    a = Tick(s_a, act)
                    a(nc.scalar.activation(u[:, :, :], dt[:, :, :], ACT.Abs))
                    a(nc.scalar.activation(u[:, :, :], u[:, :, :], ACT.Exp, scale=-1.0))
                    act.wait_ge(s_v, 1)
                    a(nc.scalar.activation(u[:, :, :], u[:, :, :], ACT.Ln, bias=one[:, 0:1]))
                    nc.scalar.activation(A[:, :, :], A[:, :, :], ACT.Exp).then_inc(s_a, 1)

                @block.vector
                def _(dve):
                    v = Tick(s_v, dve)
                    v(nc.vector.memset(one[:, :], 1.0))
                    dve.wait_ge(s_a, 4)
                    v(nc.vector.scalar_tensor_tensor(dt[:, :, :], dt[:, :, :], 0.0, u[:, :, :], ALU.max, ALU.add))
                    v(nc.vector.tensor_tensor(u[:, :, :], dt[:, :, :], xsT[:, :, :], ALU.mult))
                    v(nc.vector.tensor_scalar(A[:, :, :], A[:, :, :], -1.0, None, ALU.mult))
        with Phase(nc, "mamb") as mid:
            yT = mid.sb("yT", [P, 2, NP])
            for ct in range(2):
                with Phase(nc, f"mamb{ct}") as ph:
                    ident = g.ident
                    rowb = ph.sb("rowb", [1, 2, NP])
                    bc = [ph.sb(f"bc{k}", [P, NP]) for k in range(2)]
                    dA = ph.sb("dA", [P, NP])
                    st = ph.sb("st", [P, NP])
                    hs = ph.sb("hs", [P, NP])
                    hc = ph.sb("hc", [P, NP])
                    acc = ph.ps("acc", [P, NP])
                    s_B, s_C, s_bb, s_bC, s_dA, s_x, s_h, s_hc, s_y = ph.sems("B", "C", "bb", "bC", "dA", "x", "h", "hc", "y")
                    block = ph.block()

                    @block.sync
                    def _(sp):
                        with sp.Fori(0, S, 1) as s:
                            a = sp.snap(s + R)
                            c = sp.snap(s + (R + S))
                            need = sp.snap(s)
                            sp.wait_ge(s_bb, need)
                            sp.sem_inc(g.waited, 1)
                            sp.dma_start(rowb[0:1, 0, :], dbc_dram[bass.ds(a, 1), :]).then_inc(s_B, 16)
                            sp.wait_ge(s_bC, need)
                            sp.sem_inc(g.waited, 1)
                            sp.dma_start(rowb[0:1, 1, :], dbc_dram[bass.ds(c, 1), :]).then_inc(s_C, 16)

                    @block.gpsimd
                    def _(pool):
                        with pool.Fori(0, S, 1) as s:
                            pool.wait_ge(s_B, (s + 1) * 16)
                            pool.wait_ge(s_x, s)
                            pool.sem_inc(g.waited, 1)
                            nc.gpsimd.partition_broadcast(bc[0][:, :], rowb[0:1, 0, :]).then_inc(s_bb, 1)
                            pool.wait_ge(s_C, (s + 1) * 16)
                            pool.wait_ge(s_hc, s)
                            pool.sem_inc(g.waited, 1)
                            nc.gpsimd.partition_broadcast(bc[1][:, :], rowb[0:1, 1, :]).then_inc(s_bC, 1)

                    @block.scalar
                    def _(act):
                        with act.Fori(0, S, 1) as s:
                            act.wait_ge(s_h, s)
                            nc.scalar.activation(dA[:, :], dt[:, ct, :], ACT.Exp, scale=A[:, ct, bass.ds(s, 1)]).then_inc(s_dA, 1)
                        act.wait_ge(s_y, S)
                        for a, b in BANKS:
                            nc.scalar.copy(yT[:, ct, a:b], acc[:, a:b])

                    @block.vector
                    def _(dve):
                        with dve.Fori(0, S, 1) as s:
                            dve.wait_ge(s_bb, s + 1)
                            nc.vector.tensor_tensor(st[:, :], u[:, ct, :], bc[0][:, :], ALU.mult).then_inc(s_x, 1)
                            dve.wait_ge(s_x, s + 1)
                            dve.wait_ge(s_dA, s + 1)
                            nc.vector.tensor_tensor_scan(hs[:, :], dA[:, :], st[:, :], 0.0, ALU.mult, ALU.add).then_inc(s_h, 1)
                            dve.wait_ge(s_h, s + 1)
                            dve.wait_ge(s_bC, s + 1)
                            dve.wait_ge(s_y, s)
                            nc.vector.tensor_tensor(hc[:, :], hs[:, :], bc[1][:, :], ALU.mult).then_inc(s_hc, 1)

                    @block.tensor
                    def _(pe):
                        for a, b in BANKS:
                            nc.tensor.matmul(acc[:, a:b], g.zeros[:, 0:P], g.zeros[:, 0:b - a], start=True, stop=False)
                        with pe.Fori(0, S - 1, 1) as s:
                            pe.wait_ge(s_hc, s + 1)
                            for a, b in BANKS:
                                last = nc.tensor.matmul(acc[:, a:b], ident[:, :], hc[:, a:b], start=False, stop=False)
                            last.then_inc(s_y, 1)
                        pe.wait_ge(s_hc, S)
                        for a, b in BANKS:
                            last = nc.tensor.matmul(acc[:, a:b], ident[:, :], hc[:, a:b], start=False, stop=True)
                        last.then_inc(s_y, 1)
            with Phase(nc, "mamo") as ph:
                xc = ph.sb("xc", [P, 2, NP])
                z = u
                out = dt
                outv = out[:, :, :].rearrange("p k n -> p (k n)").rearrange("p (t d) -> p t d", d=D)
                mm = [ph.ps(f"mm{k}", [P, BANK]) for k in range(2)]
                s_in, s_v, s_r, s_m, s_e, s_st = ph.sems("in", "v", "r", "m", "e", "st")
                pairs = [range(a, min(a + 2, T)) for a in range(0, T, 2)]
                block = ph.block()

                @block.sync
                def _(sp):
                    sp.dma_start(xc[:, :, :], xc_dram.rearrange("k p n -> p k n")).then_inc(s_in, 16)
                    sp.dma_start(z[:, :, :], z_dram.rearrange("k p n -> p k n")).then_inc(s_in, 16)
                    sp.wait_ge(s_e, len(pairs))
                    sp.dma_start(nodes(ym_dram), outv).then_inc(s_st, 16)
                    sp.wait_ge(s_st, 16)

                @block.vector
                def _(dve):
                    v = Tick(s_v, dve)
                    dve.wait_ge(s_in, 32)
                    for k in range(2):
                        v(nc.vector.scalar_tensor_tensor(yT[:, k, :], xc[:, k, :], cols[:, 2, k:k + 1], yT[:, k, :], ALU.mult, ALU.add))
                        v(nc.vector.tensor_tensor(yT[:, k, :], yT[:, k, :], z[:, k, :], ALU.mult))
                    dve.sem_inc(s_r, 1)

                @block.tensor
                def _(pe):
                    pe.wait_ge(s_r, 1)
                    for q, pr in enumerate(pairs):
                        if q > 1:
                            pe.wait_ge(s_e, q - 1)
                        for n, t in enumerate(pr):
                            for k in range(2):
                                last = nc.tensor.matmul(mm[q % 2][:, n * D:(n + 1) * D], yT[:, k, t * P:(t + 1) * P], outT[:, k, :],
                                                        start=k == 0, stop=k == 1)
                        last.then_inc(s_m, 1)

                @block.scalar
                def _(act):
                    for q, pr in enumerate(pairs):
                        act.wait_ge(s_m, q + 1)
                        nc.scalar.copy(outv[:, pr[0]:pr[-1] + 1, :].rearrange("p t d -> p (t d)"), mm[q % 2][:, 0:len(pr) * D]).then_inc(s_e, 1)


def mixed_branches(nc, g, x_dram, hl_dram, ym_dram, gg, gb, wl, wg, f1w, f1b, f2w, f2b, ng, nb, x_out):
    ha_dram = nc.dram_tensor("h_attn", (NP, D), F32).ap()
    s_dram = nc.dram_tensor("h_and_ff", (NP, D), F32).ap()
    with Phase(nc, "mixa") as ph:
        y = ph.sb("y", [P, T, D])
        x = ph.sb("x", [P, T, D])
        rows = ph.sb("rows", [P, 2, D])
        moved_rows(nc, "mixag", g, ym_dram, y, False)
        norm = Norm(ph, "n")
        s_in, s_v, s_o, s_st = ph.sems("in", "v", "o", "st")
        block = ph.block()

        @block.sync
        def _(sp):
            sp.dma_start(x[:, :, :], nodes(x_dram)).then_inc(s_in, 16)
            for k, a in enumerate((gg, gb)):
                sp.dma_start(rows[:, k, :], row(a)).then_inc(s_in, 16)
            sp.wait_ge(s_o, 1)
            sp.dma_start(nodes(ha_dram), y[:, :, :]).then_inc(s_st, 16)
            sp.wait_ge(s_st, 16)

        @block.vector
        def _(dve):
            v = Tick(s_v, dve)
            dve.wait_ge(s_in, 48)
            v(nc.vector.tensor_tensor(y[:, :, :], y[:, :, :], x[:, :, :], ALU.add))
            norm.dve(nc, dve, v, y, rows[:, 0, :], rows[:, 1, :])
            dve.sem_inc(s_o, 1)

        @block.scalar
        def _(act):
            norm.act(nc, act, y)
    with Phase(nc, "mixb") as top:
        lT = top.sb("lT", [P, 2, D])
        gT = top.sb("gT", [P, 2, D])
        f1T = top.sb("f1T", [P, 2, 2 * D])
        f2T = top.sb("f2T", [P, 4, D])
        f1c = top.sb("f1c", [P, 4])
        f2r = top.sb("f2r", [P, D])
        turned_weights(nc, "mixbt", g, [(wl, lT), (wg, gT), (f1w, f1T), (f2w, f2T)])
        load_all(nc, "mixbl", [(f1c[:, :], f1b.rearrange("(c p) -> p c", p=P)), (f2r[:, :], row(f2b))])
        with Phase(nc, "mixc") as ph:
            both = [ph.sb(f"both{u}", [P, 2, D]) for u in range(2)]
            bothT = ph.sb("bothT", [P, 4, P])
            gate = ph.sb("gate", [P, D])
            dif = ph.sb("dif", [P, D])
            h = ph.sb("h", [P, D])
            hT = ph.sb("hT", [P, 2, P])
            hid = ph.sb("hid", [P, 4, P])
            res = [ph.sb(f"res{u}", [P, D]) for u in range(2)]
            tp = ph.ps("tp", [P, BANK])
            ga = ph.ps("ga", [P, D])
            tq = ph.ps("tq", [P, D])
            mh = ph.ps("mh", [P, BANK])
            mo = ph.ps("mo", [P, D])
            s_in = ph.sems("in0", "in1")
            s_st = ph.pool_sems(g, 2)
            s_t, s_tc, s_g, s_gs, s_h, s_q, s_qc, s_m, s_mr, s_o, s_r, s_v = ph.sems(
                "t", "tc", "g", "gs", "h", "q", "qc", "m", "mr", "o", "r", "v")
            block = ph.block()

            def turns(eng, step):
                with eng.Fori(0, T // 2, 1) as i:
                    step(2 * i, i, 0)
                    step(2 * i + 1, i, 1)
                step(T - 1, T // 2, 0)

            @block.sync
            def _(sp):
                def step(t, i, u):
                    a = sp.snap(t * P) if not isinstance(t, int) else t * P
                    need = sp.snap(t + 1) if not isinstance(t, int) else t + 1
                    sp.wait_ge(s_r, need)
                    sp.sem_inc(g.waited, 1)
                    sp.dma_start(both[u][:, 0, :], hl_dram[bass.ds(a, P), :]).then_inc(s_in[u], 16)
                    sp.dma_start(both[u][:, 1, :], ha_dram[bass.ds(a, P), :]).then_inc(s_in[u], 16)
                turns(sp, step)

            @block.tensor
            def _(pe):
                def step(t, i, u):
                    pe.wait_ge(s_in[u], (i + 1) * 32)
                    for c in range(4):
                        last = nc.tensor.transpose(tp[:, c * P:(c + 1) * P], both[u][:, c // 2, (c % 2) * P:(c % 2 + 1) * P], g.ident[:, :])
                    last.then_inc(s_t, 1)
                    pe.wait_ge(s_tc, t + 1)
                    for c in range(4):
                        last = nc.tensor.matmul(ga[:, :], bothT[:, c, :], (lT if c < 2 else gT)[:, c % 2, :], start=c == 0, stop=c == 3)
                    last.then_inc(s_g, 1)
                    pe.wait_ge(s_h, t + 1)
                    for k in range(2):
                        last = nc.tensor.transpose(tq[:, k * P:(k + 1) * P], h[:, k * P:(k + 1) * P], g.ident[:, :])
                    last.then_inc(s_q, 1)
                    pe.wait_ge(s_qc, t + 1)
                    for c in range(4):
                        for k in range(2):
                            last = nc.tensor.matmul(mh[:, c * P:(c + 1) * P], f1T[:, k, c * P:(c + 1) * P], hT[:, k, :], start=k == 0, stop=k == 1)
                    last.then_inc(s_m, 1)
                    pe.wait_ge(s_mr, t + 1)
                    for c in range(4):
                        last = nc.tensor.matmul(mo[:, :], hid[:, c, :], f2T[:, c, :], start=c == 0, stop=c == 3)
                    last.then_inc(s_o, 1)
                turns(pe, step)

            @block.scalar
            def _(act):
                def step(t, i, u):
                    act.wait_ge(s_t, t + 1)
                    nc.scalar.copy(bothT[:, :, :].rearrange("p c n -> p (c n)"), tp[:, :]).then_inc(s_tc, 1)
                    act.wait_ge(s_g, t + 1)
                    act.wait_ge(s_h, t)
                    nc.scalar.activation(gate[:, :], ga[:, :], ACT.Sigmoid).then_inc(s_gs, 1)
                    act.wait_ge(s_q, t + 1)
                    nc.scalar.copy(hT[:, :, :].rearrange("p c n -> p (c n)"), tq[:, :]).then_inc(s_qc, 1)
                    act.wait_ge(s_m, t + 1)
                    for c in range(4):
                        last = nc.scalar.activation(hid[:, c, :], mh[:, c * P:(c + 1) * P], ACT.Relu, bias=f1c[:, c:c + 1])
                    last.then_inc(s_mr, 1)
                turns(act, step)

            @block.vector
            def _(dve):
                v = Tick(s_v, dve)
                dve.sem_inc(s_r, 2)

                def step(t, i, u):
                    dve.wait_ge(s_in[u], (i + 1) * 32)
                    dve.wait_ge(s_qc, t)
                    v(nc.vector.tensor_tensor(dif[:, :], both[u][:, 0, :], both[u][:, 1, :], ALU.subtract))
                    dve.wait_ge(s_gs, t + 1)
                    v(nc.vector.tensor_tensor(dif[:, :], dif[:, :], gate[:, :], ALU.mult))
                    nc.vector.tensor_tensor(h[:, :], dif[:, :], both[u][:, 1, :], ALU.add).then_inc(s_h, 1)
                    dve.wait_ge(s_h, t + 1)
                    dve.wait_ge(s_st[u], i * 16)
                    v(nc.vector.tensor_tensor(res[u][:, :], h[:, :], f2r[:, :], ALU.add))
                    dve.wait_ge(s_o, t + 1)
                    nc.vector.tensor_tensor(res[u][:, :], res[u][:, :], mo[:, :], ALU.add).then_inc(s_r, 1)
                with dve.Fori(0, T // 2, 1) as i:
                    v.loop(i, 6)
                    step(2 * i, i, 0)
                    step(2 * i + 1, i, 1)
                v.end(T // 2)
                step(T - 1, T // 2, 0)

            @block.gpsimd
            def _(pool):
                def step(t, i, u):
                    pool.wait_ge(s_r, t + 3)
                    pool.dma_start(s_dram[bass.ds(t * P, P), :], res[u][:, :]).then_inc(s_st[u], 16)
                turns(pool, step)
                pool.wait_ge(s_st[0], (T - T // 2) * 16)
                pool.wait_ge(s_st[1], (T // 2) * 16)
    residual_norm(nc, "mixn", x_dram, s_dram, x_out, ng, nb)


def residual_norm(nc, name, x_dram, h_dram, x_out, gain=None, shift=None):
    with Phase(nc, name) as ph:
        h = ph.sb("h", [P, T, D])
        x = ph.sb("x", [P, T, D])
        rows = ph.sb("rows", [P, 2, D])
        inner = Norm(ph, "a")
        outer = Norm(ph, "b")
        s_in, s_v, s_o, s_st = ph.sems("in", "v", "o", "st")
        block = ph.block()
        jobs = [(x[:, :, :], nodes(x_dram)), (h[:, :, :], nodes(h_dram))]
        if gain is not None:
            jobs += [(rows[:, 0, :], row(gain)), (rows[:, 1, :], row(shift))]
        if x_out.shape[0] == NP:
            parts = [(nodes(x_out), x[:, :, :])]
        else:
            whole = N // P
            parts = [(nodes(x_out[0:whole * P, :]), x[:, 0:whole, :]), (x_out[whole * P:N, :], x[0:N - whole * P, whole, :])]

        @block.sync
        def _(sp):
            for to, a in jobs:
                sp.dma_start(to, a).then_inc(s_in, 16)
            sp.wait_ge(s_o, 1)
            for to, a in parts:
                sp.dma_start(to, a).then_inc(s_st, 16)
            sp.wait_ge(s_st, 16 * len(parts))

        @block.vector
        def _(dve):
            v = Tick(s_v, dve)
            dve.wait_ge(s_in, 16 * len(jobs))
            if gain is not None:
                inner.dve(nc, dve, v, h, rows[:, 0, :], rows[:, 1, :])
            v(nc.vector.tensor_tensor(x[:, :, :], x[:, :, :], h[:, :, :], ALU.add))
            outer.dve(nc, dve, v, x)
            dve.sem_inc(s_o, 1)

        @block.scalar
        def _(act):
            if gain is not None:
                inner.act(nc, act, h)
            outer.act(nc, act, x)


def relational_stack(nc, g, x_dram, weights, roots, biases, x_out):
    L = 3
    table = nc.dram_tensor("rel_table", (REL * NP, D), F32).ap()
    own = nc.dram_tensor("rel_own", (NP, D), F32).ap()
    hs = [nc.dram_tensor(f"rel_h{n}", (NP, D), F32).ap() for n in range(L)]
    for n in range(L):
        with Phase(nc, f"rel{n}w") as ph:
            w = ph.sb("w", [P, 2, (REL + 1) * D])
            load_all(nc, f"rel{n}l",
                     [(w[:, :, r * D:(r + 1) * D], weights[n, r].rearrange("(k p) e -> p k e", p=P)) for r in range(REL)] +
                     [(w[:, :, REL * D:], roots[n].rearrange("(k p) e -> p k e", p=P))])
            project(nc, f"rel{n}p", g, hs[n - 1] if n else x_dram, w, (REL + 1) * D,
                    lambda t, out: [(table.rearrange("(r n) d -> n r d", r=REL)[bass.ds(t * P, P), :, :],
                                     out[:, 0:REL * D].rearrange("p (r d) -> p r d", d=D)),
                                    (own[bass.ds(t * P, P), :], out[:, REL * D:])])
        gather_sum(nc, f"rel{n}s", g, table, own, biases[n], ACT.Relu if n < L - 1 else ACT.Sigmoid, hs[n])
    residual_norm(nc, "reln", x_dram, hs[L - 1], x_out)


def gather_sum(nc, name, g, table, own, bias, func, out):
    G = G_SUM
    with Phase(nc, name) as ph:
        rows = [ph.sb(f"rows{u}", [P, D]) for u in range(G)]
        at = [ph.sb(f"at{u}", [P, 1], I32) for u in range(G)]
        hot = [ph.sb(f"hot{u}", [P, P]) for u in range(G)]
        mine = ph.sb("mine", [P, D])
        bias_row = ph.sb("bias_row", [1, D])
        res = [ph.sb(f"res{u}", [P, D]) for u in range(2)]
        acc = ph.ps("acc", [P, D])
        s_in = ph.pool_sems(g, G)
        s_at, s_hot, s_used, s_sum, s_own, s_mine, s_bias, s_res, s_st = ph.sems(
            "at", "hot", "used", "sum", "own", "mine", "bias", "res", "st")
        block = ph.block()

        @block.vector
        def _(dve):
            with dve.Fori(0, T, 1) as t:
                first, count, before = span_of(dve, g, t, G)
                with dve.Fori(0, count, 1) as j:
                    c0 = step_start(nc, first + j * G)
                    for u in range(G):
                        dve.wait_ge(s_in[u], (before + j) * 16)
                        nc.vector.tensor_copy(at[u][:, :], g.rows[:, bass.ds(c0 + u, 1)]).then_inc(s_at, 1)
                        dve.wait_ge(s_used, (before + j) * G + (u + 1))
                        nc.vector.tensor_scalar(hot[u][:, :], g.numbers[:, bass.ds(t * P, P)],
                                                g.dsts[:, bass.ds(c0 + u, 1)], None, ALU.is_equal).then_inc(s_hot, 1)

        @block.gpsimd
        def _(pool):
            with pool.Fori(0, T, 1) as t:
                first, count, before = span_of(pool, g, t, G)
                with pool.Fori(0, count, 1) as j:
                    for u in range(G):
                        pool.wait_ge(s_at, (before + j) * G + (u + 1))
                        pool.wait_ge(s_used, (before + j) * G + (u + 1))
                        pool.sem_inc(g.waited, 1)
                        pool.indirect_dma_start(rows[u][:, :], None, table,
                                                bass.IndirectOffsetOnAxis(ap=at[u][:, 0:1], axis=0)).then_inc(s_in[u], 16)

        @block.tensor
        def _(pe):
            pe.sem_inc(s_used, G)
            pe.wait_ge(s_bias, 16)
            with pe.Fori(0, T, 1) as t:
                first, count, before = span_of(pe, g, t, G)
                pe.wait_ge(s_own, (t + 1) * 16)
                pe.wait_ge(s_res, t)
                nc.tensor.matmul(acc[:, :], g.ident[:, :], mine[:, :], start=True, stop=False).then_inc(s_mine, 1)
                with pe.Fori(0, count, 1) as j:
                    for u in range(G):
                        pe.wait_ge(s_hot, (before + j) * G + (u + 1))
                        pe.wait_ge(s_in[u], (before + j) * 16 + 16)
                        nc.tensor.matmul(acc[:, :], hot[u][:, :], rows[u][:, :], start=False, stop=False).then_inc(s_used, 1)
                nc.tensor.matmul(acc[:, :], g.ones[0:1, :], bias_row[0:1, :], start=False, stop=True).then_inc(s_sum, 1)

        @block.scalar
        def _(act):
            def step(t, i, u):
                act.wait_ge(s_sum, t + 1)
                act.wait_ge(s_st, t * 16)
                nc.scalar.activation(res[u][:, :], acc[:, :], func).then_inc(s_res, 1)
            with act.Fori(0, T // 2, 1) as i:
                step(2 * i, i, 0)
                step(2 * i + 1, i, 1)
            step(T - 1, T // 2, 0)

        @block.sync
        def _(sp):
            sp.dma_start(bias_row[:, :], bias.rearrange("(o n) -> o n", o=1)).then_inc(s_bias, 16)
            sp.dma_start(mine[:, :], own[0:P, :]).then_inc(s_own, 16)

            def step(t, i, u, more):
                a = sp.snap(t * P) if not isinstance(t, int) else t * P
                b = sp.snap((t + 1) * P) if not isinstance(t, int) else 0
                need = sp.snap(t + 1) if not isinstance(t, int) else t + 1
                if more:
                    sp.wait_ge(s_mine, need)
                    sp.sem_inc(g.waited, 1)
                    sp.dma_start(mine[:, :], own[bass.ds(b, P), :]).then_inc(s_own, 16)
                sp.wait_ge(s_res, need)
                sp.sem_inc(g.waited, 1)
                sp.dma_start(out[bass.ds(a, P), :], res[u][:, :]).then_inc(s_st, 16)
            with sp.Fori(0, T // 2, 1) as i:
                step(2 * i, i, 0, True)
                step(2 * i + 1, i, 1, True)
            step(T - 1, T // 2, 0, False)
            sp.wait_ge(s_st, 16 * T)


def last_attention(nc, g, x_dram, W, a_l, a_r, bias, lin_w, lin_b, out):
    H = 2
    F = H * 64
    pr_dram = nc.dram_tensor("last_rows", (NP, H * 65 + 2 * H), F32).ap()
    agg_dram = nc.dram_tensor("last_agg", (H, 65, NP), F32).ap()
    h_dram = nc.dram_tensor("last_h", (NP, D), F32).ap()
    with Phase(nc, "las") as top:
        scores = top.sb("scores", [P, T, 2 * H])
        with Phase(nc, "lasw") as ph:
            weights = ph.sb("weights", [P, 2, F + 2 * H])
            WT = ph.sb("WT", [P, 1, D])
            load_all(nc, "laswl", [(weights[:, :, 0:F], W.rearrange("(k p) n -> p k n", p=P))])
            turned_weights(nc, "laswt", g, [(W, WT)])
            score_weights(nc, "lasws", g, None, WT, a_l, a_r, H, weights)
            project(nc, "lasp", g, x_dram, weights, F + 2 * H, lambda t, out: [(pr_dram[bass.ds(t * P, P), :], out[:, :])],
                    extra=scores, ones_at=H)
        attention(nc, "lat", g, H, pr_dram, scores, agg_dram, True)
        with Phase(nc, "laso") as ph:
            h = ph.sb("h", [P, T, F])
            o = ph.sb("o", [P, T, D])
            lw = ph.sb("lw", [P, D])
            br = ph.sb("br", [P, F])
            lr = ph.sb("lr", [P, D])
            turned = [ph.sb(f"turned{u}", [P, 2 * P]) for u in range(2)]
            heads_to_nodes(nc, "lash", g, H, agg_dram, h, (ALU.max, 1e-30))
            tp = [ph.ps(f"tp{u}", [P, BANK]) for u in range(2)]
            mm = [ph.ps(f"mm{u}", [P, BANK]) for u in range(2)]
            s_in, s_v, s_a, s_t, s_c, s_m, s_r, s_o, s_st = ph.sems("in", "v", "a", "t", "c", "m", "r", "o", "st")
            pairs = [range(a, min(a + 2, T)) for a in range(0, T, 2)]
            block = ph.block()

            @block.sync
            def _(sp):
                for to, a in ((lw[:, :], lin_w), (br[:, :], row(bias)), (lr[:, :], row(lin_b))):
                    sp.dma_start(to, a).then_inc(s_in, 16)
                sp.wait_ge(s_o, 1)
                sp.dma_start(nodes(h_dram), o[:, :, :]).then_inc(s_st, 16)
                sp.wait_ge(s_st, 16)

            @block.tensor
            def _(pe):
                pe.wait_ge(s_a, 1)
                for k, pr in enumerate(pairs):
                    if k > 1:
                        pe.wait_ge(s_c, k - 1)
                    for n, t in enumerate(pr):
                        last = nc.tensor.transpose(tp[k % 2][:, n * P:(n + 1) * P], h[:, t, :], g.ident[:, :])
                    last.then_inc(s_t, 1)
                    pe.wait_ge(s_c, k + 1)
                    if k > 1:
                        pe.wait_ge(s_r, k - 1)
                    for n, t in enumerate(pr):
                        last = nc.tensor.matmul(mm[k % 2][:, n * D:(n + 1) * D], turned[k % 2][:, n * P:(n + 1) * P], lw[:, :],
                                                start=True, stop=True)
                    last.then_inc(s_m, 1)

            @block.scalar
            def _(act):
                for k, pr in enumerate(pairs):
                    act.wait_ge(s_t, k + 1)
                    nc.scalar.copy(turned[k % 2][:, 0:len(pr) * P], tp[k % 2][:, 0:len(pr) * P]).then_inc(s_c, 1)

            @block.vector
            def _(dve):
                v = Tick(s_v, dve)
                dve.wait_ge(s_in, 48)
                v(nc.vector.tensor_tensor(h[:, :, :], h[:, :, :], br[:, :].unsqueeze(1).to_broadcast([P, T, F]), ALU.add))
                nc.vector.tensor_scalar(h[:, :, :], h[:, :, :], 0.0, None, ALU.max).then_inc(s_a, 1)
                for k, pr in enumerate(pairs):
                    dve.wait_ge(s_m, k + 1)
                    nc.vector.tensor_tensor(o[:, pr[0]:pr[-1] + 1, :],
                                            mm[k % 2][:, 0:len(pr) * D].rearrange("p (t d) -> p t d", d=D),
                                            lr[:, :].unsqueeze(1).to_broadcast([P, len(pr), D]), ALU.add).then_inc(s_r, 1)
                dve.wait_ge(s_r, len(pairs))
                v(nc.vector.tensor_scalar(o[:, :, :], o[:, :, :], 0.0, None, ALU.max))
                dve.sem_inc(s_o, 1)
    residual_norm(nc, "lasn", x_dram, h_dram, out)


def program(nc, x, src, dst, kind, noise, gcn, local, ssm, mix, rel, last, out):
    ctx = ExitStack()
    with ctx:
        g = Shared()

        def sb(name, shape, dt=F32):
            return ctx.enter_context(nc.sbuf_tensor(f"g_{name}", shape, dt))

        def dram(name, shape, dt=F32):
            return nc.dram_tensor(name, shape, dt).ap()

        g.ident = sb("ident", [P, P])
        g.ones = sb("ones", [P, P])
        g.zeros = sb("zeros", [P, BANK], BF16)
        g.numbers = sb("numbers", [P, NP], F16)
        g.srcs = sb("srcs", [P, CT * P])
        g.dsts = sb("dsts", [P, CT * P])
        g.rows = sb("rows", [P, CT * P], I32)
        g.spans = sb("spans", [1, 1 + 2 * len(SPANS), 32], I32)
        g.indeg = sb("indeg", [P, T])
        g.dinv = sb("dinv", [P, T])
        g.rank = sb("rank", [P, T], I32)
        g.adj = dram("adj", (NP, NP))
        g.absent = dram("absent", (NP, NP), BF16)
        xs = [dram(f"x{n}", (NP, D)) for n in range(4)]
        hl, ym = dram("h_local", (NP, D)), dram("y_sorted", (NP, D))
        g.waited = ctx.enter_context(nc.semaphore("waited"))
        g.pool_sems = [ctx.enter_context(nc.semaphore(f"pool_dma{n}")) for n in range(36)]

        def clear():
            free = nc.free_semaphores
            nc.all_engine_barrier(sems_to_clear=range(min(free), max(free) + 1))

        def stage(f, *args):
            f(nc, g, *args)
            clear()

        def graph(nc, g):
            constants(nc, g)
            edge_tables(nc, g, src, dst, kind)
            with Phase(nc, "deg") as ph:
                g.outdeg = ph.sb("outdeg", [P, NP])
                adjacency(nc, g)
                ranking.keys(g.outdeg)

        with Phase(nc, "rank") as ph:
            ranking = Ranking(nc, g, ph, noise)
            graph(nc, g)
            load_x(nc, g, x, xs[0])
            gcn_stack(nc, g, xs[0], ranking, *gcn, xs[1])
        clear()
        stage(local_branch, xs[1], *local, hl)
        stage(mamba, xs[1], *ssm, ym)
        stage(mixed_branches, xs[1], hl, ym, *mix, xs[2])
        stage(relational_stack, xs[2], *rel, xs[3])
        last_attention(nc, g, xs[3], *last, out)

_FIRST = ['x', 'src', 'dst', 'edge_type_8', 'node_vec']
_GCN = ['L0_gnn_W1', 'L0_gnn_b1', 'L0_gnn_W2', 'L0_gnn_b2', 'L0_gnn_W3', 'L0_gnn_b3', 'L0_gnn_W4', 'L0_gnn_b4']
_LOCAL = ['L1_gnn_gat_w', 'L1_gnn_gat_a_src', 'L1_gnn_gat_a_tgt', 'L1_gnn_gat_b', 'L1_gnn_ln_local_g', 'L1_gnn_ln_local_b']
_SSM = ['L1_gnn_in_proj_w', 'L1_gnn_conv_w', 'L1_gnn_conv_b', 'L1_gnn_x_proj_w', 'L1_gnn_dt_proj_w', 'L1_gnn_dt_proj_b', 'L1_gnn_A_log', 'L1_gnn_D_param', 'L1_gnn_out_proj_w']
_MIX = ['L1_gnn_ln_global_g', 'L1_gnn_ln_global_b', 'L1_gnn_wl', 'L1_gnn_wg', 'L1_gnn_ff1_w', 'L1_gnn_ff1_b', 'L1_gnn_ff2_w', 'L1_gnn_ff2_b', 'L1_gnn_ln2_g', 'L1_gnn_ln2_b']
_REL = ['L2_gnn_weights', 'L2_gnn_roots', 'L2_gnn_biases']
_LAST = ['L3_gnn_W', 'L3_gnn_attn_l', 'L3_gnn_attn_r', 'L3_gnn_gat_bias', 'L3_gnn_lin_W', 'L3_gnn_lin_b']


def kernel(**inputs):
    import numpy as _np
    import concourse.bacc as _bacc
    from concourse import mybir as _mybir
    from concourse.bass_utils import run_bass_kernel_spmd as _run

    nc = _bacc.Bacc("TRN2", target_bir_lowering=False, num_devices=1)
    arrays = {}

    def given(names):
        aps = []
        for name in names:
            a = _np.ascontiguousarray(inputs[name])
            arrays[f"in_{name}"] = a
            aps.append(nc.dram_tensor(f"in_{name}", a.shape, _mybir.dt.from_np(a.dtype), kind="ExternalInput").ap())
        return aps

    first = given(_FIRST)
    rest = [given(names) for names in (_GCN, _LOCAL, _SSM, _MIX, _REL, _LAST)]
    out = nc.dram_tensor("out", (N, D), F32, kind="ExternalOutput").ap()
    program(nc, *first, *rest, out)
    r = _run(nc, [arrays], core_ids=[0])
    return r.results[0]["out"]
```

```python
from contextlib import ExitStack

import concourse.bass as bass
from concourse import mybir

F32, BF16, F16, I32 = mybir.dt.float32, mybir.dt.bfloat16, mybir.dt.float16, mybir.dt.int32
ALU, ACT, AX = mybir.AluOpType, mybir.ActivationFunctionType, mybir.AxisListType

P = 128
N = 3125
D = 256
T = -(-N // P)
NP = T * P
E = 100000
C = -(-E // P)
CT = -(-C // P)
G_ADJ, G_SUM = 4, 6
SPANS = [G_ADJ, G_SUM]
PAD = NP - 1
HALF = NP // 2
REL = 8
BANK = 512
BANKS = [(b, min(b + BANK, NP)) for b in range(0, NP, BANK)]
NEG = -2.0 ** 100
EPS = 1e-5
J = 400
NJ = NP // J


class Shared:
    pass


class Tick:

    def __init__(self, sem, eng=None):
        self.sem, self.eng, self.n, self.i, self.per, self.base = sem, eng, 0, None, 0, 0

    def loop(self, i, per):
        self.base, self.n, self.i, self.per = self.n, 0, i, per

    def end(self, turns):
        assert self.n == self.per, (self.n, self.per)
        self.n, self.i = self.base + turns * self.per, None

    def value(self):
        return self.n if self.i is None else self.i * self.per + (self.base + self.n)

    def __call__(self, ins):
        ins.then_inc(self.sem, 1)
        self.n += 1
        self.eng.wait_ge(self.sem, self.value())


class Phase:

    def __init__(self, nc, name):
        self.nc, self.name, self.ctx = nc, name, ExitStack()

    def __enter__(self):
        self.ctx.__enter__()
        return self

    def __exit__(self, *e):
        return self.ctx.__exit__(*e)

    def sb(self, name, shape, dt=F32):
        return self.ctx.enter_context(self.nc.sbuf_tensor(f"{self.name}_{name}", shape, dt))

    def ps(self, name, shape, dt=F32):
        return self.ctx.enter_context(self.nc.psum_tensor(f"{self.name}_{name}", shape, dt))

    def sem(self, name):
        return self.ctx.enter_context(self.nc.semaphore(f"{self.name}_{name}"))

    def sems(self, *names):
        return [self.sem(n) for n in names]

    def pool_sems(self, g, n):
        return [g.pool_sems.pop(0) for _ in range(n)]

    def block(self):
        return self.ctx.enter_context(self.nc.Block())


def constants(nc, g):
    with Phase(nc, "const") as ph:
        s_fill, s_sel = ph.sems("fill", "sel")
        num = ph.sb("num", [P, NP], I32)
        s_iota, s_cast = ph.sems("iota", "cast")
        block = ph.block()

        @block.gpsimd
        def _(pool):
            nc.gpsimd.memset(g.ident[:, :], 1.0).then_inc(s_fill, 1)
            nc.gpsimd.memset(g.ones[:, :], 1.0)
            nc.gpsimd.memset(g.zeros[:, :], 0.0)
            pool.wait_ge(s_fill, 1)
            nc.gpsimd.affine_select(out=g.ident[:, :], in_=g.ident[:, :], compare_op=ALU.is_equal, fill=0.0,
                                    base=0, pattern=[[-1, P]], channel_multiplier=1).then_inc(s_sel, 1)
            pool.wait_ge(s_sel, 1)
            nc.gpsimd.tensor_copy(g.ident16[:, :], g.ident[:, :])
            nc.gpsimd.iota(num[:, :], [[1, NP]], base=-HALF, channel_multiplier=0).then_inc(s_iota, 1)

        @block.vector
        def _(dve):
            dve.wait_ge(s_iota, 1)
            nc.vector.tensor_copy(g.numbers[:, :], num[:, :]).then_inc(s_cast, 1)


def edge_tables(nc, g, src, dst, kind):
    full = E // P
    tail = E - full * P
    R = CT - 1
    with Phase(nc, "edge") as ph:
        raw = ph.sb("raw", [P, 3, CT, P], I32)
        val = ph.sb("val", [P, 3, CT, P])
        node = ph.sb("node", [P, CT, P])
        ends = ph.sb("ends", [P, 2 * CT])
        endsT = ph.sb("endsT", [2 * CT, P])
        row = ph.sb("row", [32, 2, CT * P])
        cnum = ph.sb("cnum", [32, C])
        cnumi = ph.sb("cnumi", [32, C], I32)
        hit = ph.sb("hit", [32, C])
        low = ph.sb("low", [32, C])
        tmp = ph.sb("tmp", [32, C])
        edge0 = ph.sb("edge0", [32, 2])
        edge0i = ph.sb("edge0i", [32, 2], I32)
        span = ph.sb("span", [32, 2])
        steps = ph.sb("steps", [32, 1 + len(SPANS)])
        flat = ph.sb("flat", [1, 2 + 2 * len(SPANS), 32])
        psum = [ph.ps(f"t{k}", [P, CT * P]) for k in range(3)]
        pend = ph.ps("pend", [2 * CT, P])
        dram_ends = nc.dram_tensor("ends_rows", (2, CT * P), F32).ap()
        dram_span = nc.dram_tensor("span_rows", (1 + len(SPANS), 32), F32).ap()
        s_fill, s_in, s_val, s_end, s_T, s_Tc, s_st, s_row, s_v, s_io, s_sp, s_fl = ph.sems(
            "fill", "in", "val", "end", "T", "Tc", "st", "row", "v", "io", "sp", "fl")
        block = ph.block()

        @block.gpsimd
        def _(pool):
            nc.gpsimd.memset(raw[:, :, R, :], PAD).then_inc(s_fill, 1)
            nc.gpsimd.iota(cnumi[:, :], [[1, C]], base=0, channel_multiplier=0).then_inc(s_io, 1)
            nc.gpsimd.iota(edge0i[:, :], [[P, 2]], base=0, channel_multiplier=P).then_inc(s_io, 1)

        @block.sync
        def _(sp):
            sp.wait_ge(s_fill, 1)
            for k, a in enumerate((src, dst, kind)):
                sp.dma_start(raw[:, k, 0:R, :], a[0:R * P * P].rearrange("(r c e) -> c r e", c=P, e=P)).then_inc(s_in, 16)
                sp.dma_start(raw[0:full - R * P, k, R, :],
                             a[R * P * P:full * P].rearrange("(c e) -> c e", e=P)).then_inc(s_in, 16)
                sp.dma_start(raw[full - R * P:full - R * P + 1, k, R, 0:tail],
                             a[full * P:E].rearrange("(c e) -> c e", c=1)).then_inc(s_in, 16)
            sp.wait_ge(s_Tc, 1)
            sp.dma_start(dram_ends.rearrange("k (r p) -> (k r) p", p=P), endsT[:, :]).then_inc(s_st, 16)
            sp.wait_ge(s_st, 16)
            sp.dma_start(row[:, :, :].rearrange("p k n -> p (k n)"),
                         dram_ends.rearrange("k n -> (k n)").partition_broadcast(32)).then_inc(s_row, 16)
            sp.wait_ge(s_sp, 1)
            with nc.allow_non_contiguous_dma(reason="96 numbers"):
                sp.dma_start(dram_span.rearrange("k t -> t k"), steps[:, :]).then_inc(s_st, 16)
            sp.wait_ge(s_st, 32)
            sp.dma_start(flat[:, 0:1 + len(SPANS), :].rearrange("o k t -> o (k t)"),
                         dram_span.rearrange("k t -> (k t)").rearrange("(o n) -> o n", o=1)).then_inc(s_fl, 16)

        @block.tensor
        def _(pe):
            pe.wait_ge(s_val, 1)
            for k, a in enumerate((val[:, 0], val[:, 1], node[:, :, :])):
                for r in range(CT):
                    last = nc.tensor.transpose(psum[k][:, r * P:(r + 1) * P], a[:, r, :], g.ident[:, :])
            last.then_inc(s_T, 1)
            pe.wait_ge(s_end, 1)
            nc.tensor.transpose(pend[:, :], ends[:, :], g.ident[:, :]).then_inc(s_T, 1)

        @block.vector
        def _(dve):
            v = Tick(s_v, dve)
            dve.wait_ge(s_in, 9 * 16)
            v(nc.vector.tensor_copy(val[:, :, :, :], raw[:, :, :, :]))
            v(nc.vector.tensor_scalar(node[:, R, :], val[:, 2, R, :], float(REL - 1), None, ALU.min))
            v(nc.vector.tensor_copy(val[:, 2, R, :], node[:, R, :]))
            nc.vector.scalar_tensor_tensor(node[:, :, :], val[:, 2], float(NP), val[:, 0], ALU.mult, ALU.add).then_inc(s_val, 1)
            v(nc.vector.tensor_reduce(ends[:, 0:CT], val[:, 1], AX.X, ALU.min))
            nc.vector.tensor_reduce(ends[:, CT:], val[:, 1], AX.X, ALU.max).then_inc(s_end, 1)
            dve.wait_ge(s_T, 1)
            nc.vector.tensor_scalar(g.srcs[:, :], psum[0][:, :], -float(HALF), None, ALU.add)
            nc.vector.tensor_scalar(g.dsts[:, :], psum[1][:, :], -float(HALF), None, ALU.add)
            nc.vector.tensor_copy(g.rows[:, :], psum[2][:, :])
            dve.wait_ge(s_T, 2)
            nc.vector.tensor_copy(endsT[:, :], pend[:, :]).then_inc(s_Tc, 1)
            dve.wait_ge(s_io, 2)
            nc.vector.tensor_copy(cnum[:, :], cnumi[:, :])
            v(nc.vector.tensor_copy(edge0[:, :], edge0i[:, :]))
            dve.wait_ge(s_row, 16)
            v(nc.vector.tensor_scalar(tmp[:, :], row[:, 0, 0:C], edge0[:, 1:2], None, ALU.is_lt))
            v(nc.vector.scalar_tensor_tensor(hit[:, :], row[:, 1, 0:C], edge0[:, 0:1], tmp[:, :], ALU.is_ge, ALU.mult))
            v(nc.vector.scalar_tensor_tensor(low[:, :], hit[:, :], -1e6, cnum[:, :], ALU.mult, ALU.add))
            v(nc.vector.tensor_scalar(low[:, :], low[:, :], 1e6, float(C - 1), ALU.add, ALU.min))
            v(nc.vector.scalar_tensor_tensor(tmp[:, :], cnum[:, :], 1.0, hit[:, :], ALU.add, ALU.mult))
            v(nc.vector.tensor_reduce(span[:, 0:1], low[:, :], AX.X, ALU.min))
            v(nc.vector.tensor_reduce(span[:, 1:2], tmp[:, :], AX.X, ALU.max))
            v(nc.vector.tensor_tensor(span[:, 1:2], span[:, 1:2], span[:, 0:1], ALU.subtract))
            v(nc.vector.tensor_scalar(span[:, 1:2], span[:, 1:2], 1.0, None, ALU.max))
            v(nc.vector.tensor_copy(steps[:, 0:1], span[:, 0:1]))
            for k, size in enumerate(SPANS):
                v(nc.vector.tensor_scalar(tmp[:, :], cnum[:, :], float(size), span[:, 1:2], ALU.mult, ALU.is_lt))
                v(nc.vector.tensor_reduce(steps[:, 1 + k:2 + k], tmp[:, :], AX.X, ALU.add))
                if size == G_SUM:
                    v(nc.vector.tensor_scalar(steps[:, 1 + k:2 + k], steps[:, 1 + k:2 + k], 2.0, None, ALU.max))
            dve.sem_inc(s_sp, 1)
            dve.wait_ge(s_fl, 16)
            K = len(SPANS)
            v(nc.vector.memset(flat[:, 1 + 2 * K, :], 1.0))
            for k in range(K):
                v(nc.vector.tensor_tensor_scan(flat[:, 1 + K + k, :], flat[:, 1 + 2 * K, :], flat[:, 1 + k, :], 0.0,
                                               ALU.mult, ALU.add))
                v(nc.vector.tensor_tensor(flat[:, 1 + K + k, :], flat[:, 1 + K + k, :], flat[:, 1 + k, :], ALU.subtract))
            nc.vector.tensor_copy(g.spans[:, :, :], flat[:, 0:1 + 2 * K, :])


def span_of(eng, g, t, size):
    k, K = SPANS.index(size), len(SPANS)
    most = -(-C // size)
    first = eng.value_load(g.spans[0:1, 0, bass.ds(t, 1)], min_val=0, max_val=C - 1)
    count = eng.value_load(g.spans[0:1, 1 + k, bass.ds(t, 1)], min_val=2 if size == G_SUM else 1, max_val=most)
    before = eng.value_load(g.spans[0:1, 1 + K + k, bass.ds(t, 1)], min_val=0, max_val=T * most)
    return first, count, before


def step_start(nc, chunk):
    return nc.s_assert_within(chunk, 0, C - 1 + G_SUM, skip_runtime_bounds_check_because="spans end at C")


def adjacency(nc, g):
    G = G_ADJ
    NB = len(BANKS)
    with Phase(nc, "adj") as ph:
        to = ph.sb("to", [P, 4, P], BF16)
        frm = ph.sb("frm", [P, 4, NP], BF16)
        counts = ph.sb("counts", [P, NP])
        miss = ph.sb("miss", [P, NP], BF16)
        junk = ph.sb("junk", [P, NP], BF16)
        outsum = ph.sb("outsum", [P, NP])
        turned = ph.sb("turned", [P, NP])
        acc = ph.ps("acc", [P, NP])
        s_hot, s_used, s_sum, s_copied, s_masked, s_miss, s_adj, s_tp, s_tpc, s_bc = ph.sems(
            "hot", "used", "sum", "copied", "masked", "miss", "adjst", "tp", "tpc", "bc")
        s_v = ph.sem("v")
        s_in = ph.sem("indeg")
        high = ph.sb("high", [P, NP], BF16)
        low = ph.sb("low", [P, NP], BF16)
        most = ph.sb("most", [P, 1])
        s_high, s_low, s_highst, s_lowst, s_w = ph.sems("high", "low", "highst", "lowst", "w")
        block = ph.block()

        @block.vector
        def _(dve):
            with dve.Fori(0, T, 1) as t:
                first, count, before = span_of(dve, g, t, G)
                with dve.Fori(0, count, 1) as j:
                    c0 = step_start(nc, first + j * G)
                    for u in range(G):
                        dve.wait_ge(s_used, (before + j) * G + (u + 1))
                        nc.vector.tensor_scalar(to[:, u, :], g.numbers[:, bass.ds(t * P, P)],
                                                g.dsts[:, bass.ds(c0 + u, 1)], None, ALU.is_equal)
                        nc.vector.tensor_scalar(frm[:, u, :], g.numbers[:, :],
                                                g.srcs[:, bass.ds(c0 + u, 1)], None, ALU.is_equal).then_inc(s_hot, 1)
                dve.wait_ge(s_copied, (t + 1) * NB)
                dve.wait_ge(s_miss, t * 16)
                nc.vector.tensor_scalar(miss[:, :], counts[:, :], 0.0, NEG, ALU.is_equal, ALU.mult).then_inc(s_masked, 1)
            dve.wait_ge(s_bc, 1)
            w = Tick(s_w, dve)
            w(nc.vector.tensor_copy(g.outdeg[:, :], acc[:, :]))
            w(nc.vector.tensor_reduce(most[:, :], g.outdeg[:, :], AX.X, ALU.max))
            w(nc.vector.tensor_scalar(most[:, :], most[:, :], 256.0, 1.0, ALU.is_gt, ALU.add))
            nc.vector.tensor_scalar(g.strips_before[:, :], g.numbers[0:1, 0:32], float(HALF), most[0:1, 0:1], ALU.add, ALU.mult)

        @block.gpsimd
        def _(pool):
            nc.gpsimd.memset(outsum[:, :], 0.0).then_inc(s_v, 1)
            with pool.Fori(0, T, 1) as t:
                pool.wait_ge(s_copied, (t + 1) * NB)
                pool.wait_ge(s_v, t + 1)
                nc.gpsimd.tensor_tensor(outsum[:, :], outsum[:, :], counts[:, :], ALU.add).then_inc(s_v, 1)
                pool.wait_ge(s_tpc, (t + 2) * NB)
                pool.wait_ge(s_highst, t * 16)
                pool.sem_inc(g.waited, 1)
                nc.gpsimd.tensor_copy(high[:, :], turned[:, :]).then_inc(s_high, 1)
                pool.wait_ge(s_lowst, t * 16)
                pool.wait_ge(s_high, t + 1)
                nc.gpsimd.tensor_tensor(low[:, :], turned[:, :], high[:, :], ALU.subtract).then_inc(s_low, 1)

        @block.tensor
        def _(pe):
            pe.sem_inc(s_used, 4)
            pe.sem_inc(s_tpc, NB)
            with pe.Fori(0, T, 1) as t:
                first, count, before = span_of(pe, g, t, G)
                for n, (a, b) in enumerate(BANKS):
                    pe.wait_ge(s_tpc, t * NB + (n + 1))
                    nc.tensor.matmul(acc[:, a:b], g.zeros[:, 0:P], g.zeros[:, 0:b - a], start=True, stop=False)
                with pe.Fori(0, count, 1) as j:
                    for u in range(G):
                        pe.wait_ge(s_hot, (before + j) * G + (u + 1))
                        for a, b in BANKS:
                            last = nc.tensor.matmul(acc[:, a:b], to[:, u, :], frm[:, u, a:b], start=False, stop=False)
                        last.then_inc(s_used, 1)
                for a, b in BANKS:
                    nc.tensor.matmul(acc[:, a:b], g.zeros[:, 0:P], g.zeros[:, 0:b - a], start=False, stop=True).then_inc(s_sum, 1)
                for n, (a, b) in enumerate(BANKS):
                    pe.wait_ge(s_copied, t * NB + (n + 1))
                    for c in range(a, b, P):
                        last = nc.tensor.transpose(acc[:, c:c + P], counts[:, c:c + P], g.ident[:, :])
                    last.then_inc(s_tp, 1)
            pe.wait_ge(s_v, T + 1)
            pe.wait_ge(s_tpc, (T + 1) * NB)
            for a, b in BANKS:
                last = nc.tensor.matmul(acc[:, a:b], g.ones[:, :], outsum[:, a:b], start=True, stop=True)
            last.then_inc(s_bc, 1)

        @block.scalar
        def _(act):
            with act.Fori(0, T, 1) as t:
                act.wait_ge(s_v, t + 1)
                act.wait_ge(s_masked, t)
                act.wait_ge(s_in, t)
                for n, (a, b) in enumerate(BANKS):
                    act.wait_ge(s_sum, t * NB + (n + 1))
                    nc.scalar.copy(counts[:, a:b], acc[:, a:b]).then_inc(s_copied, 1)
                act.wait_ge(s_adj, t * 16)
                act.wait_ge(s_low, t)
                for n, (a, b) in enumerate(BANKS):
                    act.wait_ge(s_tp, t * NB + (n + 1))
                    nc.scalar.copy(turned[:, a:b], acc[:, a:b]).then_inc(s_tpc, 1)
                act.wait_ge(s_copied, (t + 1) * NB)
                nc.scalar.activation(junk[:, :], counts[:, :], ACT.Copy, accum_out=g.indeg[:, bass.ds(t, 1)]).then_inc(s_in, 1)

        @block.sync
        def _(sp):
            with sp.Fori(0, T, 1) as t:
                a = sp.snap(t * P)
                masked, turned_ = sp.snap(t + 1), sp.snap((t + 2) * NB)
                sp.wait_ge(s_tpc, turned_)
                sp.sem_inc(g.waited, 1)
                sp.dma_start(g.adj[:, bass.ds(a, P)].rearrange("(s p) d -> p s d", p=P),
                             turned[:, :].rearrange("p (s d) -> p s d", d=P)).then_inc(s_adj, 16)
                sp.wait_ge(s_masked, masked)
                sp.sem_inc(g.waited, 1)
                sp.dma_start(g.absent[bass.ds(a, P), :], miss[:, :]).then_inc(s_miss, 16)
                below = sp.snap(t * P + NP)
                sp.wait_ge(s_high, masked)
                sp.sem_inc(g.waited, 1)
                sp.dma_start(g.strips[bass.ds(a, P), :], high[:, :]).then_inc(s_highst, 16)
                sp.wait_ge(s_low, masked)
                sp.sem_inc(g.waited, 1)
                sp.dma_start(g.strips[bass.ds(below, P), :], low[:, :]).then_inc(s_lowst, 16)
            sp.wait_ge(s_highst, T * 16)
            sp.wait_ge(s_lowst, T * 16)
            sp.wait_ge(s_miss, T * 16)
            sp.wait_ge(s_adj, T * 16)


def turned_weights(nc, name, g, jobs):
    blocks = []
    for n, (w, out) in enumerate(jobs):
        O, I = w.shape
        for o in range(0, O, P):
            for k in range(0, I, P):
                blocks.append((n, o, min(P, O - o), k, min(P, I - k)))
    with Phase(nc, name) as ph:
        raw = [ph.sb(f"raw{n}", [min(P, w.shape[0]), -(-w.shape[0] // P), w.shape[1]]) for n, (w, _) in enumerate(jobs)]
        tp = [ph.ps(f"tp{k}", [P, P]) for k in range(4)]
        s_in, s_t, s_c = ph.sems("in", "t", "c")
        block = ph.block()

        @block.sync
        def _(sp):
            for (w, _), r in zip(jobs, raw):
                sp.dma_start(r[:, :, :], w.rearrange("(a p) i -> p a i", p=min(P, w.shape[0]))).then_inc(s_in, 16)

        @block.tensor
        def _(pe):
            pe.wait_ge(s_in, 16 * len(jobs))
            for b, (n, o, no, k, ni) in enumerate(blocks):
                if b >= 4:
                    pe.wait_ge(s_c, b - 3)
                nc.tensor.transpose(tp[b % 4][0:ni, 0:no], raw[n][0:no, o // P, k:k + ni], g.ident[0:no, 0:no]).then_inc(s_t, 1)

        @block.scalar
        def _(act):
            for b, (n, o, no, k, ni) in enumerate(blocks):
                act.wait_ge(s_t, b + 1)
                nc.scalar.copy(jobs[n][1][0:ni, k // P, o:o + no], tp[b % 4][0:ni, 0:no]).then_inc(s_c, 1)


def project(nc, name, g, x, weights, width, store, scale=None, extra=None, ones_at=None):
    chunks = [(a, min(a + BANK, width)) for a in range(0, width, BANK)]
    NC = len(chunks)
    heads = ones_at or 0
    with Phase(nc, name) as ph:
        tile = [ph.sb(f"tile{u}", [P, D]) for u in range(2)]
        turned = [ph.sb(f"turned{u}", [P, 2, P]) for u in range(2)]
        res = [ph.sb(f"res{u}", [P, width + heads]) for u in range(2)]
        tp = [ph.ps(f"tp{u}", [P, D]) for u in range(2)]
        mm = [ph.ps(f"mm{n}", [P, BANK]) for n in range(NC)]
        s_in = ph.sems("in0", "in1")
        s_st = ph.pool_sems(g, 2)
        s_tp, s_turn, s_mm, s_done, s_one = ph.sems("tp", "turn", "mm", "done", "one")
        nst = len(store(0, res[0]))
        block = ph.block()

        def turns(eng, step):
            with eng.Fori(0, T // 2, 1) as i:
                step(2 * i, i, 0)
                step(2 * i + 1, i, 1)
            step(T - 1, T // 2, 0)

        @block.sync
        def _(sp):
            def step(t, i, u):
                a = sp.snap(t * P) if not isinstance(t, int) else t * P
                need = sp.snap(t + 1) if not isinstance(t, int) else t + 1
                sp.wait_ge(s_tp, need)
                sp.sem_inc(g.waited, 1)
                sp.dma_start(tile[u][:, :], x[bass.ds(a, P), :]).then_inc(s_in[u], 16)
            turns(sp, step)

        @block.tensor
        def _(pe):
            pe.sem_inc(s_tp, 2)
            pe.sem_inc(s_done, NC)

            def turn(t, i, u):
                pe.wait_ge(s_in[u], (i + 1) * 16)
                for k in range(2):
                    last = nc.tensor.transpose(tp[u][:, k * P:(k + 1) * P], tile[u][:, k * P:(k + 1) * P], g.ident[:, :])
                last.then_inc(s_tp, 1)

            def multiply(t, u):
                pe.wait_ge(s_turn, t + 1)
                for n, (a, b) in enumerate(chunks):
                    pe.wait_ge(s_done, t * NC + (n + 1))
                    for k in range(2):
                        last = nc.tensor.matmul(mm[n][:, 0:b - a], turned[u][:, k, :], weights[:, k, a:b],
                                                start=k == 0, stop=k == 1)
                    last.then_inc(s_mm, 1)
            turn(0, 0, 0)
            with pe.Fori(0, T // 2, 1) as i:
                turn(2 * i + 1, i, 1)
                multiply(2 * i, 0)
                turn(2 * i + 2, i + 1, 0)
                multiply(2 * i + 1, 1)
            multiply(T - 1, 0)

        @block.scalar
        def _(act):
            def step(t, i, u):
                act.wait_ge(s_tp, t + 3)
                nc.scalar.copy(turned[u][:, :, :].rearrange("p k n -> p (k n)"), tp[u][:, :]).then_inc(s_turn, 1)
            turns(act, step)

        @block.vector
        def _(dve):
            if heads:
                for u in range(2):
                    nc.vector.memset(res[u][:, 0:heads * 65], 1.0).then_inc(s_one, 1)
                dve.wait_ge(s_one, 2)

            def step(t, i, u):
                dve.wait_ge(s_st[u], i * (16 * nst))
                for n, (a, b) in enumerate(chunks):
                    dve.wait_ge(s_mm, t * NC + (n + 1))
                    if heads:
                        nc.vector.tensor_copy(res[u][:, 0:heads * 65].rearrange("p (h c) -> p h c", c=65)[:, :, 0:64],
                                              mm[n][:, 0:heads * 64].rearrange("p (h c) -> p h c", c=64))
                        nc.vector.tensor_copy(extra[:, bass.ds(t, 1), :].rearrange("p a c -> p (a c)"),
                                              mm[n][:, heads * 64:width])
                        last = nc.vector.tensor_copy(res[u][:, heads * 65:], mm[n][:, heads * 64:width])
                    elif scale is not None:
                        last = nc.vector.tensor_scalar(res[u][:, a:b], mm[n][:, 0:b - a], scale[:, bass.ds(t, 1)], None, ALU.mult)
                    else:
                        last = nc.vector.tensor_copy(res[u][:, a:b], mm[n][:, 0:b - a])
                    last.then_inc(s_done, 1)
            turns(dve, step)

        @block.gpsimd
        def _(pool):
            def step(t, i, u):
                pool.wait_ge(s_done, (t + 2) * NC)
                for to, out in store(t, res[u]):
                    pool.dma_start(to, out).then_inc(s_st[u], 16)
            turns(pool, step)
            pool.wait_ge(s_st[0], (T - T // 2) * 16 * nst)
            pool.wait_ge(s_st[1], (T // 2) * 16 * nst)


def aggregate(nc, name, g, F, y, out, beside=None, y_dram=None):
    U = 5
    W = 3 * F
    with Phase(nc, name) as ph:
        strip = [ph.sb(f"strip{u}", [P, NP], BF16) for u in range(U)]
        split = ph.sb("split", [P, T, W], BF16)
        rest = ph.sb("rest", [P, T, F])
        sums = ph.sb("sums", [P, T, W])
        acc = [ph.ps(f"acc{u}", [P, BANK]) for u in range(U)]
        s_in = ph.sems(*(f"in{u}" for u in range(U)))
        s_free = ph.sems(*(f"free{u}" for u in range(U)))
        s_y, s_split, s_sum, s_out, s_v = ph.sems("y", "split", "sum", "out", "v")
        part = lambda k: split[:, :, k * F:(k + 1) * F]
        block = ph.block()

        def strips_of(eng, i):
            return (eng.value_load(g.strips_before[0:1, 1:2], min_val=1, max_val=2),
                    eng.value_load(g.strips_before[0:1, bass.ds(i, 1)], min_val=0, max_val=2 * T))

        @block.sync
        def _(sp):
            if y_dram is not None:
                sp.dma_start(y[:, :, :], nodes(y_dram)).then_inc(s_y, 16)
            with sp.Fori(0, T // U, 1) as i:
                count, before = strips_of(sp, i)
                for u in range(U):
                    with sp.Fori(0, count, 1) as q:
                        a = sp.snap(q * NP + (i * (U * P) + u * P))
                        sp.wait_ge(s_free[u], before + q + 1)
                        sp.sem_inc(g.waited, 1)
                        sp.dma_start(strip[u][:, :], g.strips[bass.ds(a, P), :]).then_inc(s_in[u], 16)

        @block.tensor
        def _(pe):
            for u in range(U):
                pe.sem_inc(s_free[u], 1)
            pe.sem_inc(s_out, U)
            pe.wait_ge(s_split, 1)
            with pe.Fori(0, T // U, 1) as i:
                count, before = strips_of(pe, i)
                for u in range(U):
                    pe.wait_ge(s_out, i * U + (u + 1))
                    nc.tensor.matmul(acc[u][:, 0:W], g.ident16[:, :],
                                     split[:, bass.ds(i * U + u, 1), :].rearrange("p t w -> p (t w)"), start=True, stop=False)
                    with pe.Fori(0, count, 1) as q:
                        pe.wait_ge(s_in[u], (before + q) * 16 + 16)
                        for s in range(T):
                            last = nc.tensor.matmul(acc[u][:, 0:W], strip[u][:, s * P:(s + 1) * P], split[:, s, :],
                                                    start=False, stop=False)
                        last.then_inc(s_free[u], 1)
                    nc.tensor.matmul(acc[u][:, 0:W], g.zeros[:, 0:P], g.zeros[:, 0:W], start=False, stop=True).then_inc(s_sum, 1)

        @block.scalar
        def _(act):
            with act.Fori(0, T // U, 1) as i:
                for u in range(U):
                    act.wait_ge(s_sum, i * U + (u + 1))
                    nc.scalar.copy(sums[:, bass.ds(i * U + u, 1), :].rearrange("p t w -> p (t w)"),
                                   acc[u][:, 0:W]).then_inc(s_out, 1)

        @block.vector
        def _(dve):
            v = Tick(s_v, dve)
            if y_dram is not None:
                dve.wait_ge(s_y, 16)
            v(nc.vector.tensor_copy(part(0), y[:, :, :]))
            v(nc.vector.tensor_tensor(rest[:, :, :], y[:, :, :], part(0), ALU.subtract))
            v(nc.vector.tensor_copy(part(1), rest[:, :, :]))
            nc.vector.tensor_tensor(part(2), rest[:, :, :], part(1), ALU.subtract).then_inc(s_split, 1)
            if beside:
                beside(dve)
            dve.wait_ge(s_out, U + T)
            v(nc.vector.tensor_tensor(out[:, :, :], sums[:, :, 2 * F:3 * F], sums[:, :, F:2 * F], ALU.add))
            nc.vector.tensor_tensor(out[:, :, :], out[:, :, :], sums[:, :, 0:F], ALU.add)


GROUPS = [(0, 6), (6, 12), (12, 18), (18, T)]


class Norm:

    def __init__(self, ph, name):
        self.stats = ph.sb(f"{name}_stats", [P, T, 6])
        self.mv = ph.sb(f"{name}_mv", [P, T, 2])
        self.std, self.less, self.eps = (ph.sb(f"{name}_{n}", [P, T]) for n in ("std", "less", "eps"))
        self.s_var, self.s_std, self.s_rec, self.s_out = ph.sems(*(f"{name}_{n}" for n in ("var", "std", "rec", "out")))

    def dve(self, nc, dve, v, x, gain=None, shift=None, before=None, done=None):
        def moments(k):
            a, b = GROUPS[k]
            if before:
                before(k, a, b)
            for t in range(a, b):
                last = nc.vector.bn_stats(self.stats[:, t, :], x[:, t, :])
            v(last)
            for t in range(a, b):
                last = nc.vector.bn_aggr(self.mv[:, t, :], self.stats[:, t, :])
            last.then_inc(self.s_var, 1)

        def factors(k):
            a, b = GROUPS[k]
            dve.wait_ge(self.s_std, k + 1)
            v(nc.vector.reciprocal(self.std[:, a:b], self.std[:, a:b]))
            nc.vector.scalar_tensor_tensor(self.less[:, a:b], self.mv[:, a:b, 0], -1.0, self.std[:, a:b], ALU.mult,
                                           ALU.mult).then_inc(self.s_rec, 1)

        def finish(k):
            a, b = GROUPS[k]
            dve.wait_ge(self.s_out, b)
            if gain is not None:
                along = lambda r: r[:, :].unsqueeze(1).to_broadcast([P, b - a, D])
                v(nc.vector.tensor_tensor(x[:, a:b, :], x[:, a:b, :], along(gain), ALU.mult))
                v(nc.vector.tensor_tensor(x[:, a:b, :], x[:, a:b, :], along(shift), ALU.add))
            if done is not None:
                dve.sem_inc(done, 1)

        v(nc.vector.memset(self.eps[:, :], EPS))
        for k in range(len(GROUPS) + 2):
            if k < len(GROUPS):
                moments(k)
            if 0 < k <= len(GROUPS):
                factors(k - 1)
            if k > 1:
                finish(k - 2)

    def act(self, nc, act, x, before=None):
        for k in range(len(GROUPS) + 1):
            if k < len(GROUPS):
                a, b = GROUPS[k]
                if before:
                    before(k)
                act.wait_ge(self.s_var, k + 1)
                nc.scalar.activation(self.std[:, a:b], self.mv[:, a:b, 1], ACT.Sqrt, bias=self.eps[:, 0:1]).then_inc(self.s_std, 1)
            if k:
                act.wait_ge(self.s_rec, k)
                for t in range(*GROUPS[k - 1]):
                    nc.scalar.activation(x[:, t, :], x[:, t, :], ACT.Identity, bias=self.less[:, t:t + 1],
                                         scale=self.std[:, t:t + 1]).then_inc(self.s_out, 1)


def nodes(a):
    return a.rearrange("(t p) f -> p t f", p=P)


def row(a):
    return a.partition_broadcast(P)


def load_x(nc, g, x, x_dram):
    with Phase(nc, "loadx") as ph:
        buf = ph.sb("buf", [P, T, D])
        s_z, s_in, s_st, s_v, s_d = ph.sems("z", "in", "st", "v", "d")
        whole = N // P
        block = ph.block()

        @block.vector
        def _(dve):
            nc.vector.memset(buf[:, whole, :], 0.0).then_inc(s_z, 1)
            nc.vector.tensor_scalar(g.dinv[:, :], g.indeg[:, :], 1.0, None, ALU.add).then_inc(s_v, 1)
            dve.wait_ge(s_d, 1)
            nc.vector.reciprocal(g.dinv[:, :], g.dinv[:, :])

        @block.scalar
        def _(act):
            act.wait_ge(s_v, 1)
            nc.scalar.activation(g.dinv[:, :], g.dinv[:, :], ACT.Sqrt).then_inc(s_d, 1)

        @block.sync
        def _(sp):
            sp.wait_ge(s_z, 1)
            sp.dma_start(buf[:, 0:whole, :], nodes(x[0:whole * P, :])).then_inc(s_in, 16)
            sp.dma_start(buf[0:N - whole * P, whole, :], x[whole * P:N, :]).then_inc(s_in, 16)
            sp.wait_ge(s_in, 32)
            sp.dma_start(nodes(x_dram), buf[:, :, :]).then_inc(s_st, 16)
            sp.wait_ge(s_st, 16)


def gcn_stack(nc, g, x_dram, ranking, W1, b1, W2, b2, W3, b3, W4, b4, x_out):
    F = 64
    with Phase(nc, "gcn") as top:
        w12 = top.sb("w12", [P, 2, F])
        w34 = top.sb("w34", [F + 1, D])
        b1w2 = top.sb("b1w2", [P, F])
        b2r = top.sb("b2r", [P, F])
        b4r = top.sb("b4r", [P, D])
        y_dram = nc.dram_tensor("gcn_y", (NP, F), F32).ap()
        with Phase(nc, "gcnw") as ph:
            w1 = ph.sb("w1", [P, 2, P])
            w1T = ph.sb("w1T", [P, D])
            w2 = ph.sb("w2", [P, F])
            w3b = ph.sb("w3b", [F + 1, P])
            w3bT = ph.sb("w3bT", [P, F + 1])
            w4 = ph.sb("w4", [P, D])
            b1c = ph.sb("b1c", [P, 1])
            b1b = ph.sb("b1b", [P, P])
            tp = ph.ps("tp", [P, BANK])
            mm = ph.ps("mm", [P, BANK])
            s_in, s_t, s_tc, s_m, s_b = ph.sems("in", "t", "tc", "m", "b")
            block = ph.block()

            @block.sync
            def _(sp):
                for to, a in ((w1[:, :, :], W1.rearrange("(k p) n -> p k n", p=P)), (w2[:, :], W2), (w3b[0:F, :], W3),
                              (w3b[F:F + 1, :], b3.rearrange("(o n) -> o n", o=1)), (w4[:, :], W4),
                              (b1c[:, :], b1.rearrange("(n o) -> n o", o=1)), (b2r[:, :], row(b2)), (b4r[:, :], row(b4))):
                    sp.dma_start(to, a).then_inc(s_in, 16)

            @block.tensor
            def _(pe):
                pe.wait_ge(s_in, 8 * 16)
                for k in range(2):
                    nc.tensor.transpose(tp[:, k * P:(k + 1) * P], w1[:, k, :], g.ident[:, :])
                nc.tensor.transpose(tp[:, D:D + F + 1], w3b[:, :], g.ident[0:F + 1, 0:F + 1]).then_inc(s_t, 1)
                pe.wait_ge(s_tc, 1)
                for k in range(2):
                    nc.tensor.matmul(mm[:, k * F:(k + 1) * F], w1T[:, k * P:(k + 1) * P], w2[:, :], start=True, stop=True)
                nc.tensor.matmul(mm[:, P:P + F], b1b[:, :], w2[:, :], start=True, stop=True)
                nc.tensor.matmul(mm[0:F + 1, D:2 * D], w3bT[:, :], w4[:, :], start=True, stop=True).then_inc(s_m, 1)

            @block.vector
            def _(dve):
                dve.wait_ge(s_in, 8 * 16)
                nc.vector.tensor_copy(b1b[:, :], b1c[:, 0:1].to_broadcast([P, P]))
                dve.wait_ge(s_t, 1)
                nc.vector.tensor_copy(w1T[:, :], tp[:, 0:D])
                nc.vector.tensor_copy(w3bT[:, :], tp[:, D:D + F + 1]).then_inc(s_tc, 1)
                dve.wait_ge(s_m, 1)
                nc.vector.tensor_copy(w12[:, :, :].rearrange("p k n -> p (k n)"), mm[:, 0:P])
                nc.vector.tensor_copy(b1w2[:, :], mm[:, P:P + F])
                nc.vector.tensor_copy(w34[:, :], mm[0:F + 1, D:2 * D])

        project(nc, "gcnp", g, x_dram, w12, F, lambda t, out: [(y_dram[bass.ds(t * P, P), :], out[:, :])], scale=g.dinv)
        with Phase(nc, "gcns") as st:
            y = st.sb("y", [P, T, F + 1])
            a64 = st.sb("a64", [P, T, F])
            a65 = st.sb("a65", [P, T, F + 1])
            y64 = st.sb("y64", [P, T, F])
            for n in range(4):
                if n:
                    g.clear()
                a, yy = (a64, y64) if n < 2 else (a65, y)
                width = F if n < 2 else F + 1
                aggregate(nc, f"agg{n}", g, width, yy, a, ranking.part(n), y_dram if n == 0 else None)
                if n == 3:
                    break
                with Phase(nc, f"gcnc{n}") as ph:
                    s_v, s_a = ph.sems("v", "a")
                    block = ph.block()
                    wide = lambda w: g.dinv[:, :].unsqueeze(2).to_broadcast([P, T, w])
                    along = lambda r: r[:, :].unsqueeze(1).to_broadcast([P, T, F])

                    @block.vector
                    def _(dve):
                        v = Tick(s_v, dve)
                        v(nc.vector.tensor_tensor(a[:, :, :], a[:, :, :], wide(width), ALU.mult))
                        if n == 0:
                            v(nc.vector.tensor_tensor(a[:, :, :], a[:, :, :], along(b1w2), ALU.add))
                            nc.vector.tensor_tensor(y64[:, :, :], a[:, :, :], wide(F), ALU.mult)
                        elif n == 1:
                            nc.vector.tensor_tensor(a[:, :, :], a[:, :, :], along(b2r), ALU.add).then_inc(s_a, 1)
                            v(nc.vector.memset(y[:, :, F:F + 1], 1.0))
                            dve.wait_ge(s_a, 2)
                            nc.vector.tensor_tensor(y[:, :, :], y[:, :, :], wide(F + 1), ALU.mult)
                        else:
                            v(nc.vector.memset(a[:, :, F:F + 1], 1.0))
                            nc.vector.tensor_tensor(y[:, :, :], a[:, :, :], wide(F + 1), ALU.mult)

                    @block.scalar
                    def _(act):
                        if n == 1:
                            act.wait_ge(s_a, 1)
                            nc.scalar.activation(y[:, :, 0:F], a[:, :, :], ACT.Sigmoid).then_inc(s_a, 1)
            with Phase(nc, "gcno") as ph:
                x = ph.sb("x", [P, T, D])
                w = ph.sb("w", [P, T, D])
                turned = [ph.sb(f"turned{u}", [F + 1, 2 * P]) for u in range(2)]
                norm = Norm(ph, "n")
                tp = [ph.ps(f"tp{u}", [F + 1, BANK]) for u in range(2)]
                mm = [ph.ps(f"mm{u}", [P, BANK]) for u in range(2)]
                s_in, s_v, s_a, s_t, s_c, s_m, s_r, s_o, s_st = ph.sems("in", "v", "a", "t", "c", "m", "r", "o", "st")
                pairs = [range(a, min(a + 2, T)) for a in range(0, T, 2)]
                block = ph.block()

                @block.sync
                def _(sp):
                    sp.dma_start(x[:, :, :], nodes(x_dram)).then_inc(s_in, 16)
                    for k, (a, b) in enumerate(GROUPS):
                        sp.wait_ge(s_o, k + 1)
                        sp.dma_start(nodes(x_out)[:, a:b, :], x[:, a:b, :]).then_inc(s_st, 16)
                    sp.wait_ge(s_st, 16 * len(GROUPS))

                @block.tensor
                def _(pe):
                    pe.wait_ge(s_a, 1)
                    for k, pr in enumerate(pairs):
                        if k > 1:
                            pe.wait_ge(s_c, k - 1)
                        for n, t in enumerate(pr):
                            last = nc.tensor.transpose(tp[k % 2][:, n * P:(n + 1) * P], a65[:, t, :], g.ident[:, :])
                        last.then_inc(s_t, 1)
                        pe.wait_ge(s_c, k + 1)
                        if k > 1:
                            pe.wait_ge(s_r, k - 1)
                        for n, t in enumerate(pr):
                            last = nc.tensor.matmul(mm[k % 2][:, n * D:(n + 1) * D], turned[k % 2][:, n * P:(n + 1) * P], w34[:, :],
                                                    start=True, stop=True)
                        last.then_inc(s_m, 1)

                @block.scalar
                def _(act):
                    def before(group):
                        low = GROUPS[group + 1][0] if 0 < group < len(GROUPS) - 1 else 0 if group == 0 else T
                        high = GROUPS[min(group + 1, len(GROUPS) - 1)][1]
                        for k, pr in enumerate(pairs):
                            if low <= pr[0] < high:
                                act.wait_ge(s_t, k + 1)
                                nc.scalar.copy(turned[k % 2][:, 0:len(pr) * P], tp[k % 2][:, 0:len(pr) * P]).then_inc(s_c, 1)
                    norm.act(nc, act, x, before)

                @block.vector
                def _(dve):
                    v = Tick(s_v, dve)
                    wide = g.dinv[:, :].unsqueeze(2).to_broadcast([P, T, F + 1])
                    nc.vector.tensor_tensor(a65[:, :, :], a65[:, :, :], wide, ALU.mult).then_inc(s_a, 1)
                    dve.wait_ge(s_in, 16)

                    def before(_, a, b):
                        mine = [k for k, pr in enumerate(pairs) if a <= pr[0] < b]
                        for k in mine:
                            pr = pairs[k]
                            dve.wait_ge(s_m, k + 1)
                            nc.vector.tensor_tensor(w[:, pr[0]:pr[-1] + 1, :],
                                                    mm[k % 2][:, 0:len(pr) * D].rearrange("p (t d) -> p t d", d=D),
                                                    b4r[:, :].unsqueeze(1).to_broadcast([P, len(pr), D]), ALU.add).then_inc(s_r, 1)
                        dve.wait_ge(s_r, mine[-1] + 1)
                        v(nc.vector.scalar_tensor_tensor(x[:, a:b, :], w[:, a:b, :], 0.0, x[:, a:b, :], ALU.max, ALU.add))
                    norm.dve(nc, dve, v, x, before=before, done=s_o)


class Ranking:

    def __init__(self, nc, g, ph, noise):
        self.nc, self.g = nc, g
        self.key = ph.sb("key", [P, NP])
        self.keyc = ph.sb("keyc", [P, T])
        self.own = ph.sb("own", [P, T])
        self.before = ph.sb("before", [P, NP], BF16)
        self.same = ph.sb("same", [P, NP], BF16)
        self.less = ph.sb("less", [P, NP], BF16)
        self.rank = ph.sb("rank", [P, T])
        self.s_v = ph.sems("v0", "v1", "v2", "v3")
        self.noise = noise

    def keys(self, outdeg):
        nc, key = self.nc, self.key
        with Phase(nc, "rankk") as ph:
            nrow = ph.sb("nrow", [P, N])
            owni = ph.sb("owni", [P, T], I32)
            key_dram = nc.dram_tensor("key_row", (1, NP), F32).ap()
            s_in, s_v, s_k, s_st, s_kc, s_io = ph.sems("in", "v", "k", "st", "kc", "io")
            block = ph.block()

            @block.gpsimd
            def _(pool):
                nc.gpsimd.iota(owni[:, :], [[P, T]], base=-HALF, channel_multiplier=1).then_inc(s_io, 1)

            @block.sync
            def _(sp):
                sp.dma_start(nrow[:, :], row(self.noise)).then_inc(s_in, 16)
                sp.wait_ge(s_k, 1)
                sp.dma_start(key_dram, key[0:1, :]).then_inc(s_st, 16)
                sp.wait_ge(s_st, 16)
                with nc.allow_non_contiguous_dma(reason="one key for each node"):
                    sp.dma_start(self.keyc[:, :], key_dram.rearrange("o (t p) -> p (o t)", p=P)).then_inc(s_kc, 16)
                sp.wait_ge(s_kc, 16)

            @block.vector
            def _(dve):
                v = Tick(s_v, dve)
                dve.wait_ge(s_in, 16)
                v(nc.vector.memset(key[:, N:NP], 1e30))
                nc.vector.tensor_tensor(key[:, 0:N], outdeg[:, 0:N], nrow[:, :], ALU.add).then_inc(s_k, 1)
                dve.wait_ge(s_io, 1)
                v(nc.vector.tensor_copy(self.own[:, :], owni[:, :]))

    def part(self, n):
        nc, key = self.nc, self.key
        start, end = n * T // 4, (n + 1) * T // 4

        def work(dve):
            v = Tick(self.s_v[n], dve)
            with dve.Fori(0, end - start, 1) as i:
                v.loop(i, 3)
                at = bass.ds(i + start, 1)
                v(nc.vector.tensor_scalar(self.before[:, :], self.g.numbers[:, :], self.own[:, at], None, ALU.is_lt))
                v(nc.vector.scalar_tensor_tensor(self.same[:, :], key[:, :], self.keyc[:, at], self.before[:, :],
                                                 ALU.is_equal, ALU.mult))
                v(nc.vector.scalar_tensor_tensor(self.less[:, :], key[:, :], self.keyc[:, at], self.same[:, :],
                                                 ALU.is_lt, ALU.add, accum_out=self.rank[:, at]))
            v.end(end - start)
            if end == T:
                nc.vector.tensor_copy(self.g.rank[:, :], self.rank[:, :])
        return work


def score_rows(nc, name, g, H, extra, row_dram, col0=0):
    W = extra.shape[2]
    half = [(0, 13), (13, T)]
    with Phase(nc, name) as ph:
        rows = [ph.sb(f"rows{k}", [13 * W, P]) for k in range(2)]
        tp = [ph.ps(f"tp{k}", [13 * W, P]) for k in range(2)]
        s_t, s_c, s_st = ph.sems("t", "c", "st")
        block = ph.block()

        @block.tensor
        def _(pe):
            for k, (a, b) in enumerate(half):
                nc.tensor.transpose(tp[k][0:(b - a) * W, :], extra[:, a:b, :].rearrange("p t c -> p (t c)"), g.ident[:, :]).then_inc(s_t, 1)

        @block.vector
        def _(dve):
            for k, (a, b) in enumerate(half):
                dve.wait_ge(s_t, k + 1)
                nc.vector.tensor_copy(rows[k][0:(b - a) * W, :], tp[k][0:(b - a) * W, :]).then_inc(s_c, 1)

        @block.sync
        def _(sp):
            for k, (a, b) in enumerate(half):
                sp.wait_ge(s_c, k + 1)
                for t in range(a, b):
                    sp.dma_start(row_dram[:, t * P:(t + 1) * P], rows[k][(t - a) * W:(t - a + 1) * W, :]).then_inc(s_st, 16)
            sp.wait_ge(s_st, 16 * T)


def attention(nc, name, g, H, pr_dram, scores, agg_dram, by_target, side=None):
    with Phase(nc, name) as top:
        rows_dram = nc.dram_tensor(f"{name}_scores", (2 * H, NP), F32).ap()
        m_dram = nc.dram_tensor(f"{name}_best", (H, NP), F32).ap()
        score_rows(nc, f"{name}s", g, H, scores, rows_dram)
        top_m = top.sb("m", [P, T, H])
        top_p = top.sb("mp", [P, 1])
        with Phase(nc, f"{name}m") as ph:
            srow = ph.sb("srow", [P, H, NP])
            gone = [ph.sb(f"gone{u}", [P, NP], BF16) for u in range(2)]
            junk = ph.sb("junk", [P, H, NP], BF16)
            top4 = ph.sb("top4", [P, 2, H])
            best = ph.sb("best", [P, T, H])
            s_row, s_used, s_v, s_x = ph.sems("row", "used", "v", "x")
            s_in = ph.sems("in0", "in1")
            if side:
                side_ph = ph.ctx.enter_context(Phase(nc, f"{name}i"))
                block = ph.block()
                side.beside(side_ph, block)
            else:
                block = ph.block()

            @block.sync
            def _(sp):
                sp.dma_start(srow[:, :, :].rearrange("p h n -> p (h n)"),
                             row(rows_dram[0:H, :].rearrange("h n -> (h n)"))).then_inc(s_row, 16)

                def step(t, i, u):
                    a = sp.snap(t * P) if not isinstance(t, int) else t * P
                    need = sp.snap(t + 1) if not isinstance(t, int) else t + 1
                    sp.wait_ge(s_used, need)
                    sp.sem_inc(g.waited, 1)
                    sp.dma_start(gone[u][:, :], g.absent[bass.ds(a, P), :]).then_inc(s_in[u], 16)
                with sp.Fori(0, T // 2, 1) as i:
                    step(2 * i, i, 0)
                    step(2 * i + 1, i, 1)
                step(T - 1, T // 2, 0)

            @block.vector
            def _(dve):
                dve.wait_ge(s_row, 16)
                dve.sem_inc(s_used, 2)

                def step(t, i, u):
                    dve.wait_ge(s_in[u], (i + 1) * 16)
                    dve.sem_inc(g.waited, 1)
                    for h in range(H):
                        last = nc.vector.tensor_tensor_reduce(out=junk[:, h, :], in0=gone[u][:, :], in1=srow[:, h, :], scale=1.0,
                                                              scalar=-3e38, op0=ALU.add, op1=ALU.max,
                                                              accum_out=top4[:, u, h:h + 1])
                    last.then_inc(s_x, 1)
                    dve.wait_ge(s_x, t + 1)
                    nc.vector.tensor_copy(best[:, bass.ds(t, 1), :].rearrange("p a h -> p (a h)"), top4[:, u, :]).then_inc(s_used, 1)
                with dve.Fori(0, T // 2, 1) as i:
                    step(2 * i, i, 0)
                    step(2 * i + 1, i, 1)
                step(T - 1, T // 2, 0)
                v = Tick(s_v, dve)
                dve.wait_ge(s_used, T + 2)
                if by_target:
                    v(nc.vector.tensor_scalar(top_m[:, :, :], best[:, :, :], 0.5 * NEG, -NEG, ALU.is_lt, ALU.mult))
                    v(nc.vector.tensor_tensor(best[:, :, :], best[:, :, :], top_m[:, :, :], ALU.add))
                v(nc.vector.tensor_tensor(best[:, :, :], best[:, :, :], scores[:, :, H:2 * H], ALU.add))
                v(nc.vector.scalar_tensor_tensor(top_m[:, :, :], best[:, :, :], 0.2, best[:, :, :], ALU.mult, ALU.max))
                if not by_target:
                    real = N - (T - 1) * P
                    v(nc.vector.tensor_reduce(top_p[:, :], top_m[:, 0:T - 1, :], AX.XY, ALU.max))
                    v(nc.vector.tensor_reduce(top4[0:real, 0, 0:1], top_m[0:real, T - 1, :], AX.X, ALU.max))
                    v(nc.vector.tensor_tensor(top_p[0:real, :], top_p[0:real, :], top4[0:real, 0, 0:1], ALU.max))
        if by_target:
            score_rows(nc, f"{name}t", g, H, top_m, m_dram)
        U = 5
        with Phase(nc, f"{name}x") as ph:
            t1 = ph.sb("t1", [P, H, NP])
            t2 = ph.sb("t2", [P, H, NP])
            s08 = ph.sb("s08", [P, T, H])
            s02 = ph.sb("s02", [P, T, H])
            allm = ph.sb("allm", [P, 1])
            allp = ph.sb("allp", [P, P])
            adj = [ph.sb(f"adj{u}", [P, J]) for u in range(U)]
            feat = [ph.sb(f"feat{u}", [P, H * 65]) for u in range(U)]
            w = [ph.sb(f"w{u}", [P, H, J]) for u in range(U)]
            agg = ph.sb("agg", [65, H, J])
            acc = [[ph.ps(f"acc{k}_{h}", [65, J]) for h in range(H)] for k in range(2)]
            s_row, s_v, s_ready = ph.sems("row", "v", "ready")
            s_in = ph.sems(*(f"in{u}" for u in range(U)))
            s_z, s_e, s_w, s_pw, s_used, s_sum, s_out, s_st = ph.sems("z", "e", "w", "pw", "used", "sum", "out", "st")
            s_pm, s_mp, s_t2 = ph.sems("pm", "mp", "t2")
            R = T // U
            on_pool = lambda u: 2 if H == 4 and u % 2 else max(1, H // 4)
            block = ph.block()

            def rounds(eng, step, j, some):
                def one(i):
                    for u in range(U):
                        step(j, i * U + u, j * T + i * U + u, j * R + i, u)
                if len(some) == 1:
                    return one(some[0])
                with eng.Fori(some[0], some[-1] + 1, 1) as i:
                    one(i)

            def turns(eng, step):
                with eng.Fori(0, NJ, 1) as j:
                    rounds(eng, step, j, range(R))

            @block.sync
            def _(sp):
                if not by_target:
                    with nc.allow_non_contiguous_dma(reason="one number for each partition"):
                        sp.dma_start(m_dram[0:1, 0:P].rearrange("o p -> p o"), top_p[:, :]).then_inc(s_mp, 16)
                sp.dma_start(t1[:, :, :].rearrange("p h n -> p (h n)"),
                             row(rows_dram[H:2 * H, :].rearrange("h n -> (h n)"))).then_inc(s_row, 16)
                if by_target:
                    sp.dma_start(t2[:, :, :].rearrange("p h n -> p (h n)"),
                                 row(m_dram.rearrange("h n -> (h n)"))).then_inc(s_row, 16)
                else:
                    sp.wait_ge(s_mp, 16)
                    sp.dma_start(allp[:, :], row(m_dram[0:1, 0:P].rearrange("o p -> (o p)"))).then_inc(s_row, 16)

                def step(j, s, q, n, u):
                    a = sp.snap(s * P)
                    c = sp.snap(j * J)
                    need = sp.snap(q + 1)
                    sp.wait_ge(s_used, need)
                    sp.sem_inc(g.waited, 1)
                    sp.dma_start(adj[u][:, :], g.adj[bass.ds(a, P), bass.ds(c, J)]).then_inc(s_in[u], 16)
                    sp.dma_start(feat[u][:, :], pr_dram[bass.ds(a, P), 0:H * 65]).then_inc(s_in[u], 16)
                turns(sp, step)

            @block.vector
            def _(dve):
                v = Tick(s_v, dve)
                dve.wait_ge(s_row, 32)
                if by_target:
                    v(nc.vector.tensor_tensor(t1[:, :, :], t1[:, :, :], t2[:, :, :], ALU.subtract))
                    v(nc.vector.tensor_scalar(t2[:, :, :], t2[:, :, :], -0.8, None, ALU.mult))
                    v(nc.vector.scalar_tensor_tensor(t2[:, :, :], t1[:, :, :], 0.2, t2[:, :, :], ALU.mult, ALU.add))
                    v(nc.vector.tensor_scalar(s02[:, :, :], scores[:, :, 0:H], 0.2, None, ALU.mult))
                else:
                    v(nc.vector.tensor_reduce(allm[:, :], allp[:, :], AX.X, ALU.max))
                    v(nc.vector.tensor_scalar(t2[:, H // 2:, :], t1[:, H // 2:, :], 0.2, None, ALU.mult))
                    v(nc.vector.tensor_scalar(s02[:, :, :], scores[:, :, 0:H], 0.2, allm[:, 0:1], ALU.mult, ALU.subtract))
                v(nc.vector.tensor_scalar(s08[:, :, :], scores[:, :, 0:H], 0.8, None, ALU.mult))
                dve.sem_inc(s_ready, 1)
                if not by_target:
                    dve.wait_ge(s_t2, H // 2)

                def scores_of(j, s, q, u):
                    dve.wait_ge(s_used, q + 1)
                    c = j * J if isinstance(j, int) else dve.snap(j * J)
                    for h in range(H):
                        last = nc.vector.scalar_tensor_tensor(w[u][:, h, :], t1[:, h, bass.ds(c, J)],
                                                              s08[:, bass.ds(s, 1), h], t2[:, h, bass.ds(c, J)],
                                                              ALU.add, ALU.max)
                    last.then_inc(s_z, 1)

                def weights_of(q, n, u):
                    dve.wait_ge(s_in[u], (n + 1) * 32)
                    dve.wait_ge(s_e, q + 1)
                    k = on_pool(u)
                    nc.vector.scalar_tensor_tensor(w[u][:, k:, :], w[u][:, k:, :], 1.0,
                                                   adj[u][:, :].unsqueeze(1).to_broadcast([P, H - k, J]),
                                                   ALU.min, ALU.mult).then_inc(s_w, 1)

                LEAD = 2

                def targets(j, final):
                    with dve.Fori(0, R - 1, 1) as i:
                        for u in range(U):
                            s = i * U + (u + LEAD)
                            scores_of(j, s, j * T + s, (u + LEAD) % U)
                            weights_of(j * T + i * U + u, j * R + i, u)
                    for s in range((R - 1) * U, T):
                        ahead = s + LEAD
                        if ahead < T:
                            scores_of(j, ahead, j * T + ahead, ahead % U)
                        elif not final:
                            scores_of(j + 1, ahead - T, j * T + ahead, ahead % U)
                        weights_of(j * T + s, j * R + (R - 1), s % U)
                for s in range(LEAD):
                    scores_of(0, s, s, s)
                with dve.Fori(0, NJ - 1, 1) as j:
                    targets(j, False)
                targets(NJ - 1, True)

            @block.scalar
            def _(act):
                if not by_target:
                    act.wait_ge(s_row, 32)
                    for h in range(H // 2):
                        nc.scalar.activation(t2[:, h, :], t1[:, h, :], ACT.Copy, scale=0.2).then_inc(s_t2, 1)
                act.wait_ge(s_ready, 1)

                def step(j, s, q, n, u):
                    act.wait_ge(s_z, q + 1)
                    for h in range(H):
                        last = nc.scalar.activation(w[u][:, h, :], w[u][:, h, :], ACT.Exp, bias=s02[:, bass.ds(s, 1), h])
                    last.then_inc(s_e, 1)

                def end(j, k):
                    act.wait_ge(s_sum, j + 1)
                    act.wait_ge(s_st, j * 16)
                    for h in range(H):
                        last = nc.scalar.copy(agg[:, h, :], acc[k][h][:, :])
                    last.then_inc(s_out, 1)
                    act.wait_ge(s_out, j + 3)
                    act.sem_inc(g.waited, 1)
                    at = j * J if isinstance(j, int) else act.snap(j * J)
                    act.dma_start(agg_dram[:, :, bass.ds(at, J)].rearrange("h c n -> c h n"), agg[:, :, :]).then_inc(s_st, 16)

                first, others = range(1), range(1, R)
                rounds(act, step, 0, first)
                with act.Fori(0, NJ // 2 - 1, 1) as i:
                    for k in range(2):
                        j = 2 * i + k
                        rounds(act, step, j, others)
                        rounds(act, step, j + 1, first)
                        end(j, k)
                rounds(act, step, NJ - 2, others)
                rounds(act, step, NJ - 1, first)
                end(NJ - 2, 0)
                rounds(act, step, NJ - 1, others)
                end(NJ - 1, 1)
                act.wait_ge(s_st, NJ * 16)

            @block.tensor
            def _(pe):
                pe.sem_inc(s_used, U)
                pe.sem_inc(s_out, 2)

                def targets(j, k):
                    def step(j, s, q, n, u):
                        pe.wait_ge(s_in[u], (n + 1) * 32)
                        pe.wait_ge(s_w, q + 1)
                        pe.wait_ge(s_pw, q + 1)
                        for h in range(H):
                            last = nc.tensor.matmul(acc[k][h][:, :], feat[u][:, h * 65:(h + 1) * 65], w[u][:, h, :], start=False, stop=False)
                        last.then_inc(s_used, 1)
                    pe.wait_ge(s_out, j + 1)
                    for h in range(H):
                        nc.tensor.matmul(acc[k][h][:, :], g.zeros[:, 0:65], g.zeros[:, 0:J], start=True, stop=False)
                    rounds(pe, step, j, range(R))
                    for h in range(H):
                        last = nc.tensor.matmul(acc[k][h][:, :], g.zeros[:, 0:65], g.zeros[:, 0:J], start=False, stop=True)
                    last.then_inc(s_sum, 1)
                with pe.Fori(0, NJ // 2, 1) as i:
                    for k in range(2):
                        targets(2 * i + k, k)

            @block.gpsimd
            def _(pool):
                def step(j, s, q, n, u):
                    pool.wait_ge(s_in[u], (n + 1) * 32)
                    pool.wait_ge(s_e, q + 1)
                    pool.sem_inc(g.waited, 1)
                    mine = w[u][:, 0:on_pool(u), :]
                    nc.gpsimd.tensor_scalar(mine, mine, 1.0, None, ALU.min).then_inc(s_pm, 1)
                    pool.wait_ge(s_pm, q + 1)
                    nc.gpsimd.tensor_tensor(mine, mine, adj[u][:, :].unsqueeze(1).to_broadcast([P, on_pool(u), J]),
                                            ALU.mult).then_inc(s_pw, 1)
                turns(pool, step)


def heads_to_nodes(nc, name, g, H, agg_dram, out, floor):
    with Phase(nc, name) as ph:
        part = [ph.sb(f"part{u}", [65, H, P]) for u in range(2)]
        den = ph.sb("den", [P, H])
        tp = [ph.ps(f"tp{u}", [P, BANK]) for u in range(2)]
        s_in = ph.sems("in0", "in1")
        s_t, s_o, s_v = ph.sems("t", "o", "v")
        block = ph.block()

        def turns(eng, step):
            with eng.Fori(0, T // 2, 1) as i:
                step(2 * i, i, 0)
                step(2 * i + 1, i, 1)
            step(T - 1, T // 2, 0)

        @block.sync
        def _(sp):
            def step(t, i, u):
                a = sp.snap(t * P) if not isinstance(t, int) else t * P
                need = sp.snap(t + 1) if not isinstance(t, int) else t + 1
                sp.wait_ge(s_t, need)
                sp.sem_inc(g.waited, 1)
                sp.dma_start(part[u][:, :, :], agg_dram[:, :, bass.ds(a, P)].rearrange("h c n -> c h n")).then_inc(s_in[u], 16)
            turns(sp, step)

        @block.tensor
        def _(pe):
            pe.sem_inc(s_t, 2)

            def step(t, i, u):
                pe.wait_ge(s_in[u], (i + 1) * 16)
                pe.wait_ge(s_o, t)
                for h in range(H):
                    last = nc.tensor.transpose(tp[u][:, h * 65:(h + 1) * 65], part[u][:, h, :], g.ident[0:65, 0:65])
                last.then_inc(s_t, 1)
            turns(pe, step)

        @block.vector
        def _(dve):
            def step(t, i, u):
                dve.wait_ge(s_t, t + 3)
                heads = tp[u][:, 0:H * 65].rearrange("p (h c) -> p h c", c=65)
                nc.vector.tensor_scalar(den[:, :].unsqueeze(2), heads[:, :, 64:65], floor[1], None, floor[0]).then_inc(s_v, 1)
                dve.wait_ge(s_v, 2 * t + 1)
                nc.vector.reciprocal(den[:, :], den[:, :]).then_inc(s_v, 1)
                dve.wait_ge(s_v, 2 * t + 2)
                nc.vector.tensor_tensor(out[:, bass.ds(t, 1), :].rearrange("p a (h c) -> p (a h) c", c=64), heads[:, :, 0:64],
                                        den[:, :].unsqueeze(2).to_broadcast([P, H, 64]), ALU.mult).then_inc(s_o, 1)
            turns(dve, step)


def score_weights(nc, name, g, W, turned, a_src, a_tgt, H, out):
    K = H * 64 // P
    with Phase(nc, name) as ph:
        diag = ph.sb("diag", [P, K, 2 * H])
        mm = ph.ps("mm", [P, 2 * 2 * H])
        s_z, s_in, s_m = ph.sems("z", "in", "m")
        block = ph.block()

        @block.vector
        def _(dve):
            nc.vector.memset(diag[:, :, :], 0.0).then_inc(s_z, 1)
            dve.wait_ge(s_m, 1)
            nc.vector.tensor_copy(out[:, :, H * 64:H * 66], mm[:, :].rearrange("p (k c) -> p k c", k=2))

        @block.sync
        def _(sp):
            sp.wait_ge(s_z, 1)
            for n, a in enumerate((a_src, a_tgt)):
                for h in range(H):
                    p = 64 * (h % 2)
                    with nc.allow_non_contiguous_dma(reason="64 numbers"):
                        sp.dma_start(diag[p:p + 64, h // 2, n * H + h:n * H + h + 1],
                                     a[h, :].rearrange("(c o) -> c o", o=1)).then_inc(s_in, 16)

        @block.tensor
        def _(pe):
            pe.wait_ge(s_in, 2 * H * 16)
            for k in range(2):
                for o in range(K):
                    last = nc.tensor.matmul(mm[:, k * 2 * H:(k + 1) * 2 * H], turned[:, o, k * P:(k + 1) * P], diag[:, o, :],
                                            start=o == 0, stop=o == K - 1)
            last.then_inc(s_m, 1)


class SortedInput:

    def __init__(self, nc, g, x_dram, inT, raw_dram, z_dram):
        self.nc, self.g, self.x_dram, self.inT, self.raw_dram, self.z_dram = nc, g, x_dram, inT, raw_dram, z_dram
        self.xs_dram = nc.dram_tensor("sorted_x", (NP, D), F32).ap()

    def beside(self, ph, block):
        nc, g, inT = self.nc, self.g, self.inT
        buf = ph.sb("side_buf", [P, T * D])
        xsT = ph.sb("side_xsT", [P, 2, NP])
        rows = buf[:, :].rearrange("p (t d) -> p t d", d=D)
        halves = buf[:, :].rearrange("p (k n) -> p k n", k=2)
        tp = [ph.ps(f"side_tp{u}", [P, D]) for u in range(2)]
        mm = [ph.ps(f"side_mm{u}", [P, BANK]) for u in range(4)]
        (s_dma,) = ph.pool_sems(g, 1)
        s_t, s_c, s_mm, s_ev = ph.sems("side_t", "side_c", "side_mm", "side_ev")
        NB = len(BANKS)
        jobs = [(n, a, b) for n in (2, 3, 0, 1) for a, b in BANKS]
        SORTED, Z_STORED, STORED = (T + 2) * 16, (T + 3) * 16, (T + 4) * 16

        @block.gpsimd
        def _(pool):
            pool.dma_start(rows, nodes(self.x_dram)).then_inc(s_dma, 16)
            pool.wait_ge(s_dma, 16)
            for t in range(T):
                pool.indirect_dma_start(self.xs_dram, bass.IndirectOffsetOnAxis(ap=g.rank[:, t:t + 1], axis=0),
                                        rows[:, t, :], None).then_inc(s_dma, 16)
            pool.wait_ge(s_dma, (T + 1) * 16)
            pool.dma_start(rows, nodes(self.xs_dram)).then_inc(s_dma, 16)
            pool.wait_ge(s_ev, 2 * NB)
            pool.dma_start(self.z_dram.rearrange("k p n -> p k n"), halves).then_inc(s_dma, 16)
            pool.wait_ge(s_ev, 4 * NB)
            pool.dma_start(self.raw_dram.rearrange("k p n -> p k n"), halves).then_inc(s_dma, 16)
            pool.wait_ge(s_dma, STORED)

        @block.tensor
        def _(pe):
            pe.wait_ge(s_dma, SORTED)
            for t in range(T):
                if t > 1:
                    pe.wait_ge(s_c, t - 1)
                for k in range(2):
                    last = nc.tensor.transpose(tp[t % 2][:, k * P:(k + 1) * P], rows[:, t, k * P:(k + 1) * P], g.ident[:, :])
                last.then_inc(s_t, 1)
            pe.wait_ge(s_c, T)
            for q, (n, a, b) in enumerate(jobs):
                if q >= 4:
                    pe.wait_ge(s_ev, q - 3)
                for k in range(2):
                    last = nc.tensor.matmul(mm[q % 4][:, 0:b - a], inT[:, k, n * P:(n + 1) * P], xsT[:, k, a:b],
                                            start=k == 0, stop=k == 1)
                last.then_inc(s_mm, 1)

        @block.scalar
        def _(act):
            for t in range(T):
                act.wait_ge(s_t, t + 1)
                nc.scalar.copy(xsT[:, :, t * P:(t + 1) * P], tp[t % 2][:, :].rearrange("p (k n) -> p k n", k=2)).then_inc(s_c, 1)
            for q, (n, a, b) in enumerate(jobs):
                if q == 2 * NB:
                    act.wait_ge(s_dma, Z_STORED)
                act.wait_ge(s_mm, q + 1)
                nc.scalar.activation(halves[:, n % 2, a:b], mm[q % 4][:, 0:b - a],
                                     ACT.Silu if n >= 2 else ACT.Copy).then_inc(s_ev, 1)


def local_branch(nc, g, x_dram, gat_w, a_src, a_tgt, gat_b, gain, shift, hl_dram, in_w, raw_dram, z_dram):
    H = 4
    pr_dram = nc.dram_tensor("local_rows", (NP, H * 65 + 2 * H), F32).ap()
    agg_dram = nc.dram_tensor("local_agg", (H, 65, NP), F32).ap()
    with Phase(nc, "loc") as top:
        scores = top.sb("scores", [P, T, 2 * H])
        inT = top.sb("inT", [P, 2, 2 * D])
        with Phase(nc, "locw") as ph:
            weights = ph.sb("weights", [P, 2, H * 64 + 2 * H])
            raw = ph.sb("raw", [P, 2, D])
            turned_weights(nc, "locwt", g, [(gat_w, weights), (in_w, inT)])
            load_all(nc, "locwl", [(raw[:, :, :], gat_w.rearrange("(k p) i -> p k i", p=P))])
            score_weights(nc, "locws", g, None, raw, a_src, a_tgt, H, weights)
            project(nc, "locp", g, x_dram, weights, H * 66, lambda t, out: [(pr_dram[bass.ds(t * P, P), :], out[:, :])],
                    extra=scores, ones_at=H)
        attention(nc, "gat", g, H, pr_dram, scores, agg_dram, False,
                  SortedInput(nc, g, x_dram, inT, raw_dram, z_dram))
        with Phase(nc, "loco") as ph:
            h = ph.sb("h", [P, T, D])
            x = ph.sb("x", [P, T, D])
            w = ph.sb("w", [P, T, D])
            rows = ph.sb("rows", [P, 3, D])
            norm = Norm(ph, "n")
            heads_to_nodes(nc, "loch", g, H, agg_dram, h, (ALU.add, 1e-16))
            s_in, s_row, s_v, s_a, s_e, s_o, s_st = ph.sems("in", "row", "v", "a", "e", "o", "st")
            block = ph.block()

            @block.sync
            def _(sp):
                for k, r in enumerate((gat_b, gain, shift)):
                    sp.dma_start(rows[:, k, :], row(r)).then_inc(s_row, 16)
                for k, (a, b) in enumerate(GROUPS):
                    if k:
                        sp.wait_ge(s_in, 16 * k)
                    sp.dma_start(x[:, a:b, :], nodes(x_dram)[:, a:b, :]).then_inc(s_in, 16)
                for k, (a, b) in enumerate(GROUPS):
                    sp.wait_ge(s_o, k + 1)
                    sp.dma_start(nodes(hl_dram)[:, a:b, :], h[:, a:b, :]).then_inc(s_st, 16)
                sp.wait_ge(s_st, 16 * len(GROUPS))

            @block.vector
            def _(dve):
                v = Tick(s_v, dve)
                dve.wait_ge(s_row, 48)
                for k, (a, b) in enumerate(GROUPS):
                    dve.wait_ge(s_in, 16 * (k + 1))
                    part = h[:, a:b, :]
                    v(nc.vector.tensor_tensor(part, part, x[:, a:b, :], ALU.add))
                    v(nc.vector.tensor_tensor(part, part, rows[:, 0, :].unsqueeze(1).to_broadcast([P, b - a, D]), ALU.add))
                    nc.vector.tensor_scalar(w[:, a:b, :], part, 0.0, None, ALU.min).then_inc(s_a, 1)

                def before(k, a, b):
                    dve.wait_ge(s_e, k + 1)
                    v(nc.vector.tensor_scalar(h[:, a:b, :], h[:, a:b, :], 0.0, -1.0, ALU.max, ALU.add))
                    v(nc.vector.tensor_tensor(h[:, a:b, :], h[:, a:b, :], w[:, a:b, :], ALU.add))
                norm.dve(nc, dve, v, h, rows[:, 1, :], rows[:, 2, :], before, s_o)

            @block.scalar
            def _(act):
                for k, (a, b) in enumerate(GROUPS):
                    act.wait_ge(s_a, k + 1)
                    nc.scalar.activation(w[:, a:b, :], w[:, a:b, :], ACT.Exp).then_inc(s_e, 1)
                norm.act(nc, act, h)


def load_all(nc, name, jobs):
    with Phase(nc, name) as ph:
        s_in = ph.sem("in")
        block = ph.block()

        @block.sync
        def _(sp):
            for to, a in jobs:
                with nc.allow_non_contiguous_dma(reason="small parameters"):
                    sp.dma_start(to, a).then_inc(s_in, 16)
            sp.wait_ge(s_in, 16 * len(jobs))


def moved_rows(nc, name, g, table, buf, scatter):
    with Phase(nc, name) as ph:
        (s_m,) = ph.pool_sems(g, 1)
        block = ph.block()

        @block.gpsimd
        def _(pool):
            for t in range(T):
                at = bass.IndirectOffsetOnAxis(ap=g.rank[:, t:t + 1], axis=0)
                if scatter:
                    pool.indirect_dma_start(table, at, buf[:, t, :], None).then_inc(s_m, 16)
                else:
                    pool.indirect_dma_start(buf[:, t, :], None, table, at).then_inc(s_m, 16)
            pool.wait_ge(s_m, 16 * T)


def banked_products(nc, ph, name, block, jobs, evict):
    mm = [ph.ps(f"{name}_mm{k}", [P, BANK]) for k in range(4)]
    s_mm, s_ev = ph.sems(f"{name}_mm", f"{name}_ev")
    todo = [(n, a, b) for n in range(len(jobs)) for a, b in BANKS]

    @block.tensor
    def _(pe):
        for q, (n, a, b) in enumerate(todo):
            if q >= 4:
                pe.wait_ge(s_ev, q - 3)
            rows, terms = jobs[n]
            for k, (w, x) in enumerate(terms):
                last = nc.tensor.matmul(mm[q % 4][0:rows, 0:b - a], w, x[:, a:b], start=k == 0, stop=k == len(terms) - 1)
            last.then_inc(s_mm, 1)

    @block.scalar
    def _(act):
        for q, (n, a, b) in enumerate(todo):
            act.wait_ge(s_mm, q + 1)
            evict(n, a, b, mm[q % 4][0:jobs[n][0], 0:b - a]).then_inc(s_ev, 1)


def mamba(nc, g, raw_dram, z_dram, conv_w, conv_b, x_w, dt_w, dt_b, A_log, D_par, out_w, ym_dram):
    S, R, K = 16, 16, 4
    dbc_dram = nc.dram_tensor("dbc", (R + 2 * S, NP), F32).ap()
    xc_dram = nc.dram_tensor("conv_x", (2, P, NP), F32).ap()
    with Phase(nc, "mam") as top:
        xT = top.sb("xT", [P, 2, R + 2 * S])
        dtT = top.sb("dtT", [P, 1, D])
        outT = top.sb("outT", [P, 2, D])
        cw = top.sb("cw", [P, 2, K])
        cols = top.sb("cols", [P, 3, 2])
        A = top.sb("A", [P, 2, S])
        one = top.sb("one", [P, 1])
        turned_weights(nc, "mamwt", g, [(x_w, xT), (dt_w, dtT), (out_w, outT)])
        by_part = lambda a: a.rearrange("(k p) -> p k", p=P)
        load_all(nc, "mamwl", [(cw[:, :, :], conv_w.rearrange("(k p) c -> p k c", p=P)), (cols[:, 0, :], by_part(conv_b)),
                               (cols[:, 1, :], by_part(dt_b)), (cols[:, 2, :], by_part(D_par)),
                               (A[:, :, :], A_log.rearrange("(k p) s -> p k s", p=P))])
        dt = top.sb("dt", [P, 2, NP])
        u = top.sb("u", [P, 2, NP])
        with Phase(nc, "mama") as ph:
            xsT = ph.sb("xsT", [P, 2, NP])
            raw = ph.sb("raw", [P, 2, K - 1 + NP])
            with Phase(nc, "mamac") as pp:
                s_in, s_v, s_c = pp.sems("in", "v", "c")
                block = pp.block()

                @block.vector
                def _(dve):
                    v = Tick(s_v, dve)
                    v(nc.vector.memset(raw[:, :, 0:K - 1], 0.0))
                    for k in range(2):
                        dve.wait_ge(s_in, 16 * (k + 1))
                        v(nc.vector.tensor_scalar(xsT[:, k, :], raw[:, k, 0:NP], cw[:, k, 0:1], None, ALU.mult))
                        for c in range(1, K):
                            ins = nc.vector.scalar_tensor_tensor(xsT[:, k, :], raw[:, k, c:c + NP], cw[:, k, c:c + 1],
                                                                 xsT[:, k, :], ALU.mult, ALU.add)
                            v(ins)
                        dve.sem_inc(s_c, 1)

                @block.scalar
                def _(act):
                    for k in range(2):
                        act.wait_ge(s_c, k + 1)
                        nc.scalar.activation(xsT[:, k, :], xsT[:, k, :], ACT.Silu, bias=cols[:, 0, k:k + 1])

                @block.sync
                def _(sp):
                    for k in range(2):
                        if k:
                            sp.wait_ge(s_in, 16 * k)
                        sp.dma_start(raw[:, k, K - 1:], raw_dram[k]).then_inc(s_in, 16)
            with Phase(nc, "mamad") as pp:
                dbc = pp.sb("dbc", [R + 2 * S, NP])
                s_st = pp.sem("st")
                with Phase(nc, "mamae") as pq:
                    s_st = pq.sem("st")
                    block = pq.block()
                    banked_products(nc, pq, "mamae", block,
                                    [(R + 2 * S, [(xT[:, k, :], xsT[:, k, :]) for k in range(2)])],
                                    lambda n, a, b, psum: nc.scalar.copy(dbc[:, a:b], psum))

                    @block.sync
                    def _(sp):
                        sp.dma_start(xc_dram.rearrange("k p n -> p k n"), xsT[:, :, :]).then_inc(s_st, 16)
                        sp.wait_ge(s_st, 16)
                with Phase(nc, "mamag") as pq:
                    s_st = pq.sem("st")
                    block = pq.block()
                    banked_products(nc, pq, "mamag", block,
                                    [(P, [(dtT[0:R, 0, n * P:(n + 1) * P], dbc[0:R, :])]) for n in range(2)],
                                    lambda n, a, b, psum: nc.scalar.activation(dt[:, n, a:b], psum, ACT.Identity, bias=cols[:, 1, n:n + 1]))

                    @block.sync
                    def _(sp):
                        sp.dma_start(dbc_dram, dbc[:, :]).then_inc(s_st, 16)
                        sp.wait_ge(s_st, 16)
            with Phase(nc, "mamas") as pp:
                s_v, s_a, s_b = pp.sems("v", "a", "b")
                block = pp.block()

                @block.scalar
                def _(act):
                    a = Tick(s_a, act)
                    a(nc.scalar.activation(u[:, :, :], dt[:, :, :], ACT.Abs))
                    a(nc.scalar.activation(u[:, :, :], u[:, :, :], ACT.Exp, scale=-1.0))
                    act.wait_ge(s_v, 1)
                    a(nc.scalar.activation(u[:, :, :], u[:, :, :], ACT.Ln, bias=one[:, 0:1]))
                    nc.scalar.activation(A[:, :, :], A[:, :, :], ACT.Exp).then_inc(s_a, 1)

                @block.vector
                def _(dve):
                    v = Tick(s_v, dve)
                    v(nc.vector.memset(one[:, :], 1.0))
                    dve.wait_ge(s_a, 4)
                    v(nc.vector.scalar_tensor_tensor(dt[:, :, :], dt[:, :, :], 0.0, u[:, :, :], ALU.max, ALU.add))
                    v(nc.vector.tensor_tensor(u[:, :, :], dt[:, :, :], xsT[:, :, :], ALU.mult))
                    v(nc.vector.tensor_scalar(A[:, :, :], A[:, :, :], -1.0, None, ALU.mult))
        with Phase(nc, "mamb") as mid:
            yT = mid.sb("yT", [P, 2, NP])
            for ct in range(2):
                with Phase(nc, f"mamb{ct}") as ph:
                    ident = g.ident
                    rowb = ph.sb("rowb", [1, 2, NP])
                    bc = [ph.sb(f"bc{k}", [P, NP]) for k in range(2)]
                    dA = ph.sb("dA", [P, NP])
                    st = ph.sb("st", [P, NP])
                    hs = ph.sb("hs", [P, NP])
                    hc = ph.sb("hc", [P, NP])
                    acc = ph.ps("acc", [P, NP])
                    s_B, s_C, s_bb, s_bC, s_dA, s_x, s_h, s_hc, s_y = ph.sems("B", "C", "bb", "bC", "dA", "x", "h", "hc", "y")
                    block = ph.block()

                    @block.sync
                    def _(sp):
                        with sp.Fori(0, S, 1) as s:
                            a = sp.snap(s + R)
                            c = sp.snap(s + (R + S))
                            need = sp.snap(s)
                            sp.wait_ge(s_bb, need)
                            sp.sem_inc(g.waited, 1)
                            sp.dma_start(rowb[0:1, 0, :], dbc_dram[bass.ds(a, 1), :]).then_inc(s_B, 16)
                            sp.wait_ge(s_bC, need)
                            sp.sem_inc(g.waited, 1)
                            sp.dma_start(rowb[0:1, 1, :], dbc_dram[bass.ds(c, 1), :]).then_inc(s_C, 16)

                    @block.gpsimd
                    def _(pool):
                        with pool.Fori(0, S, 1) as s:
                            pool.wait_ge(s_B, (s + 1) * 16)
                            pool.wait_ge(s_x, s)
                            pool.sem_inc(g.waited, 1)
                            nc.gpsimd.partition_broadcast(bc[0][:, :], rowb[0:1, 0, :]).then_inc(s_bb, 1)
                            pool.wait_ge(s_C, (s + 1) * 16)
                            pool.wait_ge(s_hc, s)
                            pool.sem_inc(g.waited, 1)
                            nc.gpsimd.partition_broadcast(bc[1][:, :], rowb[0:1, 1, :]).then_inc(s_bC, 1)

                    @block.scalar
                    def _(act):
                        with act.Fori(0, S, 1) as s:
                            act.wait_ge(s_h, s)
                            nc.scalar.activation(dA[:, :], dt[:, ct, :], ACT.Exp, scale=A[:, ct, bass.ds(s, 1)]).then_inc(s_dA, 1)
                        act.wait_ge(s_y, S)
                        for a, b in BANKS:
                            nc.scalar.copy(yT[:, ct, a:b], acc[:, a:b])

                    @block.vector
                    def _(dve):
                        with dve.Fori(0, S, 1) as s:
                            dve.wait_ge(s_bb, s + 1)
                            nc.vector.tensor_tensor(st[:, :], u[:, ct, :], bc[0][:, :], ALU.mult).then_inc(s_x, 1)
                            dve.wait_ge(s_x, s + 1)
                            dve.wait_ge(s_dA, s + 1)
                            nc.vector.tensor_tensor_scan(hs[:, :], dA[:, :], st[:, :], 0.0, ALU.mult, ALU.add).then_inc(s_h, 1)
                            dve.wait_ge(s_h, s + 1)
                            dve.wait_ge(s_bC, s + 1)
                            dve.wait_ge(s_y, s)
                            nc.vector.tensor_tensor(hc[:, :], hs[:, :], bc[1][:, :], ALU.mult).then_inc(s_hc, 1)

                    @block.tensor
                    def _(pe):
                        for a, b in BANKS:
                            nc.tensor.matmul(acc[:, a:b], g.zeros[:, 0:P], g.zeros[:, 0:b - a], start=True, stop=False)
                        with pe.Fori(0, S - 1, 1) as s:
                            pe.wait_ge(s_hc, s + 1)
                            for a, b in BANKS:
                                last = nc.tensor.matmul(acc[:, a:b], ident[:, :], hc[:, a:b], start=False, stop=False)
                            last.then_inc(s_y, 1)
                        pe.wait_ge(s_hc, S)
                        for a, b in BANKS:
                            last = nc.tensor.matmul(acc[:, a:b], ident[:, :], hc[:, a:b], start=False, stop=True)
                        last.then_inc(s_y, 1)
            with Phase(nc, "mamo") as ph:
                xc = ph.sb("xc", [P, 2, NP])
                z = u
                out = dt
                outv = out[:, :, :].rearrange("p k n -> p (k n)").rearrange("p (t d) -> p t d", d=D)
                mm = [ph.ps(f"mm{k}", [P, BANK]) for k in range(2)]
                s_in, s_v, s_r, s_m, s_e, s_st = ph.sems("in", "v", "r", "m", "e", "st")
                pairs = [range(a, min(a + 2, T)) for a in range(0, T, 2)]
                block = ph.block()

                @block.sync
                def _(sp):
                    sp.dma_start(xc[:, :, :], xc_dram.rearrange("k p n -> p k n")).then_inc(s_in, 16)
                    sp.dma_start(z[:, :, :], z_dram.rearrange("k p n -> p k n")).then_inc(s_in, 16)
                    sp.wait_ge(s_e, len(pairs))
                    sp.dma_start(nodes(ym_dram), outv).then_inc(s_st, 16)
                    sp.wait_ge(s_st, 16)

                @block.vector
                def _(dve):
                    v = Tick(s_v, dve)
                    dve.wait_ge(s_in, 32)
                    for k in range(2):
                        v(nc.vector.scalar_tensor_tensor(yT[:, k, :], xc[:, k, :], cols[:, 2, k:k + 1], yT[:, k, :], ALU.mult, ALU.add))
                        v(nc.vector.tensor_tensor(yT[:, k, :], yT[:, k, :], z[:, k, :], ALU.mult))
                    dve.sem_inc(s_r, 1)

                @block.tensor
                def _(pe):
                    pe.wait_ge(s_r, 1)
                    for q, pr in enumerate(pairs):
                        if q > 1:
                            pe.wait_ge(s_e, q - 1)
                        for n, t in enumerate(pr):
                            for k in range(2):
                                last = nc.tensor.matmul(mm[q % 2][:, n * D:(n + 1) * D], yT[:, k, t * P:(t + 1) * P], outT[:, k, :],
                                                        start=k == 0, stop=k == 1)
                        last.then_inc(s_m, 1)

                @block.scalar
                def _(act):
                    for q, pr in enumerate(pairs):
                        act.wait_ge(s_m, q + 1)
                        nc.scalar.copy(outv[:, pr[0]:pr[-1] + 1, :].rearrange("p t d -> p (t d)"), mm[q % 2][:, 0:len(pr) * D]).then_inc(s_e, 1)


def mixed_branches(nc, g, x_dram, hl_dram, ym_dram, gg, gb, wl, wg, f1w, f1b, f2w, f2b, ng, nb, x_out):
    ha_dram = nc.dram_tensor("h_attn", (NP, D), F32).ap()
    s_dram = nc.dram_tensor("h_and_ff", (NP, D), F32).ap()
    with Phase(nc, "mixa") as ph:
        y = ph.sb("y", [P, T, D])
        x = ph.sb("x", [P, T, D])
        rows = ph.sb("rows", [P, 2, D])
        moved_rows(nc, "mixag", g, ym_dram, y, False)
        norm = Norm(ph, "n")
        s_in, s_row, s_v, s_o, s_st = ph.sems("in", "row", "v", "o", "st")
        block = ph.block()

        @block.sync
        def _(sp):
            for k, r in enumerate((gg, gb)):
                sp.dma_start(rows[:, k, :], row(r)).then_inc(s_row, 16)
            for k, (a, b) in enumerate(GROUPS):
                if k:
                    sp.wait_ge(s_in, 16 * k)
                sp.dma_start(x[:, a:b, :], nodes(x_dram)[:, a:b, :]).then_inc(s_in, 16)
            for k, (a, b) in enumerate(GROUPS):
                sp.wait_ge(s_o, k + 1)
                sp.dma_start(nodes(ha_dram)[:, a:b, :], y[:, a:b, :]).then_inc(s_st, 16)
            sp.wait_ge(s_st, 16 * len(GROUPS))

        @block.vector
        def _(dve):
            v = Tick(s_v, dve)
            dve.wait_ge(s_row, 32)

            def before(k, a, b):
                dve.wait_ge(s_in, 16 * (k + 1))
                v(nc.vector.tensor_tensor(y[:, a:b, :], y[:, a:b, :], x[:, a:b, :], ALU.add))
            norm.dve(nc, dve, v, y, rows[:, 0, :], rows[:, 1, :], before, s_o)

        @block.scalar
        def _(act):
            norm.act(nc, act, y)
    with Phase(nc, "mixb") as top:
        lT = top.sb("lT", [P, 2, D])
        gT = top.sb("gT", [P, 2, D])
        f1T = top.sb("f1T", [P, 2, 2 * D])
        f2T = top.sb("f2T", [P, 4, D])
        f1c = top.sb("f1c", [P, 4])
        f2r = top.sb("f2r", [P, D])
        turned_weights(nc, "mixbt", g, [(wl, lT), (wg, gT), (f1w, f1T), (f2w, f2T)])
        load_all(nc, "mixbl", [(f1c[:, :], f1b.rearrange("(c p) -> p c", p=P)), (f2r[:, :], row(f2b))])
        with Phase(nc, "mixc") as ph:
            both = [ph.sb(f"both{u}", [P, 2, D]) for u in range(2)]
            bothT = ph.sb("bothT", [P, 4, P])
            gate = ph.sb("gate", [P, D])
            dif = ph.sb("dif", [P, D])
            h = [ph.sb(f"h{u}", [P, D]) for u in range(2)]
            hT = ph.sb("hT", [P, 2, P])
            hid = ph.sb("hid", [P, 4, P])
            res = [ph.sb(f"res{u}", [P, D]) for u in range(2)]
            tp = ph.ps("tp", [P, BANK])
            ga = ph.ps("ga", [P, D])
            tq = ph.ps("tq", [P, D])
            mh = ph.ps("mh", [P, BANK])
            mo = ph.ps("mo", [P, D])
            s_in = ph.sems("in0", "in1")
            s_st = ph.pool_sems(g, 2)
            s_free, s_t, s_tc, s_g, s_gs, s_h, s_q, s_qc, s_m, s_mr, s_o, s_r, s_v = ph.sems(
                "free", "t", "tc", "g", "gs", "h", "q", "qc", "m", "mr", "o", "r", "v")
            block = ph.block()

            def turns(eng, step):
                with eng.Fori(0, T // 2, 1) as i:
                    step(2 * i, i, 0)
                    step(2 * i + 1, i, 1)
                step(T - 1, T // 2, 0)

            @block.sync
            def _(sp):
                def step(t, i, u):
                    a = sp.snap(t * P) if not isinstance(t, int) else t * P
                    need = sp.snap(t + 1) if not isinstance(t, int) else t + 1
                    sp.wait_ge(s_free, need)
                    sp.sem_inc(g.waited, 1)
                    sp.dma_start(both[u][:, 0, :], hl_dram[bass.ds(a, P), :]).then_inc(s_in[u], 16)
                    sp.dma_start(both[u][:, 1, :], ha_dram[bass.ds(a, P), :]).then_inc(s_in[u], 16)
                turns(sp, step)

            def staged(eng, first, step, last):
                first()
                with eng.Fori(0, T // 2, 1) as i:
                    step(2 * i, 0, i)
                    step(2 * i + 1, 1, i + 1)
                last(T - 1)

            @block.tensor
            def _(pe):
                def turn(u, i):
                    pe.wait_ge(s_in[u], (i + 1) * 32)
                    for c in range(4):
                        last = nc.tensor.transpose(tp[:, c * P:(c + 1) * P], both[u][:, c // 2, (c % 2) * P:(c % 2 + 1) * P], g.ident[:, :])
                    last.then_inc(s_t, 1)

                def gates(t):
                    pe.wait_ge(s_tc, t + 1)
                    for c in range(4):
                        last = nc.tensor.matmul(ga[:, :], bothT[:, c, :], (lT if c < 2 else gT)[:, c % 2, :], start=c == 0, stop=c == 3)
                    last.then_inc(s_g, 1)

                def mix_turned(t, u):
                    pe.wait_ge(s_h, t + 1)
                    pe.sem_inc(s_free, 1)
                    for k in range(2):
                        last = nc.tensor.transpose(tq[:, k * P:(k + 1) * P], h[u][:, k * P:(k + 1) * P], g.ident[:, :])
                    last.then_inc(s_q, 1)

                def forward(t):
                    pe.wait_ge(s_qc, t + 1)
                    for c in range(4):
                        for k in range(2):
                            last = nc.tensor.matmul(mh[:, c * P:(c + 1) * P], f1T[:, k, c * P:(c + 1) * P], hT[:, k, :], start=k == 0, stop=k == 1)
                    last.then_inc(s_m, 1)
                    pe.wait_ge(s_mr, t + 1)
                    pe.wait_ge(s_r, t + 2)
                    for c in range(4):
                        last = nc.tensor.matmul(mo[:, :], hid[:, c, :], f2T[:, c, :], start=c == 0, stop=c == 3)
                    last.then_inc(s_o, 1)

                pe.sem_inc(s_free, 2)

                def first():
                    turn(0, 0)
                    gates(0)

                def step(t, u, nxt):
                    turn(1 - u, nxt)
                    mix_turned(t, u)
                    gates(t + 1)
                    forward(t)

                def last_(t):
                    mix_turned(t, 0)
                    forward(t)
                staged(pe, first, step, last_)

            @block.scalar
            def _(act):
                def turned_in(t):
                    act.wait_ge(s_t, t + 1)
                    nc.scalar.copy(bothT[:, :, :].rearrange("p c n -> p (c n)"), tp[:, :]).then_inc(s_tc, 1)

                def sigmoid(t):
                    act.wait_ge(s_g, t + 1)
                    act.wait_ge(s_h, t)
                    nc.scalar.activation(gate[:, :], ga[:, :], ACT.Sigmoid).then_inc(s_gs, 1)

                def forward(t):
                    act.wait_ge(s_q, t + 1)
                    nc.scalar.copy(hT[:, :, :].rearrange("p c n -> p (c n)"), tq[:, :]).then_inc(s_qc, 1)
                    act.wait_ge(s_m, t + 1)
                    for c in range(4):
                        last = nc.scalar.activation(hid[:, c, :], mh[:, c * P:(c + 1) * P], ACT.Relu, bias=f1c[:, c:c + 1])
                    last.then_inc(s_mr, 1)

                def step(t, u, nxt):
                    sigmoid(t)
                    turned_in(t + 1)
                    forward(t)

                def last_(t):
                    sigmoid(t)
                    forward(t)
                staged(act, lambda: turned_in(0), step, last_)

            @block.vector
            def _(dve):
                v = Tick(s_v, dve)
                dve.sem_inc(s_r, 2)

                def mix(t, u, i):
                    dve.wait_ge(s_in[u], (i + 1) * 32)
                    if not isinstance(t, int):
                        dve.wait_ge(s_h, t)
                    v(nc.vector.tensor_tensor(dif[:, :], both[u][:, 0, :], both[u][:, 1, :], ALU.subtract))
                    dve.wait_ge(s_gs, t + 1)
                    v(nc.vector.tensor_tensor(dif[:, :], dif[:, :], gate[:, :], ALU.mult))
                    nc.vector.tensor_tensor(h[u][:, :], dif[:, :], both[u][:, 1, :], ALU.add).then_inc(s_h, 1)

                def finish(t, u, i):
                    dve.wait_ge(s_h, t + 1)
                    dve.wait_ge(s_st[u], i * 16)
                    v(nc.vector.tensor_tensor(res[u][:, :], h[u][:, :], f2r[:, :], ALU.add))
                    dve.wait_ge(s_o, t + 1)
                    nc.vector.tensor_tensor(res[u][:, :], res[u][:, :], mo[:, :], ALU.add).then_inc(s_r, 1)
                mix(0, 0, 0)
                with dve.Fori(0, T // 2, 1) as i:
                    v.loop(i, 6)
                    mix(2 * i + 1, 1, i)
                    finish(2 * i, 0, i)
                    mix(2 * i + 2, 0, i + 1)
                    finish(2 * i + 1, 1, i)
                v.end(T // 2)
                finish(T - 1, 0, T // 2)

            @block.gpsimd
            def _(pool):
                def step(t, i, u):
                    pool.wait_ge(s_r, t + 3)
                    pool.dma_start(s_dram[bass.ds(t * P, P), :], res[u][:, :]).then_inc(s_st[u], 16)
                turns(pool, step)
                pool.wait_ge(s_st[0], (T - T // 2) * 16)
                pool.wait_ge(s_st[1], (T // 2) * 16)
    residual_norm(nc, "mixn", x_dram, s_dram, x_out, ng, nb)


def residual_norm(nc, name, x_dram, h_dram, x_out, gain=None, shift=None):
    with Phase(nc, name) as ph:
        h = ph.sb("h", [P, T, D])
        x = ph.sb("x", [P, T, D])
        rows = ph.sb("rows", [P, 2, D])
        inner = Norm(ph, "a")
        outer = Norm(ph, "b")
        s_in, s_row, s_v, s_o, s_st = ph.sems("in", "row", "v", "o", "st")
        block = ph.block()
        whole = N // P

        def stores(a, b):
            if x_out.shape[0] == NP:
                return [(nodes(x_out)[:, a:b, :], x[:, a:b, :])]
            own = [(nodes(x_out[0:whole * P, :])[:, a:min(b, whole), :], x[:, a:min(b, whole), :])]
            return own + ([(x_out[whole * P:N, :], x[0:N - whole * P, whole, :])] if b > whole else [])

        @block.sync
        def _(sp):
            if gain is not None:
                for k, r in enumerate((gain, shift)):
                    sp.dma_start(rows[:, k, :], row(r)).then_inc(s_row, 16)
            for k, (a, b) in enumerate(GROUPS):
                if k:
                    sp.wait_ge(s_in, 32 * k)
                sp.dma_start(x[:, a:b, :], nodes(x_dram)[:, a:b, :]).then_inc(s_in, 16)
                sp.dma_start(h[:, a:b, :], nodes(h_dram)[:, a:b, :]).then_inc(s_in, 16)
            n = 0
            for k, (a, b) in enumerate(GROUPS):
                sp.wait_ge(s_o, k + 1)
                for to, tiles in stores(a, b):
                    sp.dma_start(to, tiles).then_inc(s_st, 16)
                    n += 1
            sp.wait_ge(s_st, 16 * n)

        @block.vector
        def _(dve):
            v = Tick(s_v, dve)

            def loaded(k, a, b):
                dve.wait_ge(s_in, 32 * (k + 1))

            def added(k, a, b):
                if gain is None:
                    loaded(k, a, b)
                v(nc.vector.tensor_tensor(x[:, a:b, :], x[:, a:b, :], h[:, a:b, :], ALU.add))
            if gain is not None:
                dve.wait_ge(s_row, 32)
                inner.dve(nc, dve, v, h, rows[:, 0, :], rows[:, 1, :], loaded)
            outer.dve(nc, dve, v, x, before=added, done=s_o)

        @block.scalar
        def _(act):
            if gain is not None:
                inner.act(nc, act, h)
            outer.act(nc, act, x)


def relational_stack(nc, g, x_dram, weights, roots, biases, x_out):
    L = 3
    tables = [nc.dram_tensor(f"rel_table{n}", (REL * NP, D), F32).ap() for n in range(2)]
    owns = [nc.dram_tensor(f"rel_own{n}", (NP, D), F32).ap() for n in range(2)]
    h = nc.dram_tensor("rel_h", (NP, D), F32).ap()

    def pieces(w, n):
        return ([(w[:, :, r * D:(r + 1) * D], weights[n, r].rearrange("(k p) e -> p k e", p=P)) for r in range(REL)] +
                [(w[:, :, REL * D:], roots[n].rearrange("(k p) e -> p k e", p=P))])

    def stores(n):
        return lambda t, out: [(tables[n % 2].rearrange("(r n) d -> n r d", r=REL)[bass.ds(t * P, P), :, :],
                                out[:, 0:REL * D].rearrange("p (r d) -> p r d", d=D)),
                               (owns[n % 2][bass.ds(t * P, P), :], out[:, REL * D:])]
    with Phase(nc, "rel0w") as ph:
        w = ph.sb("w", [P, 2, (REL + 1) * D])
        load_all(nc, "rel0l", pieces(w, 0))
        project(nc, "rel0p", g, x_dram, w, (REL + 1) * D, stores(0))
    for n in range(L):
        if n < L - 1:
            gather_sum(nc, f"rel{n}s", g, tables[n % 2], owns[n % 2], biases[n], ACT.Relu,
                       then=(lambda w, n=n: pieces(w, n + 1), stores(n + 1)))
        else:
            gather_sum(nc, f"rel{n}s", g, tables[n % 2], owns[n % 2], biases[n], ACT.Sigmoid, out=h)
    residual_norm(nc, "reln", x_dram, h, x_out)


def gather_sum(nc, name, g, table, own, bias, func, out=None, then=None):
    G = G_SUM
    WIDE = (REL + 1) * D
    chunks = [(a, min(a + BANK, WIDE)) for a in range(0, WIDE, BANK)]
    NC = len(chunks)
    EARLY = 3
    with Phase(nc, name) as ph:
        rows = [ph.sb(f"rows{u}", [P, D]) for u in range(G)]
        at = [ph.sb(f"at{u}", [P, 1], I32) for u in range(G)]
        hot = [ph.sb(f"hot{u}", [P, P]) for u in range(G)]
        mine = ph.sb("mine", [P, D])
        bias_row = ph.sb("bias_row", [1, D])
        res = [ph.sb(f"res{u}", [P, D]) for u in range(2)]
        acc = ph.ps("acc", [P, D])
        s_in = ph.pool_sems(g, G)
        s_at, s_hot, s_used, s_sum, s_own, s_mine, s_bias, s_res, s_st = ph.sems(
            "at", "hot", "used", "sum", "own", "mine", "bias", "res", "st")
        if then:
            w = ph.sb("w", [P, 2, WIDE])
            turned = [ph.sb(f"turned{u}", [P, 2, P]) for u in range(2)]
            prod = [ph.sb(f"prod{u}", [P, WIDE]) for u in range(2)]
            tp = ph.ps("tp", [P, D])
            mm = [ph.ps(f"mm{n}", [P, BANK]) for n in range(NC)]
            s_w, s_tp, s_turn, s_mm, s_done = ph.sems("w", "tp", "turn", "mm", "done")
            s_pst = ph.sems("pst0", "pst1")
        block = ph.block()

        def periods(eng, step):
            with eng.Fori(0, T // 2, 1) as i:
                step(2 * i + 1, 1, i)
                step(2 * i + 2, 0, i)

        @block.vector
        def _(dve):
            with dve.Fori(0, T, 1) as t:
                first, count, before = span_of(dve, g, t, G)
                with dve.Fori(0, count, 1) as j:
                    c0 = step_start(nc, first + j * G)
                    for u in range(G):
                        dve.wait_ge(s_in[u], (before + j) * 16)
                        nc.vector.tensor_copy(at[u][:, :], g.rows[:, bass.ds(c0 + u, 1)]).then_inc(s_at, 1)
                        dve.wait_ge(s_used, (before + j) * G + (u + 1))
                        nc.vector.tensor_scalar(hot[u][:, :], g.numbers[:, bass.ds(t * P, P)],
                                                g.dsts[:, bass.ds(c0 + u, 1)], None, ALU.is_equal).then_inc(s_hot, 1)

        @block.gpsimd
        def _(pool):
            with pool.Fori(0, T, 1) as t:
                first, count, before = span_of(pool, g, t, G)
                with pool.Fori(0, count, 1) as j:
                    for u in range(G):
                        pool.wait_ge(s_at, (before + j) * G + (u + 1))
                        pool.wait_ge(s_used, (before + j) * G + (u + 1))
                        pool.sem_inc(g.waited, 1)
                        pool.indirect_dma_start(rows[u][:, :], None, table,
                                                bass.IndirectOffsetOnAxis(ap=at[u][:, 0:1], axis=0)).then_inc(s_in[u], 16)

        @block.tensor
        def _(pe):
            pe.sem_inc(s_used, G)

            def begin(t):
                pe.wait_ge(s_own, t * 16 + 16)
                nc.tensor.matmul(acc[:, :], g.ident[:, :], mine[:, :], start=True, stop=False).then_inc(s_mine, 1)

            def add(step):
                for u in range(G):
                    pe.wait_ge(s_hot, step * G + (u + 1))
                    pe.wait_ge(s_in[u], step * 16 + 16)
                    nc.tensor.matmul(acc[:, :], hot[u][:, :], rows[u][:, :], start=False, stop=False).then_inc(s_used, 1)

            def end():
                nc.tensor.matmul(acc[:, :], g.ones[0:1, :], bias_row[0:1, :], start=False, stop=True).then_inc(s_sum, 1)

            def turn(u):
                for k in range(2):
                    last = nc.tensor.transpose(tp[:, k * P:(k + 1) * P], res[u][:, k * P:(k + 1) * P], g.ident[:, :])
                last.then_inc(s_tp, 1)

            def multiply(t, u, part):
                pe.wait_ge(s_turn, t + 1)
                for n in part:
                    a, b = chunks[n]
                    pe.wait_ge(s_done, t * NC + (n + 1))
                    for k in range(2):
                        last = nc.tensor.matmul(mm[n][:, 0:b - a], turned[u][:, k, :], w[:, k, a:b], start=k == 0, stop=k == 1)
                    last.then_inc(s_mm, 1)

            pe.wait_ge(s_bias, 16)
            if then:
                pe.sem_inc(s_done, NC)
                pe.wait_ge(s_w, (REL + 1) * 16)

            def tile(count, before):
                with pe.Fori(0, count, 1) as j:
                    add(before + j)
            first, count, before = span_of(pe, g, 0, G)
            begin(0)
            tile(count, before)
            end()

            def step(t, u, i):
                first, count, before = span_of(pe, g, t, G)
                pe.wait_ge(s_res, t)
                begin(t)
                if not then:
                    tile(count, before)
                    end()
                    return
                turn(1 - u)
                add(before)
                multiply(t - 1, 1 - u, range(EARLY))
                with pe.Fori(1, count, 1) as j:
                    add(before + j)
                end()
                multiply(t - 1, 1 - u, range(EARLY, NC))
            periods(pe, step)
            if then:
                pe.wait_ge(s_res, T)
                turn(0)
                multiply(T - 1, 0, range(NC))

        @block.scalar
        def _(act):
            def activate(t, u):
                act.wait_ge(s_sum, t + 1)
                if out is not None and not (isinstance(t, int) and t == 0):
                    act.wait_ge(s_st, t * 16)
                nc.scalar.activation(res[u][:, :], acc[:, :], func).then_inc(s_res, 1)

            def turned_in(t, u):
                act.wait_ge(s_tp, t + 1)
                nc.scalar.copy(turned[u][:, :, :].rearrange("p k n -> p (k n)"), tp[:, :]).then_inc(s_turn, 1)

            def products(t, u, i, part):
                if part[0] == 0:
                    act.wait_ge(s_pst[u], i * 32)
                for n in part:
                    a, b = chunks[n]
                    act.wait_ge(s_mm, t * NC + (n + 1))
                    nc.scalar.copy(prod[u][:, a:b], mm[n][:, 0:b - a]).then_inc(s_done, 1)
                if part[-1] == NC - 1:
                    act.wait_ge(s_done, t * NC + 2 * NC)
                    act.sem_inc(g.waited, 1)
                    for to, tile in then[1](t, prod[u]):
                        act.dma_start(to, tile).then_inc(s_pst[u], 16)

            activate(0, 0)

            def step(t, u, i):
                if then:
                    turned_in(t - 1, 1 - u)
                    products(t - 1, 1 - u, i, range(EARLY))
                activate(t, u)
                if then:
                    products(t - 1, 1 - u, i, range(EARLY, NC))
            periods(act, step)
            if then:
                turned_in(T - 1, 0)
                products(T - 1, 0, T // 2, range(NC))
                act.wait_ge(s_pst[0], 32 * (T // 2 + 1))
                act.wait_ge(s_pst[1], 32 * (T // 2))

        @block.sync
        def _(sp):
            sp.dma_start(bias_row[:, :], bias.rearrange("(o n) -> o n", o=1)).then_inc(s_bias, 16)
            sp.dma_start(mine[:, :], own[0:P, :]).then_inc(s_own, 16)
            if then:
                for to, a in then[0](w):
                    sp.dma_start(to, a).then_inc(s_w, 16)

            def load(t):
                b = sp.snap(t * P)
                need = sp.snap(t)
                sp.wait_ge(s_mine, need)
                sp.sem_inc(g.waited, 1)
                sp.dma_start(mine[:, :], own[bass.ds(b, P), :]).then_inc(s_own, 16)

            def store(t, u):
                a, need = (t * P, t + 1) if isinstance(t, int) else (sp.snap(t * P), sp.snap(t + 1))
                sp.wait_ge(s_res, need)
                sp.sem_inc(g.waited, 1)
                sp.dma_start(out[bass.ds(a, P), :], res[u][:, :]).then_inc(s_st, 16)

            def step(t, u, i):
                load(t)
                if out is not None:
                    store(t - 1, 1 - u)
            periods(sp, step)
            if out is not None:
                store(T - 1, 0)
                sp.wait_ge(s_st, 16 * T)


def last_attention(nc, g, x_dram, W, a_l, a_r, bias, lin_w, lin_b, out):
    H = 2
    F = H * 64
    pr_dram = nc.dram_tensor("last_rows", (NP, H * 65 + 2 * H), F32).ap()
    agg_dram = nc.dram_tensor("last_agg", (H, 65, NP), F32).ap()
    h_dram = nc.dram_tensor("last_h", (NP, D), F32).ap()
    with Phase(nc, "las") as top:
        scores = top.sb("scores", [P, T, 2 * H])
        with Phase(nc, "lasw") as ph:
            weights = ph.sb("weights", [P, 2, F + 2 * H])
            WT = ph.sb("WT", [P, 1, D])
            load_all(nc, "laswl", [(weights[:, :, 0:F], W.rearrange("(k p) n -> p k n", p=P))])
            turned_weights(nc, "laswt", g, [(W, WT)])
            score_weights(nc, "lasws", g, None, WT, a_l, a_r, H, weights)
            project(nc, "lasp", g, x_dram, weights, F + 2 * H, lambda t, out: [(pr_dram[bass.ds(t * P, P), :], out[:, :])],
                    extra=scores, ones_at=H)
        attention(nc, "lat", g, H, pr_dram, scores, agg_dram, True)
        with Phase(nc, "laso") as ph:
            h = ph.sb("h", [P, T, F])
            o = ph.sb("o", [P, T, D])
            lw = ph.sb("lw", [P, D])
            br = ph.sb("br", [P, F])
            lr = ph.sb("lr", [P, D])
            turned = [ph.sb(f"turned{u}", [P, 2 * P]) for u in range(2)]
            heads_to_nodes(nc, "lash", g, H, agg_dram, h, (ALU.max, 1e-30))
            tp = [ph.ps(f"tp{u}", [P, BANK]) for u in range(2)]
            mm = [ph.ps(f"mm{u}", [P, BANK]) for u in range(2)]
            s_in, s_v, s_a, s_t, s_c, s_m, s_r, s_o, s_st = ph.sems("in", "v", "a", "t", "c", "m", "r", "o", "st")
            pairs = [range(a, min(a + 2, T)) for a in range(0, T, 2)]
            block = ph.block()

            @block.sync
            def _(sp):
                for to, a in ((lw[:, :], lin_w), (br[:, :], row(bias)), (lr[:, :], row(lin_b))):
                    sp.dma_start(to, a).then_inc(s_in, 16)
                sp.wait_ge(s_o, 1)
                sp.dma_start(nodes(h_dram), o[:, :, :]).then_inc(s_st, 16)
                sp.wait_ge(s_st, 16)

            @block.tensor
            def _(pe):
                pe.wait_ge(s_a, 1)
                for k, pr in enumerate(pairs):
                    if k > 1:
                        pe.wait_ge(s_c, k - 1)
                    for n, t in enumerate(pr):
                        last = nc.tensor.transpose(tp[k % 2][:, n * P:(n + 1) * P], h[:, t, :], g.ident[:, :])
                    last.then_inc(s_t, 1)
                    pe.wait_ge(s_c, k + 1)
                    if k > 1:
                        pe.wait_ge(s_r, k - 1)
                    for n, t in enumerate(pr):
                        last = nc.tensor.matmul(mm[k % 2][:, n * D:(n + 1) * D], turned[k % 2][:, n * P:(n + 1) * P], lw[:, :],
                                                start=True, stop=True)
                    last.then_inc(s_m, 1)

            @block.scalar
            def _(act):
                for k, pr in enumerate(pairs):
                    act.wait_ge(s_t, k + 1)
                    nc.scalar.copy(turned[k % 2][:, 0:len(pr) * P], tp[k % 2][:, 0:len(pr) * P]).then_inc(s_c, 1)

            @block.vector
            def _(dve):
                v = Tick(s_v, dve)
                dve.wait_ge(s_in, 48)
                v(nc.vector.tensor_tensor(h[:, :, :], h[:, :, :], br[:, :].unsqueeze(1).to_broadcast([P, T, F]), ALU.add))
                nc.vector.tensor_scalar(h[:, :, :], h[:, :, :], 0.0, None, ALU.max).then_inc(s_a, 1)
                for k, pr in enumerate(pairs):
                    dve.wait_ge(s_m, k + 1)
                    nc.vector.tensor_tensor(o[:, pr[0]:pr[-1] + 1, :],
                                            mm[k % 2][:, 0:len(pr) * D].rearrange("p (t d) -> p t d", d=D),
                                            lr[:, :].unsqueeze(1).to_broadcast([P, len(pr), D]), ALU.add).then_inc(s_r, 1)
                dve.wait_ge(s_r, len(pairs))
                v(nc.vector.tensor_scalar(o[:, :, :], o[:, :, :], 0.0, None, ALU.max))
                dve.sem_inc(s_o, 1)
    residual_norm(nc, "lasn", x_dram, h_dram, out)


def program(nc, x, src, dst, kind, noise, gcn, local, ssm, mix, rel, last, out):
    ctx = ExitStack()
    with ctx:
        g = Shared()

        def sb(name, shape, dt=F32):
            return ctx.enter_context(nc.sbuf_tensor(f"g_{name}", shape, dt))

        def dram(name, shape, dt=F32):
            return nc.dram_tensor(name, shape, dt).ap()

        g.ident = sb("ident", [P, P])
        g.ones = sb("ones", [P, P])
        g.zeros = sb("zeros", [P, BANK], BF16)
        g.numbers = sb("numbers", [P, NP], F16)
        g.srcs = sb("srcs", [P, CT * P])
        g.dsts = sb("dsts", [P, CT * P])
        g.rows = sb("rows", [P, CT * P], I32)
        g.spans = sb("spans", [1, 1 + 2 * len(SPANS), 32], I32)
        g.ident16 = sb("ident16", [P, P], BF16)
        g.strips_before = sb("strips_before", [1, 32], I32)
        g.indeg = sb("indeg", [P, T])
        g.dinv = sb("dinv", [P, T])
        g.rank = sb("rank", [P, T], I32)
        g.adj = dram("adj", (NP, NP))
        g.strips = dram("strips", (2 * NP, NP), BF16)
        g.absent = dram("absent", (NP, NP), BF16)
        xs = [dram(f"x{n}", (NP, D)) for n in range(4)]
        raw, silu_z = dram("in_raw", (2, P, NP)), dram("in_silu_z", (2, P, NP))
        hl, ym = dram("h_local", (NP, D)), dram("y_sorted", (NP, D))
        g.waited = ctx.enter_context(nc.semaphore("waited"))
        g.pool_sems = [ctx.enter_context(nc.semaphore(f"pool_dma{n}")) for n in range(36)]

        def clear():
            free = nc.free_semaphores
            nc.all_engine_barrier(sems_to_clear=range(min(free), max(free) + 1))

        g.clear = clear

        def stage(f, *args):
            f(nc, g, *args)
            clear()

        def graph(nc, g):
            constants(nc, g)
            edge_tables(nc, g, src, dst, kind)
            with Phase(nc, "deg") as ph:
                g.outdeg = ph.sb("outdeg", [P, NP])
                adjacency(nc, g)
                ranking.keys(g.outdeg)

        with Phase(nc, "rank") as ph:
            ranking = Ranking(nc, g, ph, noise)
            graph(nc, g)
            load_x(nc, g, x, xs[0])
            gcn_stack(nc, g, xs[0], ranking, *gcn, xs[1])
        clear()
        stage(local_branch, xs[1], *local, hl, ssm[0], raw, silu_z)
        stage(mamba, raw, silu_z, *ssm[1:], ym)
        stage(mixed_branches, xs[1], hl, ym, *mix, xs[2])
        stage(relational_stack, xs[2], *rel, xs[3])
        last_attention(nc, g, xs[3], *last, out)

_FIRST = ['x', 'src', 'dst', 'edge_type_8', 'node_vec']
_GCN = ['L0_gnn_W1', 'L0_gnn_b1', 'L0_gnn_W2', 'L0_gnn_b2', 'L0_gnn_W3', 'L0_gnn_b3', 'L0_gnn_W4', 'L0_gnn_b4']
_LOCAL = ['L1_gnn_gat_w', 'L1_gnn_gat_a_src', 'L1_gnn_gat_a_tgt', 'L1_gnn_gat_b', 'L1_gnn_ln_local_g', 'L1_gnn_ln_local_b']
_SSM = ['L1_gnn_in_proj_w', 'L1_gnn_conv_w', 'L1_gnn_conv_b', 'L1_gnn_x_proj_w', 'L1_gnn_dt_proj_w', 'L1_gnn_dt_proj_b', 'L1_gnn_A_log', 'L1_gnn_D_param', 'L1_gnn_out_proj_w']
_MIX = ['L1_gnn_ln_global_g', 'L1_gnn_ln_global_b', 'L1_gnn_wl', 'L1_gnn_wg', 'L1_gnn_ff1_w', 'L1_gnn_ff1_b', 'L1_gnn_ff2_w', 'L1_gnn_ff2_b', 'L1_gnn_ln2_g', 'L1_gnn_ln2_b']
_REL = ['L2_gnn_weights', 'L2_gnn_roots', 'L2_gnn_biases']
_LAST = ['L3_gnn_W', 'L3_gnn_attn_l', 'L3_gnn_attn_r', 'L3_gnn_gat_bias', 'L3_gnn_lin_W', 'L3_gnn_lin_b']


def kernel(**inputs):
    import numpy as _np
    import concourse.bacc as _bacc
    from concourse import mybir as _mybir
    from concourse.bass_utils import run_bass_kernel_spmd as _run

    nc = _bacc.Bacc("TRN2", target_bir_lowering=False, num_devices=1)
    arrays = {}

    def given(names):
        aps = []
        for name in names:
            a = _np.ascontiguousarray(inputs[name])
            arrays[f"in_{name}"] = a
            aps.append(nc.dram_tensor(f"in_{name}", a.shape, _mybir.dt.from_np(a.dtype), kind="ExternalInput").ap())
        return aps

    first = given(_FIRST)
    rest = [given(names) for names in (_GCN, _LOCAL, _SSM, _MIX, _REL, _LAST)]
    out = nc.dram_tensor("out", (N, D), F32, kind="ExternalOutput").ap()
    program(nc, *first, *rest, out)
    r = _run(nc, [arrays], core_ids=[0])
    return r.results[0]["out"]
```
